# Optimizing a Trainium2 kernel written in Bass

```python
import numpy as np
import jax
import jax.numpy as jnp

def _softmax(x, axis=-1):
    return jax.nn.softmax(x, axis=axis)

def _gelu(x):
    return jax.nn.gelu(x, approximate=True)

def _silu(x):
    return jax.nn.silu(x)

def _sigmoid(x):
    return jax.nn.sigmoid(x)

def _layernorm(x, axis=-1, eps=1e-05):
    m = jnp.mean(x, axis=axis, keepdims=True)
    v = jnp.var(x, axis=axis, keepdims=True)
    return (x - m) / jnp.sqrt(v + eps)

def _scatter_add(tgt, idx, src, axis=0):
    return tgt.at[idx].add(src)

def _segment_sum(src, seg, n):
    return jax.ops.segment_sum(src, seg, n)
kernel_name = 'mk_perceiver_d2_seqx_r8_f219b7'

def setup_inputs(seed: int=0):
    np.random.seed(seed)
    _w = jnp.asarray

    def _rec_inputs():
        import jax
        import jax.numpy as jnp
        _rk = jax.random.key(seed)
        x = -0.0002928 + 1 * jax.random.normal(jax.random.fold_in(_rk, 1), (64, 32, 256), jnp.float32)
        _lenS = 32 - jax.random.randint(jax.random.fold_in(_rk, 7), (64,), 0, max(1, 32 // 4) + 1, jnp.int32)
        _lenS2 = 257 - jax.random.randint(jax.random.fold_in(_rk, 8), (64,), 0, max(1, 257 // 4) + 1, jnp.int32)
        _ctx_2048P = jax.random.normal(jax.random.fold_in(_rk, 11), (64, 16, 256), jnp.float32)
        _ctx_2048c = jax.random.dirichlet(jax.random.fold_in(_rk, 511), 0.3 * jnp.ones((16,), jnp.float32), (64, 257))
        _ctx_2048t = jnp.einsum('bsk,bkd->bsd', _ctx_2048c, _ctx_2048P)
        _ctx_2048t = _ctx_2048t * jax.lax.rsqrt(jnp.mean(jnp.square(_ctx_2048t)) + 1e-12) * 0.953939
        ctx_2048 = 4.13588e-05 + 0.999923 * (_ctx_2048t + 0.3 * jax.random.normal(jax.random.fold_in(_rk, 611), (64, 257, 256), jnp.float32))
        _validS = jnp.arange(32)[None, :] < _lenS[:, None]
        _validS2 = jnp.arange(257)[None, :] < _lenS2[:, None]
        _causal = jnp.tril(jnp.ones((32, 32), dtype=bool))
        mask_1xSxS2_ff0 = jnp.where(jnp.ones((1, 32, 257), dtype=bool), 0.0, -1000000000.0).astype(jnp.float32)
        mask_BxS2_ff1 = jnp.where(jnp.ones((64, 257), dtype=bool), 1.0, 0.0).astype(jnp.float32)
        return (x, ctx_2048, mask_1xSxS2_ff0, mask_BxS2_ff1)
    x, ctx_2048, mask_1xSxS2_ff0, mask_BxS2_ff1 = _rec_inputs()

    def _L0_xattn_setup():
        import jax, jax.numpy as jnp
        import numpy as np
        H = 256
        NH = 16
        NKV = 4
        HD = 128
        GROUPS = NH // NKV
        EPS = 1e-06
        B, S, SE = (1, 256, 512)

        def _rmsnorm(x, w, eps=EPS):
            xf = x.astype(jnp.float32)
            var = jnp.mean(xf * xf, axis=-1, keepdims=True)
            return (xf * jax.lax.rsqrt(var + eps)).astype(x.dtype) * w
        key = jax.random.key(seed)
        ks = jax.random.split(key, 12)
        sc = 0.02
        return {'hidden_states': jax.random.normal(ks[0], (B, S, H), jnp.float32), 'encoder_hidden_states': jax.random.normal(ks[1], (B, SE, H), jnp.float32), 'attention_mask': jnp.zeros((B, S, SE), jnp.float32), 'Wq': jax.random.normal(ks[2], (H, NH * HD), jnp.float32) * sc, 'bq': jax.random.normal(ks[3], (NH * HD,), jnp.float32) * sc, 'Wk': jax.random.normal(ks[4], (H, NKV * HD), jnp.float32) * sc, 'bk': jax.random.normal(ks[5], (NKV * HD,), jnp.float32) * sc, 'Wv': jax.random.normal(ks[6], (H, NKV * HD), jnp.float32) * sc, 'bv': jax.random.normal(ks[7], (NKV * HD,), jnp.float32) * sc, 'Wo': jax.random.normal(ks[8], (NH * HD, H), jnp.float32) * sc, 'qn_w': jnp.ones((HD,), jnp.float32), 'kn_w': jnp.ones((HD,), jnp.float32)}
    _L0_xattn_all = _L0_xattn_setup()
    _L0_xattn_in = {k: v for k, v in _L0_xattn_all.items() if k in ('Wq', 'bq', 'Wk', 'bk', 'Wv', 'bv', 'Wo', 'qn_w', 'kn_w')}
    del _L0_xattn_all

    def _L0_attn_setup():
        import jax, jax.numpy as jnp
        import numpy as np
        B, T, C = (4, 128, 256)
        N = 64
        H = C // N
        D_DECAY, D_AAA, D_MV, D_GATE = (64, 64, 32, 128)

        def rwkv7_op(r, w, k, v, a, b):
            Bq, Tq, Cq = r.shape
            decay = jnp.exp(-jnp.exp(w))

            def resh(t):
                return t.reshape(Bq, Tq, H, N).transpose(1, 0, 2, 3)
            rs, ws, ks, vs, as_, bs = map(resh, (r, decay, k, v, a, b))
            S0 = jnp.zeros((Bq, H, N, N), r.dtype)

            def step(S, inp):
                rt, wt, kt, vt, at, bt = inp
                sa = jnp.einsum('bhij,bhj->bhi', S, at)
                S = S * wt[:, :, None, :] + sa[:, :, :, None] * bt[:, :, None, :] + vt[:, :, :, None] * kt[:, :, None, :]
                yt = jnp.einsum('bhij,bhj->bhi', S, rt)
                return (S, yt)
            _, y = jax.lax.scan(step, S0, (rs, ws, ks, vs, as_, bs))
            return y.transpose(1, 0, 2, 3).reshape(Bq, Tq, Cq)

        def _reference_tuple_inner(x, x_r, x_w, x_k, x_v, x_a, x_g, w0, w1, w2, a0, a1, a2, v0, v1, v2, g1, g2, k_k, k_a, r_k, W_r, W_k, W_v, W_o, gn_scale, gn_offset):
            Bq, Tq, Cq = x.shape
            xx = jnp.pad(x, ((0, 0), (1, 0), (0, 0)))[:, :-1, :] - x
            xr = x + xx * x_r
            xw = x + xx * x_w
            xk = x + xx * x_k
            xv = x + xx * x_v
            xa = x + xx * x_a
            xg = x + xx * x_g
            r = xr @ W_r
            w = -jax.nn.softplus(-(w0 + jnp.tanh(xw @ w1) @ w2)) - 0.5
            k = xk @ W_k
            v = xv @ W_v
            v_first = v
            a = jax.nn.sigmoid(a0 + xa @ a1 @ a2)
            g = jax.nn.sigmoid(xg @ g1) @ g2
            kk = (k * k_k).reshape(Bq, Tq, H, N)
            nrm = jnp.sqrt(jnp.sum(kk * kk, axis=-1, keepdims=True))
            kk = (kk / jnp.maximum(nrm, 1e-12)).reshape(Bq, Tq, Cq)
            k2 = k * (1.0 + (a - 1.0) * k_a)
            o = rwkv7_op(r, w, k2, v, -kk, kk * a)
            o = (o.reshape(Bq, Tq, H, N) * gn_scale + gn_offset).reshape(Bq, Tq, Cq)
            r4 = r.reshape(Bq, Tq, H, N)
            k4 = k2.reshape(Bq, Tq, H, N)
            v4 = v.reshape(Bq, Tq, H, N)
            rwkv = jnp.sum(r4 * k4 * r_k, axis=-1, keepdims=True) * v4
            o = o + rwkv.reshape(Bq, Tq, Cq)
            out = o * g @ W_o
            return (out, v_first)
        key = jax.random.key(seed)
        ks = jax.random.split(key, 32)

        def rn(k, shape, s=0.02):
            return jax.random.normal(k, shape, jnp.float32) * s
        inp = {'x': jax.random.normal(ks[0], (B, T, C), jnp.float32), 'x_r': rn(ks[1], (1, 1, C), 0.5), 'x_w': rn(ks[2], (1, 1, C), 0.5), 'x_k': rn(ks[3], (1, 1, C), 0.5), 'x_v': rn(ks[4], (1, 1, C), 0.5), 'x_a': rn(ks[5], (1, 1, C), 0.5), 'x_g': rn(ks[6], (1, 1, C), 0.5), 'w0': rn(ks[7], (1, 1, C), 0.3), 'w1': rn(ks[8], (C, D_DECAY)), 'w2': rn(ks[9], (D_DECAY, C)), 'a0': rn(ks[10], (1, 1, C), 0.3), 'a1': rn(ks[11], (C, D_AAA)), 'a2': rn(ks[12], (D_AAA, C)), 'v0': rn(ks[13], (1, 1, C), 0.3), 'v1': rn(ks[14], (C, D_MV)), 'v2': rn(ks[15], (D_MV, C)), 'g1': rn(ks[16], (C, D_GATE)), 'g2': rn(ks[17], (D_GATE, C)), 'k_k': rn(ks[18], (1, 1, C), 0.5), 'k_a': rn(ks[19], (1, 1, C), 0.5), 'r_k': rn(ks[20], (H, N), 0.5), 'W_r': rn(ks[21], (C, C)), 'W_k': rn(ks[22], (C, C)), 'W_v': rn(ks[23], (C, C)), 'W_o': rn(ks[24], (C, C)), 'gn_scale': jnp.ones((H, N), jnp.float32) + rn(ks[25], (H, N), 0.1), 'gn_offset': rn(ks[26], (H, N), 0.1)}
        return inp
    _L0_attn_all = _L0_attn_setup()
    _L0_attn_in = {k: v for k, v in _L0_attn_all.items() if k in ('x_r', 'x_w', 'x_k', 'x_v', 'x_a', 'x_g', 'w0', 'w1', 'w2', 'a0', 'a1', 'a2', 'v0', 'v1', 'v2', 'g1', 'g2', 'k_k', 'k_a', 'r_k', 'W_r', 'W_k', 'W_v', 'W_o', 'gn_scale', 'gn_offset')}
    del _L0_attn_all

    def _L0_ffn_setup():
        import jax, jax.numpy as jnp
        import numpy as np
        DIM = 256
        INTER = 176
        E = 16
        TOPK = 4
        G = 4
        TOPK_G = 2
        N_SHARED = 2
        SHARED_INTER = N_SHARED * INTER
        ROUTE_SCALE = 1.0

        def _moe_forward(x, Wg, W1, W3, W2, Ws1, Ws3, Ws2):
            B, S, D = x.shape
            xt = x.reshape(-1, D)
            T = xt.shape[0]
            scores = jax.nn.softmax(xt @ Wg.T, axis=-1)
            sg = scores.reshape(T, G, E // G)
            group_scores = sg.max(axis=-1)
            gidx = jax.lax.top_k(group_scores, TOPK_G)[1]
            gmask = jax.nn.one_hot(gidx, G, dtype=jnp.float32).sum(axis=1) > 0
            masked = jnp.where(gmask[:, :, None], sg, -jnp.inf).reshape(T, E)
            topi = jax.lax.top_k(masked, TOPK)[1]
            weights = jnp.take_along_axis(scores, topi, axis=1) * ROUTE_SCALE
            combine = jnp.zeros((T, E), xt.dtype).at[jnp.arange(T)[:, None], topi].add(weights)
            h = jax.nn.silu(jnp.einsum('td,eid->eti', xt, W1)) * jnp.einsum('td,eid->eti', xt, W3)
            expert_out = jnp.einsum('eti,edi->etd', h, W2)
            y = jnp.einsum('etd,te->td', expert_out, combine)
            z = jax.nn.silu(xt @ Ws1.T) * (xt @ Ws3.T) @ Ws2.T
            return (y + z).reshape(B, S, D)
        key = jax.random.key(seed)
        ks = jax.random.split(key, 8)
        s = 0.02
        x = jax.random.normal(ks[0], (1, 256, DIM), dtype=jnp.float32)
        Wg = jax.random.normal(ks[1], (E, DIM), dtype=jnp.float32) * s
        W1 = jax.random.normal(ks[2], (E, INTER, DIM), dtype=jnp.float32) * s
        W3 = jax.random.normal(ks[3], (E, INTER, DIM), dtype=jnp.float32) * s
        W2 = jax.random.normal(ks[4], (E, DIM, INTER), dtype=jnp.float32) * s
        Ws1 = jax.random.normal(ks[5], (SHARED_INTER, DIM), dtype=jnp.float32) * s
        Ws3 = jax.random.normal(ks[6], (SHARED_INTER, DIM), dtype=jnp.float32) * s
        Ws2 = jax.random.normal(ks[7], (DIM, SHARED_INTER), dtype=jnp.float32) * s
        return {'x': x, 'Wg': Wg, 'W1': W1, 'W3': W3, 'W2': W2, 'Ws1': Ws1, 'Ws3': Ws3, 'Ws2': Ws2}
    _L0_ffn_all = _L0_ffn_setup()
    _L0_ffn_in = {k: v for k, v in _L0_ffn_all.items() if k in ('Wg', 'W1', 'W3', 'W2', 'Ws1', 'Ws3', 'Ws2')}
    del _L0_ffn_all

    def _L1_xattn_setup():
        import jax, jax.numpy as jnp
        import numpy as np
        H = 256
        NH = 16
        HD = H // NH
        FD = 64
        key = jax.random.key(seed)
        ks = jax.random.split(key, 12)
        B, S = (4, 512)
        s = 1.0 / np.sqrt(H)
        sf = 1.0 / np.sqrt(HD)
        return {'query': jax.random.normal(ks[0], (B, S, H), jnp.float32), 'key': jax.random.normal(ks[1], (B, S, H), jnp.float32), 'value': jax.random.normal(ks[2], (B, S, H), jnp.float32), 'attention_mask': jnp.ones((B, S), jnp.float32), 'Wq': jax.random.normal(ks[3], (H, H), jnp.float32) * s, 'bq': jnp.zeros((H,), jnp.float32), 'Wk': jax.random.normal(ks[4], (H, H), jnp.float32) * s, 'bk': jnp.zeros((H,), jnp.float32), 'Wv': jax.random.normal(ks[5], (H, H), jnp.float32) * s, 'bv': jnp.zeros((H,), jnp.float32), 'Wqf': jax.random.normal(ks[6], (FD, HD), jnp.float32) * sf, 'Wkf': jax.random.normal(ks[7], (FD, HD), jnp.float32) * sf, 'Wo': jax.random.normal(ks[8], (H, H), jnp.float32) * s, 'bo': jnp.zeros((H,), jnp.float32)}
    _L1_xattn_all = _L1_xattn_setup()
    _L1_xattn_in = {k: v for k, v in _L1_xattn_all.items() if k in ('Wq', 'bq', 'Wk', 'bk', 'Wv', 'bv', 'Wqf', 'Wkf', 'Wo', 'bo')}
    del _L1_xattn_all

    def _L1_attn_setup():
        import jax, jax.numpy as jnp
        import numpy as np
        B, SQ, H = (2, 256, 256)
        NH = 16
        HN = H // NH
        key = jax.random.key(seed)
        ks = jax.random.split(key, 6)
        query = jax.random.normal(ks[0], (B, SQ, H), dtype=jnp.float32)
        k_in = jax.random.normal(ks[1], (B, SQ, H), dtype=jnp.float32)
        v_in = jax.random.normal(ks[2], (B, SQ, H), dtype=jnp.float32)
        Wqkv = jax.random.normal(ks[3], (3 * H, H), dtype=jnp.float32) * (1.0 / np.sqrt(H))
        Wproj = jax.random.normal(ks[4], (H, H), dtype=jnp.float32) * (1.0 / np.sqrt(H))
        bproj = jnp.zeros((H,), dtype=jnp.float32)
        return {'query': query, 'key': k_in, 'value': v_in, 'Wqkv': Wqkv, 'Wproj': Wproj, 'bproj': bproj}
    _L1_attn_all = _L1_attn_setup()
    _L1_attn_in = {k: v for k, v in _L1_attn_all.items() if k in ('key', 'value', 'Wqkv', 'Wproj', 'bproj')}
    del _L1_attn_all

    def _L1_ffn_setup():
        import jax, jax.numpy as jnp
        import numpy as np
        B, S, D, F, E, SH, K = (2, 256, 256, 128, 16, 2, 2)

        def _experts_all(x, g, gb, w1, b1, w2, b2):
            y = jax.nn.gelu(jnp.einsum('bsd,edf->bsef', x, g) + gb, approximate=False)
            y = y * (jnp.einsum('bsd,edf->bsef', x, w1) + b1)
            return jnp.einsum('bsef,efd->bsed', y, w2) + b2
        key = jax.random.key(seed)
        ks = jax.random.split(key, 8)
        std = 0.02
        mk = lambda k, sh: jax.random.normal(k, sh, jnp.float32) * std
        return {'x': jax.random.normal(ks[0], (B, S, D), jnp.float32), 'wa': mk(ks[1], (D, E)), 'rg': mk(ks[2], (E, D, F)), 'rgb': jnp.zeros((E, F), jnp.float32), 'rw1': mk(ks[3], (E, D, F)), 'rb1': jnp.zeros((E, F), jnp.float32), 'rw2': mk(ks[4], (E, F, D)), 'rb2': jnp.zeros((E, D), jnp.float32), 'sg': mk(ks[5], (SH, D, F)), 'sgb': jnp.zeros((SH, F), jnp.float32), 'sw1': mk(ks[6], (SH, D, F)), 'sb1': jnp.zeros((SH, F), jnp.float32), 'sw2': mk(ks[7], (SH, F, D)), 'sb2': jnp.zeros((SH, D), jnp.float32)}
    _L1_ffn_all = _L1_ffn_setup()
    _L1_ffn_in = {k: v for k, v in _L1_ffn_all.items() if k in ('wa', 'rg', 'rgb', 'rw1', 'rb1', 'rw2', 'rb2', 'sg', 'sgb', 'sw1', 'sb1', 'sw2', 'sb2')}
    del _L1_ffn_all
    return {'x': x, 'ctx_2048': ctx_2048, 'mask_1xSxS2_ff0': mask_1xSxS2_ff0, 'mask_BxS2_ff1': mask_BxS2_ff1, 'L0_xattn_Wq': _L0_xattn_in['Wq'], 'L0_xattn_bq': _L0_xattn_in['bq'], 'L0_xattn_Wk': _L0_xattn_in['Wk'], 'L0_xattn_bk': _L0_xattn_in['bk'], 'L0_xattn_Wv': _L0_xattn_in['Wv'], 'L0_xattn_bv': _L0_xattn_in['bv'], 'L0_xattn_Wo': _L0_xattn_in['Wo'], 'L0_xattn_qn_w': _L0_xattn_in['qn_w'], 'L0_xattn_kn_w': _L0_xattn_in['kn_w'], 'L0_attn_x_r': _L0_attn_in['x_r'], 'L0_attn_x_w': _L0_attn_in['x_w'], 'L0_attn_x_k': _L0_attn_in['x_k'], 'L0_attn_x_v': _L0_attn_in['x_v'], 'L0_attn_x_a': _L0_attn_in['x_a'], 'L0_attn_x_g': _L0_attn_in['x_g'], 'L0_attn_w0': _L0_attn_in['w0'], 'L0_attn_w1': _L0_attn_in['w1'], 'L0_attn_w2': _L0_attn_in['w2'], 'L0_attn_a0': _L0_attn_in['a0'], 'L0_attn_a1': _L0_attn_in['a1'], 'L0_attn_a2': _L0_attn_in['a2'], 'L0_attn_v0': _L0_attn_in['v0'], 'L0_attn_v1': _L0_attn_in['v1'], 'L0_attn_v2': _L0_attn_in['v2'], 'L0_attn_g1': _L0_attn_in['g1'], 'L0_attn_g2': _L0_attn_in['g2'], 'L0_attn_k_k': _L0_attn_in['k_k'], 'L0_attn_k_a': _L0_attn_in['k_a'], 'L0_attn_r_k': _L0_attn_in['r_k'], 'L0_attn_W_r': _L0_attn_in['W_r'], 'L0_attn_W_k': _L0_attn_in['W_k'], 'L0_attn_W_v': _L0_attn_in['W_v'], 'L0_attn_W_o': _L0_attn_in['W_o'], 'L0_attn_gn_scale': _L0_attn_in['gn_scale'], 'L0_attn_gn_offset': _L0_attn_in['gn_offset'], 'L0_ffn_Wg': _L0_ffn_in['Wg'], 'L0_ffn_W1': _L0_ffn_in['W1'], 'L0_ffn_W3': _L0_ffn_in['W3'], 'L0_ffn_W2': _L0_ffn_in['W2'], 'L0_ffn_Ws1': _L0_ffn_in['Ws1'], 'L0_ffn_Ws3': _L0_ffn_in['Ws3'], 'L0_ffn_Ws2': _L0_ffn_in['Ws2'], 'L1_xattn_Wq': _L1_xattn_in['Wq'], 'L1_xattn_bq': _L1_xattn_in['bq'], 'L1_xattn_Wk': _L1_xattn_in['Wk'], 'L1_xattn_bk': _L1_xattn_in['bk'], 'L1_xattn_Wv': _L1_xattn_in['Wv'], 'L1_xattn_bv': _L1_xattn_in['bv'], 'L1_xattn_Wqf': _L1_xattn_in['Wqf'], 'L1_xattn_Wkf': _L1_xattn_in['Wkf'], 'L1_xattn_Wo': _L1_xattn_in['Wo'], 'L1_xattn_bo': _L1_xattn_in['bo'], 'L1_attn_key': _L1_attn_in['key'], 'L1_attn_value': _L1_attn_in['value'], 'L1_attn_Wqkv': _L1_attn_in['Wqkv'], 'L1_attn_Wproj': _L1_attn_in['Wproj'], 'L1_attn_bproj': _L1_attn_in['bproj'], 'L1_ffn_wa': _L1_ffn_in['wa'], 'L1_ffn_rg': _L1_ffn_in['rg'], 'L1_ffn_rgb': _L1_ffn_in['rgb'], 'L1_ffn_rw1': _L1_ffn_in['rw1'], 'L1_ffn_rb1': _L1_ffn_in['rb1'], 'L1_ffn_rw2': _L1_ffn_in['rw2'], 'L1_ffn_rb2': _L1_ffn_in['rb2'], 'L1_ffn_sg': _L1_ffn_in['sg'], 'L1_ffn_sgb': _L1_ffn_in['sgb'], 'L1_ffn_sw1': _L1_ffn_in['sw1'], 'L1_ffn_sb1': _L1_ffn_in['sb1'], 'L1_ffn_sw2': _L1_ffn_in['sw2'], 'L1_ffn_sb2': _L1_ffn_in['sb2']}

def reference(x, ctx_2048, mask_1xSxS2_ff0, mask_BxS2_ff1, L0_xattn_Wq, L0_xattn_bq, L0_xattn_Wk, L0_xattn_bk, L0_xattn_Wv, L0_xattn_bv, L0_xattn_Wo, L0_xattn_qn_w, L0_xattn_kn_w, L0_attn_x_r, L0_attn_x_w, L0_attn_x_k, L0_attn_x_v, L0_attn_x_a, L0_attn_x_g, L0_attn_w0, L0_attn_w1, L0_attn_w2, L0_attn_a0, L0_attn_a1, L0_attn_a2, L0_attn_v0, L0_attn_v1, L0_attn_v2, L0_attn_g1, L0_attn_g2, L0_attn_k_k, L0_attn_k_a, L0_attn_r_k, L0_attn_W_r, L0_attn_W_k, L0_attn_W_v, L0_attn_W_o, L0_attn_gn_scale, L0_attn_gn_offset, L0_ffn_Wg, L0_ffn_W1, L0_ffn_W3, L0_ffn_W2, L0_ffn_Ws1, L0_ffn_Ws3, L0_ffn_Ws2, L1_xattn_Wq, L1_xattn_bq, L1_xattn_Wk, L1_xattn_bk, L1_xattn_Wv, L1_xattn_bv, L1_xattn_Wqf, L1_xattn_Wkf, L1_xattn_Wo, L1_xattn_bo, L1_attn_key, L1_attn_value, L1_attn_Wqkv, L1_attn_Wproj, L1_attn_bproj, L1_ffn_wa, L1_ffn_rg, L1_ffn_rgb, L1_ffn_rw1, L1_ffn_rb1, L1_ffn_rw2, L1_ffn_rb2, L1_ffn_sg, L1_ffn_sgb, L1_ffn_sw1, L1_ffn_sb1, L1_ffn_sw2, L1_ffn_sb2):
    import jax
    import jax.numpy as jnp

    def _L0_xattn_ref(hidden_states, encoder_hidden_states, attention_mask, Wq, bq, Wk, bk, Wv, bv, Wo, qn_w, kn_w):
        import jax, jax.numpy as jnp
        import numpy as np
        H = 256
        NH = 16
        NKV = 4
        HD = 128
        GROUPS = NH // NKV
        EPS = 1e-06
        B, S, SE = (1, 256, 512)

        def _rmsnorm(x, w, eps=EPS):
            xf = x.astype(jnp.float32)
            var = jnp.mean(xf * xf, axis=-1, keepdims=True)
            return (xf * jax.lax.rsqrt(var + eps)).astype(x.dtype) * w
        b, s, _ = hidden_states.shape
        se = encoder_hidden_states.shape[1]
        q = (hidden_states @ Wq + bq).reshape(b, s, NH, HD).transpose(0, 2, 1, 3)
        k = (encoder_hidden_states @ Wk + bk).reshape(b, se, NKV, HD).transpose(0, 2, 1, 3)
        v = (encoder_hidden_states @ Wv + bv).reshape(b, se, NKV, HD).transpose(0, 2, 1, 3)
        k = jnp.repeat(k, GROUPS, axis=1)
        v = jnp.repeat(v, GROUPS, axis=1)
        q = _rmsnorm(q, qn_w)
        k = _rmsnorm(k, kn_w)
        scale = 1.0 / np.sqrt(HD).astype(np.float32)
        scores = jnp.einsum('bhsd,bhed->bhse', q, k) * scale
        scores = scores + attention_mask[:, None, :, :]
        probs = jax.nn.softmax(scores.astype(jnp.float32), axis=-1).astype(q.dtype)
        out = jnp.einsum('bhse,bhed->bhsd', probs, v)
        out = out.transpose(0, 2, 1, 3).reshape(b, s, NH * HD)
        return out @ Wo

    def _L0_attn_ref(x, x_r, x_w, x_k, x_v, x_a, x_g, w0, w1, w2, a0, a1, a2, v0, v1, v2, g1, g2, k_k, k_a, r_k, W_r, W_k, W_v, W_o, gn_scale, gn_offset):
        import jax, jax.numpy as jnp
        import numpy as np
        B, T, C = (4, 128, 256)
        N = 64
        H = C // N
        D_DECAY, D_AAA, D_MV, D_GATE = (64, 64, 32, 128)

        def rwkv7_op(r, w, k, v, a, b):
            Bq, Tq, Cq = r.shape
            decay = jnp.exp(-jnp.exp(w))

            def resh(t):
                return t.reshape(Bq, Tq, H, N).transpose(1, 0, 2, 3)
            rs, ws, ks, vs, as_, bs = map(resh, (r, decay, k, v, a, b))
            S0 = jnp.zeros((Bq, H, N, N), r.dtype)

            def step(S, inp):
                rt, wt, kt, vt, at, bt = inp
                sa = jnp.einsum('bhij,bhj->bhi', S, at)
                S = S * wt[:, :, None, :] + sa[:, :, :, None] * bt[:, :, None, :] + vt[:, :, :, None] * kt[:, :, None, :]
                yt = jnp.einsum('bhij,bhj->bhi', S, rt)
                return (S, yt)
            _, y = jax.lax.scan(step, S0, (rs, ws, ks, vs, as_, bs))
            return y.transpose(1, 0, 2, 3).reshape(Bq, Tq, Cq)

        def _reference_tuple_inner(x, x_r, x_w, x_k, x_v, x_a, x_g, w0, w1, w2, a0, a1, a2, v0, v1, v2, g1, g2, k_k, k_a, r_k, W_r, W_k, W_v, W_o, gn_scale, gn_offset):
            Bq, Tq, Cq = x.shape
            xx = jnp.pad(x, ((0, 0), (1, 0), (0, 0)))[:, :-1, :] - x
            xr = x + xx * x_r
            xw = x + xx * x_w
            xk = x + xx * x_k
            xv = x + xx * x_v
            xa = x + xx * x_a
            xg = x + xx * x_g
            r = xr @ W_r
            w = -jax.nn.softplus(-(w0 + jnp.tanh(xw @ w1) @ w2)) - 0.5
            k = xk @ W_k
            v = xv @ W_v
            v_first = v
            a = jax.nn.sigmoid(a0 + xa @ a1 @ a2)
            g = jax.nn.sigmoid(xg @ g1) @ g2
            kk = (k * k_k).reshape(Bq, Tq, H, N)
            nrm = jnp.sqrt(jnp.sum(kk * kk, axis=-1, keepdims=True))
            kk = (kk / jnp.maximum(nrm, 1e-12)).reshape(Bq, Tq, Cq)
            k2 = k * (1.0 + (a - 1.0) * k_a)
            o = rwkv7_op(r, w, k2, v, -kk, kk * a)
            o = (o.reshape(Bq, Tq, H, N) * gn_scale + gn_offset).reshape(Bq, Tq, Cq)
            r4 = r.reshape(Bq, Tq, H, N)
            k4 = k2.reshape(Bq, Tq, H, N)
            v4 = v.reshape(Bq, Tq, H, N)
            rwkv = jnp.sum(r4 * k4 * r_k, axis=-1, keepdims=True) * v4
            o = o + rwkv.reshape(Bq, Tq, Cq)
            out = o * g @ W_o
            return (out, v_first)
        return _reference_tuple_inner(x, x_r, x_w, x_k, x_v, x_a, x_g, w0, w1, w2, a0, a1, a2, v0, v1, v2, g1, g2, k_k, k_a, r_k, W_r, W_k, W_v, W_o, gn_scale, gn_offset)[0]

    def _L0_ffn_ref(x, Wg, W1, W3, W2, Ws1, Ws3, Ws2):
        import jax, jax.numpy as jnp
        import numpy as np
        DIM = 256
        INTER = 176
        E = 16
        TOPK = 4
        G = 4
        TOPK_G = 2
        N_SHARED = 2
        SHARED_INTER = N_SHARED * INTER
        ROUTE_SCALE = 1.0

        def _moe_forward(x, Wg, W1, W3, W2, Ws1, Ws3, Ws2):
            B, S, D = x.shape
            xt = x.reshape(-1, D)
            T = xt.shape[0]
            scores = jax.nn.softmax(xt @ Wg.T, axis=-1)
            sg = scores.reshape(T, G, E // G)
            group_scores = sg.max(axis=-1)
            gidx = jax.lax.top_k(group_scores, TOPK_G)[1]
            gmask = jax.nn.one_hot(gidx, G, dtype=jnp.float32).sum(axis=1) > 0
            masked = jnp.where(gmask[:, :, None], sg, -jnp.inf).reshape(T, E)
            topi = jax.lax.top_k(masked, TOPK)[1]
            weights = jnp.take_along_axis(scores, topi, axis=1) * ROUTE_SCALE
            combine = jnp.zeros((T, E), xt.dtype).at[jnp.arange(T)[:, None], topi].add(weights)
            h = jax.nn.silu(jnp.einsum('td,eid->eti', xt, W1)) * jnp.einsum('td,eid->eti', xt, W3)
            expert_out = jnp.einsum('eti,edi->etd', h, W2)
            y = jnp.einsum('etd,te->td', expert_out, combine)
            z = jax.nn.silu(xt @ Ws1.T) * (xt @ Ws3.T) @ Ws2.T
            return (y + z).reshape(B, S, D)
        return _moe_forward(x, Wg, W1, W3, W2, Ws1, Ws3, Ws2)

    def _L1_xattn_ref(query, key, value, attention_mask, Wq, bq, Wk, bk, Wv, bv, Wqf, Wkf, Wo, bo):
        import jax, jax.numpy as jnp
        import numpy as np
        H = 256
        NH = 16
        HD = H // NH
        FD = 64
        B, Sq, _ = query.shape
        Sk = key.shape[1]

        def heads(x, W, b, S):
            return (x @ W.T + b).reshape(B, S, NH, HD).transpose(0, 2, 1, 3)
        q = heads(query, Wq, bq, Sq)
        k = heads(key, Wk, bk, Sk)
        v = heads(value, Wv, bv, Sk)
        q_prime = jax.nn.relu(jnp.einsum('bhnd,fd->bhnf', q, Wqf))
        k_prime = jax.nn.relu(jnp.einsum('bhnd,fd->bhnf', k, Wkf))
        k_prime = k_prime * attention_mask[:, None, :, None]
        kv = jnp.einsum('bhnf,bhne->bhfe', k_prime, v)
        qkv = jnp.einsum('bhmf,bhfe->bhme', q_prime, kv)
        k_sum = jnp.sum(k_prime, axis=2)
        qk_sum = jnp.einsum('bhmf,bhf->bhm', q_prime, k_sum)[..., None]
        out = qkv / (qk_sum + 1e-08)
        out = out.transpose(0, 2, 1, 3).reshape(B, Sq, H)
        return out @ Wo.T + bo

    def _L1_attn_ref(query, key, value, Wqkv, Wproj, bproj):
        import jax, jax.numpy as jnp
        import numpy as np
        B, SQ, H = (2, 256, 256)
        NH = 16
        HN = H // NH
        b, sq, h = query.shape
        nh, hn = (NH, HN)
        norm = 1.0 / jnp.sqrt(jnp.asarray(hn, query.dtype))
        x = jnp.transpose(query, (1, 0, 2)).reshape(sq * b, h)
        mixed = x @ Wqkv.T
        mixed = mixed.reshape(sq, b, nh, 3, hn)
        q = mixed[..., 0, :]
        k = mixed[..., 1, :]
        v = mixed[..., 2, :]
        q = q.reshape(sq, b * nh, hn).transpose(1, 0, 2)
        k = k.reshape(sq, b * nh, hn).transpose(1, 0, 2)
        v = v.reshape(sq, b * nh, hn).transpose(1, 0, 2)
        attn = jnp.einsum('gqd,gkd->gqk', q, k) * norm
        attn = jax.nn.softmax(attn, axis=-1)
        ctx = jnp.einsum('gqk,gkd->gqd', attn, v)
        ctx = ctx.reshape(nh, b, sq, hn)
        ctx = jnp.transpose(ctx, (2, 1, 0, 3)).reshape(sq * b, h)
        out = ctx @ Wproj.T + bproj
        out = out.reshape(sq, b, h)
        return jnp.transpose(out, (1, 0, 2))

    def _L1_ffn_ref(x, wa, rg, rgb, rw1, rb1, rw2, rb2, sg, sgb, sw1, sb1, sw2, sb2):
        import jax, jax.numpy as jnp
        import numpy as np
        B, S, D, F, E, SH, K = (2, 256, 256, 128, 16, 2, 2)

        def _experts_all(x, g, gb, w1, b1, w2, b2):
            y = jax.nn.gelu(jnp.einsum('bsd,edf->bsef', x, g) + gb, approximate=False)
            y = y * (jnp.einsum('bsd,edf->bsef', x, w1) + b1)
            return jnp.einsum('bsef,efd->bsed', y, w2) + b2
        aff = jax.nn.sigmoid(jnp.einsum('bsd,de->bse', x, wa))
        topk_p, topk_i = jax.lax.top_k(aff, K)
        topk_p = topk_p / jnp.sum(topk_p, axis=-1, keepdims=True)
        combine = jnp.sum(jax.nn.one_hot(topk_i, E, dtype=x.dtype) * topk_p[..., None], axis=2)
        routed = jnp.einsum('bsed,bse->bsd', _experts_all(x, rg, rgb, rw1, rb1, rw2, rb2), combine)
        shared = jnp.sum(_experts_all(x, sg, sgb, sw1, sb1, sw2, sb2), axis=2)
        return x + shared + routed
    x = x + _L0_xattn_ref(_layernorm(x, axis=-1), ctx_2048, mask_1xSxS2_ff0, L0_xattn_Wq, L0_xattn_bq, L0_xattn_Wk, L0_xattn_bk, L0_xattn_Wv, L0_xattn_bv, L0_xattn_Wo, L0_xattn_qn_w, L0_xattn_kn_w)
    x = x + _L0_attn_ref(_layernorm(x, axis=-1), L0_attn_x_r, L0_attn_x_w, L0_attn_x_k, L0_attn_x_v, L0_attn_x_a, L0_attn_x_g, L0_attn_w0, L0_attn_w1, L0_attn_w2, L0_attn_a0, L0_attn_a1, L0_attn_a2, L0_attn_v0, L0_attn_v1, L0_attn_v2, L0_attn_g1, L0_attn_g2, L0_attn_k_k, L0_attn_k_a, L0_attn_r_k, L0_attn_W_r, L0_attn_W_k, L0_attn_W_v, L0_attn_W_o, L0_attn_gn_scale, L0_attn_gn_offset)
    x = x + _L0_ffn_ref(_layernorm(x, axis=-1), L0_ffn_Wg, L0_ffn_W1, L0_ffn_W3, L0_ffn_W2, L0_ffn_Ws1, L0_ffn_Ws3, L0_ffn_Ws2)
    x = x + _L1_xattn_ref(_layernorm(x, axis=-1), ctx_2048, ctx_2048, mask_BxS2_ff1, L1_xattn_Wq, L1_xattn_bq, L1_xattn_Wk, L1_xattn_bk, L1_xattn_Wv, L1_xattn_bv, L1_xattn_Wqf, L1_xattn_Wkf, L1_xattn_Wo, L1_xattn_bo)
    x = x + _L1_attn_ref(_layernorm(x, axis=-1), L1_attn_key, L1_attn_value, L1_attn_Wqkv, L1_attn_Wproj, L1_attn_bproj)
    x = x + _L1_ffn_ref(_layernorm(x, axis=-1), L1_ffn_wa, L1_ffn_rg, L1_ffn_rgb, L1_ffn_rw1, L1_ffn_rb1, L1_ffn_rw2, L1_ffn_rb2, L1_ffn_sg, L1_ffn_sgb, L1_ffn_sw1, L1_ffn_sb1, L1_ffn_sw2, L1_ffn_sb2)
    return x

_drawn_inputs = setup_inputs


def setup_inputs(seed=0):
    import zlib

    import numpy as np

    out = dict(_drawn_inputs(seed))
    spreads = {'L0_xattn_qn_w': (1.0, 0.6),
     'L0_xattn_kn_w': (1.0, 0.6),
     'L1_xattn_bq': (0.0, 2.0),
     'L1_xattn_bk': (0.0, 2.0),
     'L1_xattn_bv': (0.0, 0.1),
     'L1_xattn_bo': (0.0, 0.1),
     'L1_attn_bproj': (0.0, 0.1),
     'L1_ffn_rgb': (0.0, 0.8),
     'L1_ffn_rb1': (0.0, 0.8),
     'L1_ffn_rb2': (0.0, 0.8),
     'L1_ffn_sgb': (0.0, 0.8),
     'L1_ffn_sb1': (0.0, 0.8),
     'L1_ffn_sb2': (0.0, 0.8)}
    factors = {'L0_xattn_bq': 8.0,
     'L0_xattn_bk': 8.0,
     'L0_xattn_bv': 2.953,
     'L0_attn_x_r': 3.495,
     'L0_attn_x_w': 8.0,
     'L0_attn_x_k': 3.611,
     'L0_attn_x_v': 3.466,
     'L0_attn_x_a': 8.0,
     'L0_attn_x_g': 8.0,
     'L0_attn_w0': 8.0,
     'L0_attn_w1': 8.0,
     'L0_attn_w2': 8.0,
     'L0_attn_a0': 8.0,
     'L0_attn_a1': 8.0,
     'L0_attn_a2': 8.0,
     'L0_attn_g1': 8.0,
     'L0_attn_k_k': 8.0,
     'L0_attn_k_a': 7.714,
     'L0_attn_r_k': 6.157,
     'L0_attn_gn_scale': 8.0,
     'L0_attn_gn_offset': 8.0,
     'L0_ffn_Wg': 8.0,
     'L0_ffn_W1': 8.0,
     'L0_ffn_W3': 8.0,
     'L0_ffn_W2': 8.0,
     'L0_ffn_Ws1': 3.339,
     'L0_ffn_Ws3': 3.293,
     'L0_ffn_Ws2': 3.302,
     'L1_ffn_rg': 8.0,
     'L1_ffn_rw1': 8.0,
     'L1_ffn_rw2': 8.0,
     'L1_ffn_sg': 7.016,
     'L1_ffn_sw1': 6.827,
     'L1_ffn_sw2': 6.482,
     'L1_xattn_Wq': 2.848}
    for name, (base, spread) in spreads.items():
        noise = np.random.default_rng([zlib.crc32(name.encode()), seed]).standard_normal(out[name].shape)
        drawn = base * np.exp(spread * noise) if base else spread * noise
        out[name] = jnp.asarray(drawn.astype(out[name].dtype))
    for name, factor in factors.items():
        out[name] = (out[name] * factor).astype(out[name].dtype)
    return out
```

```python
import math
from contextlib import ExitStack, contextmanager

import concourse.bass as bass
from concourse import mybir
from concourse.alu_op_type import AluOpType as ALU

F32 = mybir.dt.float32
ACT = mybir.ActivationFunctionType
AX = mybir.AxisListType

P = 128
D = 256
CH = D // P
B = 64
SQ = 32
SK = 257
TOK = B * SQ
NT = TOK // P
BLK = 512
NBLK = TOK // BLK
TPB = BLK // P
LN_EPS = 1e-5


class Chain:

    def __init__(self, eng, sem, base=0):
        self.eng, self.sem, self.base, self.n = eng, sem, base, 0

    def link(self, ins):
        self.n += 1
        ins.then_inc(self.sem, 1)
        self.eng.wait_ge(self.sem, self.base + self.n)


class Scope:

    def __init__(self, nc, ctx, tag):
        self.nc, self.ctx, self.tag, self.sems = nc, ctx, tag, []

    def sb(self, name, shape, dt=F32):
        return self.ctx.enter_context(self.nc.sbuf_tensor(f"{self.tag}_{name}", shape, dt))

    def pb(self, name, shape, dt=F32):
        return self.ctx.enter_context(self.nc.psum_tensor(f"{self.tag}_{name}", shape, dt))

    def sem(self, name):
        s = self.ctx.enter_context(self.nc.semaphore(f"{self.tag}_{name}"))
        self.sems.append(s)
        return s

    def clear(self):
        nums = sorted(s.num for s in self.sems)
        with self.nc.Block() as block:
            @block.gpsimd
            def _(pool):
                first = 0
                for i in range(1, len(nums) + 1):
                    if i == len(nums) or nums[i] != nums[i - 1] + 1:
                        pool.sem_clear(range(nums[first], nums[i - 1] + 1))
                        first = i


@contextmanager
def scope(nc, tag):
    with ExitStack() as ctx:
        sc = Scope(nc, ctx, tag)
        yield sc
        sc.clear()


def constants(nc, sc):
    ident = sc.sb("ident", [P, P])
    neg_half = sc.sb("neg_half", [P, 16])
    zeroed = sc.sem("zeroed")
    with nc.Block() as block:
        @block.gpsimd
        def _(pool):
            pool.memset(neg_half[:, :], -0.5)
            pool.memset(ident[:, :], 0.0).then_inc(zeroed, 1)
            pool.wait_ge(zeroed, 1)
            pool.affine_select(out=ident[:, :], in_=ident[:, :], compare_op=ALU.not_equal, fill=1.0,
                               base=0, pattern=[[-1, P]], channel_multiplier=1)
    return ident, neg_half


def layernorm(nc, tag, x_sb, xnT, ident, neg_half, add_to_x=False):
    with scope(nc, tag) as sc:
        stats = sc.sb("stats", [P, NT, 6])
        mv = sc.sb("mv", [P, NT, 2])
        veps = sc.sb("veps", [P, NT])
        rstd = sc.sb("rstd", [P, NT])
        xn = sc.sb("xn", [P, 2, D])
        tp = [sc.pb(f"tp{j}", [P, CH, P]) for j in range(2)]
        stats_done = sc.sem("stats_done")
        mv_done = sc.sem("mv_done")
        veps_done = sc.sem("veps_done")
        rstd_done = sc.sem("rstd_done")
        xn_ready = sc.sem("xn_ready")
        xn_free = sc.sem("xn_free")
        xn_added = sc.sem("xn_added")
        turned = sc.sem("turned")
        tp_free = sc.sem("tp_free")
        with nc.Block() as block:
            @block.vector
            def _(dve):
                with dve.Fori(0, NT) as t:
                    dve.bn_stats(stats[:, bass.ds(t, 1), :], x_sb[:, bass.ds(t, 1), :]).then_inc(stats_done, 1)
                dve.wait_ge(stats_done, NT)
                for t in range(NT):
                    dve.bn_aggr(mv[:, t, :], stats[:, t, :]).then_inc(mv_done, 1)
                dve.wait_ge(mv_done, NT)
                dve.tensor_scalar(veps[:, :], mv[:, :, 1], LN_EPS, None, ALU.add).then_inc(veps_done, 1)
                dve.wait_ge(rstd_done, 1)
                with dve.Fori(0, NT // 2) as i:
                    for j in range(2):
                        t = i * 2 + j
                        dve.wait_ge(xn_free, t + 1)
                        dve.tensor_scalar(xn[:, j, :], x_sb[:, bass.ds(t, 1), :].rearrange("p a c -> p (a c)"),
                                          mv[:, bass.ds(t, 1), 0], rstd[:, bass.ds(t, 1)],
                                          ALU.subtract, ALU.mult).then_inc(xn_ready, 1)
                        if add_to_x:
                            dve.wait_ge(xn_ready, t + 1)
                            xt = x_sb[:, bass.ds(t, 1), :].rearrange("p a c -> p (a c)")
                            dve.tensor_tensor(xt, xt, xn[:, j, :], ALU.add).then_inc(xn_added, 1)
                            dve.wait_ge(xn_added, t + 1)

            @block.gpsimd
            def _(pool):
                pool.wait_ge(veps_done, 1)
                pool.tensor_tensor(rstd[:, :], veps[:, :], neg_half[:, 0:NT], ALU.pow).then_inc(rstd_done, 1)

            @block.tensor
            def _(pe):
                pe.sem_inc(xn_free, 2)
                with pe.Fori(0, NT // 2) as i:
                    for j in range(2):
                        t = i * 2 + j
                        pe.wait_ge(xn_ready, t + 1)
                        pe.wait_ge(tp_free, t + 1)
                        pe.transpose(tp[j][:, 0, :], xn[:, j, 0:P], ident[:, :]).then_inc(turned, 1)
                        pe.transpose(tp[j][:, 1, :], xn[:, j, P:D], ident[:, :]).then_inc(turned, 1)
                        pe.wait_ge(turned, t * 2 + 2)
                        pe.sem_inc(xn_free, 1)

            @block.scalar
            def _(act):
                act.sem_inc(tp_free, 2)
                with act.Fori(0, NT // 2) as i:
                    for j in range(2):
                        t = i * 2 + j
                        act.wait_ge(turned, t * 2 + 2)
                        act.activation(xnT[:, :, bass.ds(t * P, P)], tp[j][:, :, :], ACT.Copy).then_inc(tp_free, 1)


NKV, HD, GQ = 4, 128, 4
QH = NKV * GQ
KVW = NKV * HD
SKM = 2 * P
SPG = P // SQ
NG = B // SPG
RMS_EPS = 1e-6
SCALE = HD ** -0.5


def cross_attention(nc, x_sb, xnT, ident, neg_half, ctx_dram, w, v_last):
    with scope(nc, "xa") as osc:
        wq = osc.sb("wq", [P, CH, QH * HD])
        wkv = osc.sb("wkv", [P, CH, 2 * KVW])
        wo = osc.sb("wo", [P, QH, D])
        bq = osc.sb("bq", [P, QH * HD])
        bk = osc.sb("bk", [P, KVW])
        bv = osc.sb("bv", [P, NKV])
        qn = osc.sb("qn", [P, 1])
        kn = osc.sb("kn", [P, 1])
        mask = osc.sb("mask", [P, SK])
        kT_last = osc.sb("kT_last", [P, NKV, B])
        w_loaded = osc.sem("w_loaded")
        v_stored = osc.sem("v_stored")

        with scope(nc, "xl") as sc:
            cl = sc.sb("cl", [B, D])
            clT = sc.sb("clT", [P, CH, B])
            kb = sc.sb("kb", [B, NKV, HD])
            sq = sc.sb("sq", [B, NKV, HD])
            vb = sc.sb("vb", [B, KVW])
            ss = sc.sb("ss", [B, NKV])
            zero = sc.sb("zero", [B, NKV * KVW])
            pt = sc.pb("pt", [P, BLK])
            pk = sc.pb("pk", [P, BLK])
            pv = sc.pb("pv", [P, BLK])
            cl_loaded = sc.sem("cl_loaded")
            zeroed = sc.sem("zeroed")
            zero_stored = sc.sem("zero_stored")
            turned = sc.sem("turned")
            turned_out = sc.sem("turned_out")
            k_ready = sc.sem("k_ready")
            step = sc.sem("step")
            ss_ready = sc.sem("ss_ready")
            rs_ready = sc.sem("rs_ready")
            vb_ready = sc.sem("vb_ready")
            kn_ready = sc.sem("kn_ready")
            kT_ready = sc.sem("kT_ready")
            with nc.Block() as block:
                @block.sync
                def _(sp):
                    sp.dma_start(cl[:, :], ctx_dram[:, SKM, :]).then_inc(cl_loaded, 16)
                    for dst, src in ((wkv[:, :, 0:KVW], w["Wk"].rearrange("(h p) n -> p h n", p=P)),
                                     (wkv[:, :, KVW:2 * KVW], w["Wv"].rearrange("(h p) n -> p h n", p=P)),
                                     (bk[:, :], w["bk"].rearrange("(o n) -> o n", o=1).to_broadcast([P, KVW])),
                                     (kn[:, :], w["kn_w"].rearrange("(p o) -> p o", o=1)),
                                     (qn[:, :], w["qn_w"].rearrange("(p o) -> p o", o=1)),
                                     (bv[:, :], w["bvT"]),
                                     (wq[:, :, :], w["Wq"].rearrange("(h p) n -> p h n", p=P)),
                                     (bq[:, :], w["bq"].rearrange("(o n) -> o n", o=1).to_broadcast([P, QH * HD])),
                                     (wo[:, :, :], w["Wo"].rearrange("(h p) n -> p h n", p=P))):
                        sp.dma_start(dst, src).then_inc(w_loaded, 16)
                    for i in range(GQ):
                        sp.dma_start(mask[i * SQ:(i + 1) * SQ, :], w["mask"][0, :, :]).then_inc(w_loaded, 16)
                    sp.wait_ge(zeroed, 1)
                    sp.dma_start(v_last.rearrange("b n c -> b (n c)"), zero[:, :]).then_inc(zero_stored, 16)
                    sp.wait_ge(zero_stored, 16)
                    sp.wait_ge(vb_ready, 1)
                    for n in range(NKV):
                        o = slice(n * HD, (n + 1) * HD)
                        sp.dma_start(v_last[:, n, o], vb[:, o]).then_inc(v_stored, 16)
                    sp.wait_ge(v_stored, 16 * NKV)
                    sp.wait_ge(w_loaded, 13 * 16)

                @block.gpsimd
                def _(pool):
                    pool.memset(zero[:, :], 0.0).then_inc(zeroed, 1)
                    pool.wait_ge(ss_ready, 1)
                    pool.tensor_tensor(ss[:, :], ss[:, :], neg_half[0:B, 0:NKV], ALU.pow).then_inc(rs_ready, 1)

                @block.tensor
                def _(pe):
                    pe.wait_ge(cl_loaded, 16)
                    for c in range(CH):
                        mm = pe.transpose(pt[:, c * B:(c + 1) * B], cl[:, c * P:(c + 1) * P], ident[0:B, 0:B])
                    mm.then_inc(turned, 1)
                    pe.wait_ge(turned_out, 1)
                    pe.wait_ge(w_loaded, 13 * 16)
                    for i, dst in enumerate((pk, pv)):
                        for c in range(CH):
                            mm = pe.matmul(dst[0:B, :], clT[:, c, :], wkv[:, c, i * KVW:(i + 1) * KVW], start=(c == 0), stop=(c == 1))
                        mm.then_inc(k_ready, 1)
                    pe.wait_ge(kn_ready, 1)
                    for n in range(NKV):
                        mm = pe.transpose(pt[:, n * B:(n + 1) * B], kb[:, n, :], ident[0:B, 0:B])
                    mm.then_inc(kT_ready, 1)

                @block.vector
                def _(dve):
                    ch = Chain(dve, step)
                    dve.wait_ge(turned, 1)
                    dve.tensor_copy(clT[:, :, :], pt[:, 0:CH * B].rearrange("p (c n) -> p c n", c=CH)).then_inc(turned_out, 1)
                    dve.wait_ge(k_ready, 1)
                    dve.wait_ge(w_loaded, 13 * 16)
                    k3 = pk[0:B, :].rearrange("p (n c) -> p n c", n=NKV)
                    ch.link(dve.tensor_tensor(kb[:, :, :], k3, bk[0:B, :].rearrange("p (n c) -> p n c", n=NKV), ALU.add))
                    ch.link(dve.tensor_tensor(sq[:, :, :], kb[:, :, :], kb[:, :, :], ALU.mult))
                    ch.link(dve.tensor_reduce(ss[:, :], sq[:, :, :], AX.X, ALU.add))
                    dve.tensor_scalar(ss[:, :], ss[:, :], 1.0 / HD, RMS_EPS, ALU.mult, ALU.add).then_inc(ss_ready, 1)
                    dve.wait_ge(k_ready, 2)
                    dve.tensor_copy(vb[:, :], pv[0:B, :]).then_inc(vb_ready, 1)
                    dve.wait_ge(rs_ready, 1)
                    dve.tensor_tensor(kb[:, :, :], kb[:, :, :], ss[:, :].unsqueeze(2).to_broadcast([B, NKV, HD]), ALU.mult).then_inc(kn_ready, 1)
                    ch.link(dve.tensor_scalar(qn[:, :], qn[:, :], SCALE, None, ALU.mult))
                    dve.wait_ge(kT_ready, 1)
                    dve.tensor_scalar(kT_last[:, :, :], pt[:, 0:NKV * B].rearrange("p (n b) -> p n b", n=NKV), kn[:, 0:1], None, ALU.mult)

        with scope(nc, "xm") as sc:
            cx = [sc.sb(f"cx{i}", [P, 2, D]) for i in range(2)]
            v4 = [sc.sb(f"v4_{i}", [NKV, KVW]) for i in range(2)]
            cxT = sc.sb("cxT", [P, CH, SKM])
            kb = sc.sb("kb", [P, 2 * NKV, HD])
            ksq = sc.sb("ksq", [P, 2 * NKV, HD])
            kss = sc.sb("kss", [P, 2 * NKV])
            krs = sc.sb("krs", [P, 2 * NKV])
            kT = sc.sb("kT", [P, NKV, SK])
            V = [sc.sb(f"V{i}", [P, 2, KVW]) for i in range(2)]
            xq = sc.sb("xq", [P, CH, P])
            qb = sc.sb("qb", [P, QH, HD])
            qsq = sc.sb("qsq", [P, QH, HD])
            qss = sc.sb("qss", [P, QH])
            qrs = sc.sb("qrs", [P, QH])
            qT = sc.sb("qT", [P, SPG, QH, SQ])
            sm = sc.sb("sm", [P, NKV, SK])
            pr = sc.sb("pr", [P, NKV, SK])
            mx = sc.sb("mx", [P, NKV])
            neg = sc.sb("neg", [P, NKV])
            tot = sc.sb("tot", [P, NKV])
            rtot = sc.sb("rtot", [P, NKV])
            pT = sc.sb("pT", [P, NKV, 2, P])
            pTl = sc.sb("pTl", [NKV, P])
            oT = sc.sb("oT", [P, QH, P])
            S = [sc.pb(f"S{i}", [P, BLK]) for i in range(2)]
            KA = [sc.pb(f"KA{i}", [P, BLK]) for i in range(4)]
            T = [sc.pb(f"T{i}", [P, BLK]) for i in range(2)]
            cx_loaded = [sc.sem(f"cx_loaded{i}") for i in range(2)]
            v4_loaded = [sc.sem(f"v4_loaded{i}") for i in range(2)]
            cxT_ready = sc.sem("cxT_ready")
            cxT_out = sc.sem("cxT_out")
            kv_ready = sc.sem("kv_ready")
            kb_out = sc.sem("kb_out")
            v_out = sc.sem("v_out")
            ksq_done = sc.sem("ksq_done")
            kss_ready = sc.sem("kss_ready")
            krs_ready = sc.sem("krs_ready")
            kn_ready = sc.sem("kn_ready")
            kt_ready = sc.sem("kt_ready")
            kt_out = sc.sem("kt_out")
            kt_last = sc.sem("kt_last")
            k_step = sc.sem("k_step")
            xq_ready = sc.sem("xq_ready")
            q_ready = sc.sem("q_ready")
            q_out = sc.sem("q_out")
            qsq_done = sc.sem("qsq_done")
            q_step = sc.sem("q_step")
            qss_ready = sc.sem("qss_ready")
            qrs_ready = sc.sem("qrs_ready")
            qn_ready = sc.sem("qn_ready")
            qt_ready = sc.sem("qt_ready")
            qt_out = sc.sem("qt_out")
            s_ready = sc.sem("s_ready")
            s_out = sc.sem("s_out")
            max_done = sc.sem("max_done")
            neg_ready = sc.sem("neg_ready")
            exp_out = sc.sem("exp_out")
            rtot_ready = sc.sem("rtot_ready")
            p_ready = sc.sem("p_ready")
            pt_ready = sc.sem("pt_ready")
            pt_out_a = sc.sem("pt_out_a")
            pt_out_v = sc.sem("pt_out_v")
            pv_ready = sc.sem("pv_ready")
            ot_out = sc.sem("ot_out")
            wo_ready = sc.sem("wo_ready")
            wo_added = sc.sem("wo_added")

            def groups(eng, group):
                with eng.Fori(0, NG - 1) as g:
                    group(g, True)
                group(NG - 1, False)

            with nc.Block() as block:
                @block.sync
                def _(sp):
                    with sp.Fori(0, B // 2) as i:
                        for k in range(2):
                            n = i * 2 + k
                            sp.wait_ge(cxT_ready, n + 1)
                            sp.dma_start(cx[k][:, :, :], ctx_dram[bass.ds(n, 1), 0:SKM, :].rearrange("o (t p) c -> p (o t) c", p=P)
                                         ).then_inc(cx_loaded[k], 16)
                            sp.wait_ge(pv_ready, n + 1)
                            sp.dma_start(v4[k][:, :], v_last[bass.ds(n, 1), :, :].rearrange("o n c -> (o n) c")).then_inc(v4_loaded[k], 16)

                @block.gpsimd
                def _(pool):
                    def keys(n):
                        pool.wait_ge(kss_ready, n + 1)
                        pool.tensor_tensor(krs[:, :], kss[:, :], neg_half[:, 0:2 * NKV], ALU.pow).then_inc(krs_ready, 1)

                    def queries(g):
                        pool.wait_ge(qss_ready, g + 1)
                        pool.tensor_tensor(qrs[:, :], qss[:, :], neg_half[:, 0:QH], ALU.pow).then_inc(qrs_ready, 1)

                    keys(0)
                    queries(0)

                    def group(g, more):
                        for i in range(SPG):
                            if more or i < SPG - 1:
                                keys(g * SPG + i + 1)
                        if more:
                            queries(g + 1)

                    groups(pool, group)

                @block.tensor
                def _(pe):
                    def context(n, k, use):
                        pe.wait_ge(cx_loaded[k], use * 16)
                        for t in range(2):
                            for c in range(CH):
                                mm = pe.transpose(T[0][:, (c * 2 + t) * P:(c * 2 + t + 1) * P], cx[k][:, t, c * P:(c + 1) * P], ident[:, :])
                        mm.then_inc(cxT_ready, 1)

                    def key_value(n, first):
                        pe.wait_ge(cxT_out, n + 1)
                        if not first:
                            pe.wait_ge(v_out, n * 2)
                            pe.wait_ge(kb_out, n * 2)
                        for i in range(2):
                            for t in range(2):
                                for c in range(CH):
                                    mm = pe.matmul(KA[2 * i + t][:, :], cxT[:, c, t * P:(t + 1) * P], wkv[:, c, i * KVW:(i + 1) * KVW],
                                                   start=(c == 0), stop=(c == CH - 1))
                                mm.then_inc(kv_ready, 1)

                    def keys_turned(n):
                        pe.wait_ge(kn_ready, n + 1)
                        for i in range(2):
                            for h in range(2):
                                for t in range(2):
                                    mm = pe.transpose(T[i][:, (h * 2 + t) * P:(h * 2 + t + 1) * P], kb[:, t * NKV + 2 * i + h, :], ident[:, :])
                            mm.then_inc(kt_ready, 1)

                    def queries(g, n):
                        pe.wait_ge(xq_ready, g + 1)
                        pe.wait_ge(v_out, n * 2 + 2)
                        pe.wait_ge(kb_out, n * 2 + 2)
                        for i in range(4):
                            for c in range(CH):
                                mm = pe.matmul(KA[i][:, :], xq[:, c, :], wq[:, c, i * BLK:(i + 1) * BLK], start=(c == 0), stop=(c == CH - 1))
                            mm.then_inc(q_ready, 1)
                        pe.wait_ge(qn_ready, g + 1)
                        pe.wait_ge(kt_out, n * 2 + 2)
                        for i in range(4):
                            if i >= 2:
                                pe.wait_ge(qt_out, g * 4 + i - 1)
                            for h in range(4):
                                mm = pe.transpose(T[i % 2][:, h * P:(h + 1) * P], qb[:, i * 4 + h, :], ident[:, :])
                            mm.then_inc(qt_ready, 1)

                    pe.sem_inc(cxT_ready, 2)
                    pe.sem_inc(pv_ready, 2)
                    context(0, 0, 1)
                    key_value(0, True)
                    keys_turned(0)
                    queries(0, 0)

                    def group(g, more):
                        for i in range(SPG):
                            n = g * SPG + i
                            nxt = more or i < SPG - 1
                            k = (i + 1) % 2
                            pe.wait_ge(kt_out, n * 2 + 2)
                            pe.wait_ge(kt_last, n + 1)
                            pe.wait_ge(qt_out, g * 4 + 4)
                            pe.wait_ge(ot_out, n + 1)
                            pe.wait_ge(wo_added, g + 1)
                            for j in range(NKV):
                                if j >= 2:
                                    pe.wait_ge(s_out, n * 4 + j - 1)
                                pe.matmul(S[j % 2][:, 0:SK], qT[:, i, 4 * j:4 * j + 4, :], kT[:, j, :], start=True, stop=True).then_inc(s_ready, 1)
                            if nxt:
                                context(n + 1, k, g * 2 + (i + 1) // 2 + 1)
                                if i == 0:
                                    pe.wait_ge(q_out, g * 4 + 4)
                                key_value(n + 1, False)
                            pe.wait_ge(p_ready, n + 1)
                            pe.wait_ge(s_out, n * 4 + 4)
                            for h in range(2):
                                for j in range(2):
                                    for t in range(2):
                                        mm = pe.transpose(T[h][:, (j * 2 + t) * P:(j * 2 + t + 1) * P], pr[:, 2 * h + j, t * P:(t + 1) * P], ident[:, :])
                                mm.then_inc(pt_ready, 1)
                            pe.transpose(S[1][0:NKV, 0:P], pr[:, :, SKM], ident[:, :]).then_inc(pt_ready, 1)
                            pe.wait_ge(pt_out_a, n + 1)
                            pe.wait_ge(pt_out_v, n * 2 + 2)
                            pe.wait_ge(v_out, n * 2 + 2)
                            pe.wait_ge(v4_loaded[i % 2], (g * 2 + i // 2) * 16 + 16)
                            for j in range(NKV):
                                o = slice(j * HD, (j + 1) * HD)
                                for t in range(2):
                                    pe.matmul(S[0][:, o], V[i % 2][:, t, o], pT[:, j, t, :], start=(t == 0), stop=False)
                                mm = pe.matmul(S[0][:, o], v4[i % 2][:, o], pTl[:, :], start=False, stop=True)
                            mm.then_inc(pv_ready, 1)
                            if nxt:
                                keys_turned(n + 1)
                            if i == SPG - 1:
                                pe.wait_ge(ot_out, n + 2)
                                for h in range(QH):
                                    mm = pe.matmul(S[1][:, 0:D], oT[:, h, :], wo[:, h, :], start=(h == 0), stop=(h == QH - 1))
                                mm.then_inc(wo_ready, 1)
                                if more:
                                    queries(g + 1, n + 1)

                    groups(pe, group)

                @block.scalar
                def _(act):
                    def context(n):
                        act.wait_ge(cxT_ready, n + 3)
                        act.activation(cxT[:, :, :], T[0][:, :].rearrange("p (c t) -> p c t", c=CH), ACT.Copy).then_inc(cxT_out, 1)

                    def squares(n):
                        act.wait_ge(kb_out, n * 2 + 2)
                        act.activation(ksq[:, :, :], kb[:, :, :], ACT.Square).then_inc(ksq_done, 1)

                    def values(n, k):
                        for t in range(2):
                            act.wait_ge(kv_ready, n * 4 + 3 + t)
                            act.activation(V[k][:, t, :], KA[2 + t][:, :], ACT.Copy).then_inc(v_out, 1)

                    def keys(n):
                        for i in range(2):
                            act.wait_ge(kt_ready, n * 2 + i + 1)
                            act.activation(kT[:, 2 * i:2 * i + 2, 0:SKM], T[i][:, :].rearrange("p (h t) -> p h t", h=2), ACT.Copy,
                                           scale=kn[:, 0:1]).then_inc(kt_out, 1)

                    def query_tokens(g):
                        act.activation(xq[:, :, :], xnT[:, :, bass.ds(g * P, P)], ACT.Copy).then_inc(xq_ready, 1)

                    def queries(g):
                        act.wait_ge(q_out, g * 4 + 4)
                        act.activation(qsq[:, :, :], qb[:, :, :], ACT.Square).then_inc(qsq_done, 1)
                        for i in range(4):
                            act.wait_ge(qt_ready, g * 4 + i + 1)
                            dst = qT[:, :, 4 * i:4 * i + 4, :].rearrange("p b h s -> p h b s")
                            act.activation(dst, T[i % 2][:, :].rearrange("p (h b s) -> p h b s", h=4, b=SPG), ACT.Copy,
                                           scale=qn[:, 0:1]).then_inc(qt_out, 1)

                    query_tokens(0)
                    context(0)
                    squares(0)
                    values(0, 0)
                    keys(0)
                    queries(0)

                    def group(g, more):
                        if more:
                            query_tokens(g + 1)
                        for i in range(SPG):
                            n = g * SPG + i
                            nxt = more or i < SPG - 1
                            if nxt:
                                context(n + 1)
                            act.wait_ge(neg_ready, n + 1)
                            for j in range(NKV):
                                act.activation(pr[:, j, :], sm[:, j, :], ACT.Exp, bias=neg[:, j:j + 1],
                                               accum_out=tot[:, j:j + 1]).then_inc(exp_out, 1)
                            if nxt:
                                squares(n + 1)
                                values(n + 1, (i + 1) % 2)
                            act.wait_ge(pt_ready, n * 3 + 1)
                            act.activation(pT[:, 0:2, :, :], T[0][:, :].rearrange("p (j t q) -> p j t q", j=2, t=2), ACT.Copy).then_inc(pt_out_a, 1)
                            if nxt:
                                keys(n + 1)
                        if more:
                            queries(g + 1)

                    groups(act, group)

                @block.vector
                def _(dve):
                    def biased(n, t):
                        dve.wait_ge(kv_ready, n * 4 + t + 1)
                        dve.tensor_tensor(kb[:, t * NKV:(t + 1) * NKV, :], KA[t][:, :].rearrange("p (h c) -> p h c", h=NKV),
                                          bk[:, :].rearrange("p (h c) -> p h c", h=NKV), ALU.add).then_inc(kb_out, 1)

                    def sums(n):
                        dve.wait_ge(ksq_done, n + 1)
                        dve.tensor_reduce(kss[:, :], ksq[:, :, :], AX.X, ALU.add).then_inc(k_step, 1)
                        dve.wait_ge(k_step, n + 1)
                        dve.tensor_scalar(kss[:, :], kss[:, :], 1.0 / HD, RMS_EPS, ALU.mult, ALU.add).then_inc(kss_ready, 1)

                    def normed(n):
                        dve.wait_ge(krs_ready, n + 1)
                        dve.tensor_tensor(kb[:, :, :], kb[:, :, :], krs[:, :].unsqueeze(2).to_broadcast([P, 2 * NKV, HD]),
                                          ALU.mult).then_inc(kn_ready, 1)
                        dve.tensor_copy(kT[:, :, SKM:SK], kT_last[:, :, bass.ds(n, 1)]).then_inc(kt_last, 1)

                    def queries(g):
                        for i in range(4):
                            dve.wait_ge(q_ready, g * 4 + i + 1)
                            dve.tensor_tensor(qb[:, 4 * i:4 * i + 4, :], KA[i][:, :].rearrange("p (h c) -> p h c", h=4),
                                              bq[:, i * BLK:(i + 1) * BLK].rearrange("p (h c) -> p h c", h=4), ALU.add).then_inc(q_out, 1)
                        dve.wait_ge(qsq_done, g + 1)
                        dve.tensor_reduce(qss[:, :], qsq[:, :, :], AX.X, ALU.add).then_inc(q_step, 1)
                        dve.wait_ge(q_step, g + 1)
                        dve.tensor_scalar(qss[:, :], qss[:, :], 1.0 / HD, RMS_EPS, ALU.mult, ALU.add).then_inc(qss_ready, 1)
                        dve.wait_ge(qrs_ready, g + 1)
                        dve.tensor_tensor(qb[:, :, :], qb[:, :, :], qrs[:, :].unsqueeze(2).to_broadcast([P, QH, HD]), ALU.mult).then_inc(qn_ready, 1)

                    dve.sem_inc(ot_out, 1)
                    dve.sem_inc(wo_added, 1)
                    for t in range(2):
                        biased(0, t)
                    sums(0)
                    normed(0)
                    queries(0)

                    def group(g, more):
                        for i in range(SPG):
                            n = g * SPG + i
                            nxt = more or i < SPG - 1
                            for j in range(NKV):
                                dve.wait_ge(s_ready, n * 4 + j + 1)
                                dve.tensor_tensor(sm[:, j, :], S[j % 2][:, 0:SK], mask[:, :], ALU.add).then_inc(s_out, 1)
                                if j % 2:
                                    dve.wait_ge(s_out, n * 4 + j + 1)
                                    dve.tensor_reduce(mx[:, j - 1:j + 1], sm[:, j - 1:j + 1, :], AX.X, ALU.max).then_inc(max_done, 1)
                            dve.wait_ge(max_done, n * 2 + 2)
                            dve.tensor_scalar(neg[:, :], mx[:, :], -1.0, None, ALU.mult).then_inc(neg_ready, 1)
                            if nxt:
                                biased(n + 1, 0)
                            dve.wait_ge(exp_out, n * 4 + 4)
                            dve.reciprocal(rtot[:, :], tot[:, :]).then_inc(rtot_ready, 1)
                            dve.wait_ge(rtot_ready, n + 1)
                            dve.tensor_tensor(pr[:, :, :], pr[:, :, :], rtot[:, :].unsqueeze(2).to_broadcast([P, NKV, SK]), ALU.mult).then_inc(p_ready, 1)
                            if nxt:
                                biased(n + 1, 1)
                                sums(n + 1)
                                normed(n + 1)
                            dve.wait_ge(pt_ready, n * 3 + 2)
                            dve.tensor_copy(pT[:, 2:4, :, :], T[1][:, :].rearrange("p (j t q) -> p j t q", j=2, t=2)).then_inc(pt_out_v, 1)
                            dve.wait_ge(pt_ready, n * 3 + 3)
                            dve.tensor_copy(pTl[:, :], S[1][0:NKV, 0:P]).then_inc(pt_out_v, 1)
                            dve.wait_ge(pv_ready, n + 3)
                            dst = oT[:, :, i * SQ:(i + 1) * SQ].rearrange("p (j h) s -> p j h s", j=NKV)
                            dve.tensor_tensor(dst, S[0][:, :].rearrange("p (j h s) -> p j h s", j=NKV, h=GQ),
                                              bv[:, :].unsqueeze(2).unsqueeze(3).to_broadcast([P, NKV, GQ, SQ]), ALU.add).then_inc(ot_out, 1)
                        dve.wait_ge(wo_ready, g + 1)
                        xt = x_sb[:, bass.ds(g, 1), :].rearrange("p o c -> p (o c)")
                        dve.tensor_tensor(xt, xt, S[1][:, 0:D], ALU.add).then_inc(wo_added, 1)
                        if more:
                            queries(g + 1)

                    groups(dve, group)


RN = 64
RH = D // RN
SEQ_BLK = BLK // SQ
LEVELS = (2, 4, 8, 16)
PARAMS = ("x_k", "x_w", "x_a", "x_r", "x_v", "x_g", "w0", "a0", "k_k", "k_a", "r_k", "gn_scale", "gn_offset")
DECAY = -math.exp(-0.5)
PROJ = ("k0", "k1", "w1", "a1", "r0", "r1", "z0", "z1", "aa0", "aa1", "v0", "v1", "g1",
        "ns0", "ns1", "vt0", "vt1", "gg0", "gg1")
NQ = len(PROJ)
RING = 6


def rwkv(nc, x_sb, xnT, ident, w):
    with scope(nc, "rwkv") as sc:
        prm = sc.sb("prm", [P, CH, len(PARAMS)])

        def par(name, c, p0=0, p1=P):
            i = PARAMS.index(name)
            return prm[p0:p1, c, i:i + 1]

        W = {n: sc.sb(n, [P, CH, D]) for n in ("Wr", "Wk", "Wv", "Wo")}
        w1 = sc.sb("w1", [P, CH, 64])
        a1 = sc.sb("a1", [P, CH, 64])
        g1 = sc.sb("g1", [P, CH, P])
        w2 = sc.sb("w2", [64, D])
        a2 = sc.sb("a2", [64, D])
        g2 = sc.sb("g2", [P, D])
        head_ones = sc.sb("head_ones", [P, P])
        up_incl = sc.sb("up_incl", [P, P])
        up_strict = sc.sb("up_strict", [P, P])
        lo_pair = sc.sb("lo_pair", [P, P])
        up_pair = sc.sb("up_pair", [P, P])
        merge = [sc.sb(f"merge{n}", [P, P]) for n in LEVELS]
        carry = sc.sb("carry", [P, BLK])
        mix = {n: sc.sb(f"mix_{n}", [P, CH, BLK]) for n in "kwarvg"}
        names = ("xx", "k", "r", "v", "lw", "a", "g", "kk", "tmp", "L", "Lx")
        T = {n: sc.sb(f"T{n}", [P, CH, BLK]) for n in names}
        low = {n: sc.sb(f"low_{n}", [m, BLK]) for n, m in (("w", 64), ("a", 64), ("g", P))}
        A, Bm, K = (sc.sb(n, [P, 2, CH, BLK]) for n in ("facA", "facB", "facK"))
        R = sc.sb("facR", [P, CH, BLK])
        bonus, yT, k_add = mix["g"], mix["v"], mix["r"]
        vtok = sc.sb("vtok", [P, TPB, D])
        inv, invT, ew, mT, akT, rbT, rkT = ([sc.sb(f"{n}{u}", [P, RH, P]) for u in range(2)]
                                            for n in ("inv", "invT", "ew", "mT", "akT", "rbT", "rkT"))
        eT = [[sc.sb(f"eT{u}_{l}", [P, RH, P]) for l in range(len(LEVELS))] for u in range(2)]
        xs, us = ([sc.sb(f"{n}{u}", [P, D]) for u in range(2)] for n in ("xs", "us"))
        bank = [[sc.pb(f"bank{u}_{i}", [P, BLK]) for i in range(4)] for u in range(2)]
        ring = [bank[0][0], bank[0][1], bank[0][2], bank[0][3], bank[1][0], bank[1][1]]
        late = [bank[1][2], bank[1][3]]

        loaded = sc.sem("loaded")
        m_step = sc.sem("m_step")
        masks_ready = sc.sem("masks_ready")
        carry_ready = sc.sem("carry_ready")
        step = sc.sem("step")
        mix_ready = sc.sem("mix_ready")
        proj_ready = sc.sem("proj_ready")
        proj_out = sc.sem("proj_out")
        sq_ready = sc.sem("sq_ready")
        rk_ready = sc.sem("rk_ready")
        bonus_ready = sc.sem("bonus_ready")
        bonus_out = sc.sem("bonus_out")
        decay_ready = sc.sem("decay_ready")
        exp_ready = sc.sem("exp_ready")
        factors_ready = sc.sem("factors_ready")
        gated_ready = sc.sem("gated_ready")
        o_ready = sc.sem("o_ready")
        o_added = sc.sem("o_added")
        g_ready, g_out, t_ready, t_out, e_ready, w_ready, w_out, xv_ready, xv_out, u_ready, u_out, y_ready, y_out = (
            [sc.sem(f"{n}{u}") for u in range(2)] for n in
            ("g_ready", "g_out", "t_ready", "t_out", "e_ready", "w_ready", "w_out",
             "xv_ready", "xv_out", "u_ready", "u_out", "y_ready", "y_out"))
        NL = len(LEVELS)
        NTO = 2 * NL + 2

        def head(buf, h, j):
            if buf is R:
                return buf[:, h // 2, j * P:(j + 1) * P]
            return buf[:, h % 2, h // 2, j * P:(j + 1) * P]

        def heads(mask):
            return mask[:, :].unsqueeze(1).to_broadcast([P, RH, P])

        def four(b):
            return b[:, :].rearrange("p (h s) -> p h s", h=RH)

        with nc.Block() as block:
            @block.sync
            def _(sp):
                n = 0
                for dst, src in ((prm[:, :, :], w["prm"].rearrange("(h p) n -> p h n", p=P)),
                                 (W["Wk"][:, :, :], w["W_k"].rearrange("(h p) n -> p h n", p=P)),
                                 (w1[:, :, :], w["w1"].rearrange("(h p) n -> p h n", p=P)),
                                 (a1[:, :, :], w["a1"].rearrange("(h p) n -> p h n", p=P)),
                                 (W["Wr"][:, :, :], w["W_r"].rearrange("(h p) n -> p h n", p=P)),
                                 (w2[:, :], w["w2"]), (a2[:, :], w["a2"]),
                                 (W["Wv"][:, :, :], w["W_v"].rearrange("(h p) n -> p h n", p=P)),
                                 (g1[:, :, :], w["g1"].rearrange("(h p) n -> p h n", p=P)), (g2[:, :], w["g2"]),
                                 (W["Wo"][:, :, :], w["W_o"].rearrange("(h p) n -> p h n", p=P))):
                    sp.dma_start(dst, src).then_inc(loaded, 16)

            LOADED = 11 * 16

            @block.gpsimd
            def _(pool):
                ch = Chain(pool, m_step)

                def keep(m, pattern, base, mult, op=ALU.is_ge):
                    shape = [P] + [n for _, n in pattern]
                    v = m[:, :] if len(pattern) == 1 else m[:, :].rearrange("p (a b) -> p a b", b=pattern[1][1])
                    return pool.affine_select(out=v, in_=v, compare_op=op, fill=0.0, base=base,
                                              pattern=pattern, channel_multiplier=mult)

                def same_block(m, n):
                    ch.link(keep(m, [[-n, P // n], [0, n]], 0, 1))
                    ch.link(keep(m, [[n, P // n], [0, n]], n - 1, -1))

                for f in (A, Bm, K):
                    ch.link(pool.memset(f[0:RN, 1, :, :], 0.0))
                    ch.link(pool.memset(f[RN:P, 0, :, :], 0.0))
                ch.link(pool.memset(head_ones[:, :], 1.0))
                same_block(head_ones, RN)
                ch.link(pool.memset(up_incl[:, :], 1.0))
                same_block(up_incl, SQ)
                ch.link(keep(up_incl, [[1, P]], 0, -1))
                ch.link(pool.tensor_copy(up_strict[:, :], up_incl[:, :]))
                ch.link(keep(up_strict, [[1, P]], 0, -1, ALU.is_gt))
                ch.link(pool.tensor_copy(up_pair[:, :], up_strict[:, :]))
                same_block(up_pair, 2)
                ch.link(pool.memset(lo_pair[:, :], 1.0))
                same_block(lo_pair, 2)
                ch.link(keep(lo_pair, [[-1, P]], 0, 1, ALU.is_gt))
                for l, n in enumerate(LEVELS):
                    m = merge[l]
                    ch.link(pool.memset(m[:, :], 1.0))
                    same_block(m, 2 * n)
                    ch.link(keep(m, [[2 * n, P // (2 * n)], [0, 2 * n]], n - 1, -1))
                    v = m[:, :].rearrange("p (a b) -> p a b", b=2 * n)
                    ch.link(pool.affine_select(out=v, in_=v, compare_op=ALU.is_ge, fill=0.0, base=-n,
                                               pattern=[[0, P // (2 * n)], [1, 2 * n]], channel_multiplier=0))
                ch.link(pool.memset(carry[:, :], 1.0))
                cv = carry[:, :].rearrange("p (a b) -> p a b", b=SQ)
                ch.link(pool.memset(cv[:, :, 0:1], 0.0))
                pool.tensor_copy(lo_pair[:, 0:1], lo_pair[:, 0:1]).then_inc(masks_ready, 1)
                with pool.Fori(0, NBLK) as b:
                    for pair in range(2):
                        m = b * 2 + pair
                        for u in range(2):
                            pool.wait_ge(g_out[u], m * 5 + 2)
                            for l in range(NL):
                                pool.tensor_tensor(eT[u][l][:, :, :], mT[u][:, :, :], heads(merge[l]),
                                                   ALU.mult).then_inc(e_ready[u], 1)

            def tile_pairs(stages, b):
                for pair in range(2):
                    for stage in stages:
                        for u in range(2):
                            stage(u, 2 * pair + u, b * 2 + pair)

            @block.tensor
            def _(pe):
                pe.wait_ge(loaded, LOADED)
                pe.wait_ge(masks_ready, 1)
                with pe.Fori(0, NBLK) as b:
                    def weights(q):
                        c = int(q[-1])
                        o = slice(c * P, (c + 1) * P)
                        full = {"k": "Wk", "r": "Wr", "v": "Wv"}
                        if q in ("w1", "a1", "g1"):
                            m = q[0]
                            wt = {"w": w1, "a": a1, "g": g1}[m]
                            return [(wt[:, i, :], mix[m][:, i, :]) for i in range(CH)], (mix_ready, b * 6 + "kwarvg".index(m) + 1)
                        if q[:-1] in full:
                            m = q[0]
                            return [(W[full[m]][:, i, o], mix[m][:, i, :]) for i in range(CH)], (mix_ready, b * 6 + "kwarvg".index(m) + 1)
                        lows = {"z": (w2, "w", "w1"), "aa": (a2, "a", "a1"), "gg": (g2, "g", "g1")}
                        if q[:-1] in lows:
                            wt, m, of = lows[q[:-1]]
                            return [(wt[:, o], low[m][:, :])], (proj_out, b * NQ + PROJ.index(of) + 1)
                        return [(head_ones[:, :], T["tmp"][:, c, :])], (sq_ready, b + 1)

                    for i, q in enumerate(PROJ):
                        if i >= RING:
                            pe.wait_ge(proj_out, b * NQ + i - RING + 1)
                        dst = ring[i % RING]
                        if q in ("vt0", "vt1"):
                            pe.wait_ge(proj_out, b * NQ + PROJ.index("v1") + 1)
                            for j in range(2):
                                for c in range(CH):
                                    mm = pe.transpose(dst[:, j * D + c * P:j * D + (c + 1) * P],
                                                      T["v"][:, c, (2 * int(q[-1]) + j) * P:(2 * int(q[-1]) + j + 1) * P],
                                                      ident[:, :])
                        else:
                            pairs, waits = weights(q)
                            pe.wait_ge(*waits)
                            for n, (lhsT, rhs) in enumerate(pairs):
                                mm = pe.matmul(dst[0:lhsT.shape[-1], :], lhsT, rhs, start=(n == 0), stop=(n == len(pairs) - 1))
                        mm.then_inc(proj_ready, 1)
                    pe.wait_ge(rk_ready, b + 1)
                    pe.wait_ge(o_added, b + 1)
                    for c in range(CH):
                        pe.matmul(late[c][:, :], head_ones[:, :], T["kk"][:, c, :], start=True, stop=True).then_inc(bonus_ready, 1)
                    pe.wait_ge(factors_ready, b + 1)
                    pe.wait_ge(bonus_out, b + 1)

                    def products(dst, lhs, rhs, j):
                        for h in range(RH):
                            mm = pe.matmul(four(dst)[:, h, :], head(lhs, h, j), head(rhs, h, j), start=True, stop=True)
                        return mm

                    def s_m(u, j, m):
                        products(bank[u][0], A, Bm, j).then_inc(g_ready[u], 1)
                        products(bank[u][1], Bm, A, j).then_inc(g_ready[u], 1)

                    def s_ak_rb(u, j, m):
                        pe.wait_ge(y_out[u], m + 1)
                        products(bank[u][2], K, A, j).then_inc(g_ready[u], 1)
                        products(bank[u][3], Bm, R, j).then_inc(g_ready[u], 1)

                    def s_rk(u, j, m):
                        pe.wait_ge(g_out[u], m * 5 + 1)
                        products(bank[u][0], K, R, j).then_inc(g_ready[u], 1)

                    def s_xv(u, j, m):
                        pe.wait_ge(g_out[u], m * 5 + 3)
                        for h in range(RH):
                            mm = pe.matmul(four(bank[u][1])[:, h, :], akT[u][:, h, :],
                                           vtok[:, j, (h // 2) * P:(h // 2 + 1) * P], start=True, stop=True)
                        mm.then_inc(xv_ready[u], 1)

                    def s_w(l):
                        def go(u, j, m):
                            pe.wait_ge(t_out[u], m * NTO + 2 * l + 3)
                            pe.wait_ge(e_ready[u], m * NL + l + 1)
                            for h in range(RH):
                                mm = pe.matmul(four(bank[u][2])[:, h, :], eT[u][l][:, h, :], inv[u][:, h, :], start=True, stop=True)
                            mm.then_inc(w_ready[u], 1)
                        return go

                    def s_t(l):
                        def go(u, j, m):
                            pe.wait_ge(w_out[u], m * NL + l + 1)
                            if l == 0:
                                pe.wait_ge(g_out[u], m * 5 + 5)
                            if l < NL - 1:
                                for h in range(RH):
                                    mm = pe.matmul(four(bank[u][3])[:, h, :], invT[u][:, h, :], ew[u][:, h, :], start=True, stop=True)
                                mm.then_inc(t_ready[u], 1)
                            for h in range(RH):
                                mm = pe.matmul(four(bank[u][0])[:, h, :], ew[u][:, h, :], invT[u][:, h, :], start=True, stop=True)
                            mm.then_inc(t_ready[u], 1)
                        return go

                    def s_u(u, j, m):
                        pe.wait_ge(t_out[u], (m + 1) * NTO)
                        pe.wait_ge(xv_out[u], m * 2 + 2)
                        for h in range(RH):
                            mm = pe.matmul(four(bank[u][1])[:, h, :], invT[u][:, h, :],
                                           xs[u][:, (h // 2) * P:(h // 2 + 1) * P], start=True, stop=True)
                        mm.then_inc(u_ready[u], 1)

                    def s_y(u, j, m):
                        pe.wait_ge(u_out[u], m * 2 + 2)
                        for c in range(CH):
                            o = slice(c * P, (c + 1) * P)
                            dst = bank[u][2][:, c * D:(c + 1) * D]
                            pe.matmul(dst, us[u][:, o], rbT[u][:, 2 * c:2 * c + 2, :], start=True, stop=False)
                            mm = pe.matmul(dst, vtok[:, j, o], rkT[u][:, 2 * c:2 * c + 2, :], start=False, stop=True)
                        mm.then_inc(y_ready[u], 1)

                    stages = [s_m, s_ak_rb, s_rk, s_xv]
                    for l in range(NL):
                        stages += [s_w(l), s_t(l)]
                    tile_pairs(stages + [s_u, s_y], b)
                    pe.wait_ge(gated_ready, b + 1)
                    for j in range(TPB):
                        for c in range(CH):
                            mm = pe.matmul(late[j // 2][:, (j % 2) * D:(j % 2 + 1) * D], T["kk"][:, c, j * P:(j + 1) * P],
                                           W["Wo"][:, c, :], start=(c == 0), stop=(c == CH - 1))
                        mm.then_inc(o_ready, 1)

            @block.scalar
            def _(act):
                act.wait_ge(loaded, LOADED)
                with act.Fori(0, NBLK) as b:
                    for i, q in enumerate(PROJ):
                        c = int(q[-1])
                        src = ring[i % RING]
                        act.wait_ge(proj_ready, b * NQ + i + 1)
                        if q in ("w1", "a1", "g1"):
                            fn = {"w": ACT.Tanh, "a": ACT.Copy, "g": ACT.Sigmoid}[q[0]]
                            dst = low[q[0]]
                            ins = act.activation(dst[:, :], src[0:dst.shape[0], :], fn)
                        elif q[:-1] in "krv":
                            ins = act.activation(T[q[0]][:, c, :], src[:, :], ACT.Copy)
                        elif q[:-1] == "z":
                            ins = act.activation(T["lw"][:, c, :], src[:, :], ACT.Sigmoid, bias=par("w0", c))
                        elif q[:-1] == "aa":
                            ins = act.activation(T["a"][:, c, :], src[:, :], ACT.Sigmoid, bias=par("a0", c))
                        elif q[:-1] == "gg":
                            ins = act.activation(T["g"][:, c, :], src[:, :], ACT.Copy)
                        elif q[:-1] == "ns":
                            ins = act.activation(T["xx"][:, c, :], src[:, :], ACT.Sqrt)
                        else:
                            ins = act.activation(vtok[:, 2 * c:2 * c + 2, :], src[:, :].rearrange("p (j c) -> p j c", j=2), ACT.Copy)
                        ins.then_inc(proj_out, 1)
                    act.wait_ge(decay_ready, b + 1)
                    act.activation(mix["k"][:, :, :], T["Lx"][:, :, :], ACT.Exp).then_inc(exp_ready, 1)
                    act.activation(mix["w"][:, :, :], T["L"][:, :, :], ACT.Exp, scale=-1.0).then_inc(exp_ready, 1)
                    act.activation(mix["a"][:, :, :], T["L"][:, :, :], ACT.Exp).then_inc(exp_ready, 1)

                    def pick(dst, src):
                        s4 = src[:, :].rearrange("p (c n) -> p c n", c=CH)
                        d4 = dst[:, :].rearrange("p (c n) -> p c n", c=CH)
                        yield act.activation(d4[:, :, 0:RN], s4[:, :, 0:RN], ACT.Copy)
                        yield act.activation(d4[:, :, RN:P], s4[:, :, P + RN:D], ACT.Copy)

                    def s_xv(u, j, m):
                        act.wait_ge(xv_ready[u], m + 1)
                        for ins in pick(xs[u], bank[u][1]):
                            ins.then_inc(xv_out[u], 1)

                    def s_w(l):
                        def go(u, j, m):
                            act.wait_ge(w_ready[u], m * NL + l + 1)
                            act.activation(ew[u][:, :, :], four(bank[u][2]), ACT.Copy).then_inc(w_out[u], 1)
                        return go

                    def s_u(u, j, m):
                        act.wait_ge(u_ready[u], m + 1)
                        for ins in pick(us[u], bank[u][1]):
                            ins.then_inc(u_out[u], 1)

                    tile_pairs([s_xv] + [s_w(l) for l in range(NL)] + [s_u], b)

            @block.vector
            def _(dve):
                for u in range(2):
                    dve.sem_inc(y_out[u], 1)
                dve.sem_inc(o_added, 1)
                dve.wait_ge(loaded, LOADED)
                dve.wait_ge(masks_ready, 1)
                PER = 12
                with dve.Fori(0, NBLK) as b:
                    ch = Chain(dve, step, b * PER)
                    toks = bass.ds(b * BLK, BLK)

                    def projected(q):
                        dve.wait_ge(proj_out, b * NQ + PROJ.index(q) + 1)

                    for c in range(CH):
                        xv = xnT[:, c, toks].rearrange("p (s t) -> p s t", t=SQ)
                        xxv = T["xx"][:, c, :].rearrange("p (s t) -> p s t", t=SQ)
                        ins = dve.tensor_tensor(xxv[:, :, 1:SQ], xv[:, :, 0:SQ - 1], xv[:, :, 1:SQ], ALU.subtract)
                        ins = dve.tensor_scalar(xxv[:, :, 0:1], xv[:, :, 0:1], -1.0, None, ALU.mult)
                    ch.link(ins)
                    for m in "kwarvg":
                        for c in range(CH):
                            ins = dve.scalar_tensor_tensor(mix[m][:, c, :], T["xx"][:, c, :], par("x_" + m, c),
                                                           xnT[:, c, toks], ALU.mult, ALU.add)
                        ins.then_inc(mix_ready, 1)
                    projected("k1")
                    for c in range(CH):
                        ins = dve.tensor_scalar(T["kk"][:, c, :], T["k"][:, c, :], par("k_k", c), None, ALU.mult)
                    ch.link(ins)
                    dve.tensor_tensor(T["tmp"][:, :, :], T["kk"][:, :, :], T["kk"][:, :, :], ALU.mult).then_inc(sq_ready, 1)
                    projected("z1")
                    ch.link(dve.tensor_scalar(T["lw"][:, :, :], T["lw"][:, :, :], DECAY, None, ALU.mult))
                    for c in range(CH):
                        ins = dve.tensor_tensor_scan(T["L"][:, c, :], carry[:, :], T["lw"][:, c, :], 0.0, ALU.mult, ALU.add)
                    ch.link(ins)
                    dve.tensor_tensor(T["Lx"][:, :, :], T["L"][:, :, :], T["lw"][:, :, :], ALU.subtract).then_inc(decay_ready, 1)
                    projected("aa1")
                    for c in range(CH):
                        ins = dve.tensor_scalar(k_add[:, c, :], T["a"][:, c, :], 1.0, par("k_a", c), ALU.subtract, ALU.mult)
                    ch.link(ins)
                    ch.link(dve.scalar_tensor_tensor(T["k"][:, :, :], k_add[:, :, :], 1.0, T["k"][:, :, :], ALU.add, ALU.mult))
                    projected("ns1")
                    ch.link(dve.tensor_scalar(T["xx"][:, :, :], T["xx"][:, :, :], 1e-12, None, ALU.max))
                    ch.link(dve.reciprocal(T["xx"][:, :, :], T["xx"][:, :, :]))
                    ch.link(dve.tensor_tensor(T["xx"][:, :, :], T["kk"][:, :, :], T["xx"][:, :, :], ALU.mult))
                    for c in range(CH):
                        ins = dve.scalar_tensor_tensor(T["kk"][:, c, :], T["r"][:, c, :], par("r_k", c), T["k"][:, c, :], ALU.mult, ALU.mult)
                    ins.then_inc(rk_ready, 1)
                    dve.wait_ge(exp_ready, b * 3 + 3)
                    ch.link(dve.tensor_tensor(T["lw"][:, :, :], T["xx"][:, :, :], T["a"][:, :, :], ALU.mult))
                    for i in range(2):
                        o = slice(RN * i, RN * i + RN)
                        dve.scalar_tensor_tensor(A[o, i, :, :], T["xx"][o, :, :], -1.0, mix["k"][o, :, :], ALU.mult, ALU.mult)
                        dve.tensor_tensor(Bm[o, i, :, :], T["lw"][o, :, :], mix["w"][o, :, :], ALU.mult)
                        dve.tensor_tensor(K[o, i, :, :], T["k"][o, :, :], mix["w"][o, :, :], ALU.mult)
                    dve.tensor_tensor(R[:, :, :], T["r"][:, :, :], mix["a"][:, :, :], ALU.mult).then_inc(factors_ready, 1)
                    dve.wait_ge(bonus_ready, b * 2 + 2)
                    for c in range(CH):
                        ins = dve.tensor_tensor(bonus[:, c, :], late[c][:, :], T["v"][:, c, :], ALU.mult)
                    ins.then_inc(bonus_out, 1)

                    def masked(u, dst, i, mask, m, k):
                        dve.wait_ge(g_ready[u], m * 5 + k)
                        dve.tensor_tensor(dst[u][:, :, :], four(bank[u][i]), heads(mask), ALU.mult).then_inc(g_out[u], 1)

                    def s_m(u, j, m):
                        masked(u, inv, 0, lo_pair, m, 1)
                        masked(u, mT, 1, up_strict, m, 2)
                        dve.wait_ge(g_out[u], m * 5 + 2)
                        dve.tensor_tensor(inv[u][:, :, :], inv[u][:, :, :], heads(ident), ALU.add).then_inc(t_out[u], 1)
                        dve.tensor_tensor(invT[u][:, :, :], mT[u][:, :, :], heads(up_pair), ALU.mult).then_inc(t_out[u], 1)
                        dve.wait_ge(t_out[u], m * NTO + 2)
                        dve.tensor_tensor(invT[u][:, :, :], invT[u][:, :, :], heads(ident), ALU.add).then_inc(t_out[u], 1)

                    def s_ak_rb(u, j, m):
                        masked(u, akT, 2, up_strict, m, 3)
                        masked(u, rbT, 3, up_incl, m, 4)

                    def s_rk(u, j, m):
                        masked(u, rkT, 0, up_incl, m, 5)

                    def s_t(l):
                        def go(u, j, m):
                            n = m * (2 * NL - 1) + 2 * l
                            if l < NL - 1:
                                dve.wait_ge(t_ready[u], n + 1)
                                dve.tensor_tensor(inv[u][:, :, :], inv[u][:, :, :], four(bank[u][3]), ALU.add).then_inc(t_out[u], 1)
                                n += 1
                            dve.wait_ge(t_ready[u], n + 1)
                            dve.tensor_tensor(invT[u][:, :, :], invT[u][:, :, :], four(bank[u][0]), ALU.add).then_inc(t_out[u], 1)
                        return go

                    def s_y(u, j, m):
                        dve.wait_ge(y_ready[u], m + 1)
                        yb = bank[u][2][:, :].rearrange("p (c n) -> p c n", c=CH)
                        dve.tensor_copy(yT[0:RN, :, j * P:(j + 1) * P], yb[0:RN, :, 0:P])
                        dve.tensor_copy(yT[RN:P, :, j * P:(j + 1) * P], yb[RN:P, :, P:D]).then_inc(y_out[u], 1)

                    tile_pairs([s_m, s_ak_rb, s_rk] + [s_t(l) for l in range(NL)] + [s_y], b)
                    for u in range(2):
                        dve.wait_ge(y_out[u], b * 2 + 3)
                    for c in range(CH):
                        ins = dve.tensor_scalar(yT[:, c, :], yT[:, c, :], par("gn_scale", c), par("gn_offset", c), ALU.mult, ALU.add)
                    ch.link(ins)
                    ch.link(dve.tensor_tensor(yT[:, :, :], yT[:, :, :], bonus[:, :, :], ALU.add))
                    dve.tensor_tensor(T["kk"][:, :, :], yT[:, :, :], T["g"][:, :, :], ALU.mult).then_inc(gated_ready, 1)
                    dve.wait_ge(o_ready, b * TPB + TPB)
                    for h in range(2):
                        xh = x_sb[:, bass.ds(b * TPB + 2 * h, 2), :]
                        ins = dve.tensor_tensor(xh, xh, late[h][:, :].rearrange("p (j c) -> p j c", j=2), ALU.add)
                    ins.then_inc(o_added, 1)
                    assert ch.n == PER, ch.n


BF16 = mybir.dt.bfloat16
E = 16
TOPK0, GROUPS, TOPK_G, PER_G = 4, 4, 2, 4
TOPK1 = 2


def routing(nc, tag, xnT, ident, wg_view, combT, grouped, x_sb=None, out_bias=None):
    with scope(nc, tag) as sc:
        wg = sc.sb("wg", [P, CH, E])
        lgT = sc.sb("lgT", [E, TOK])
        lt = sc.sb("lt", [P, E, E])
        s = sc.sb("s", [P, NT, E])
        key = sc.sb("key", [P, NT, E])
        tmp = sc.sb("tmp", [P, NT, E])
        col = sc.sb("col", [P, NT])
        gkey = sc.sb("gkey", [P, NT, GROUPS])
        rank = sc.sb("rank", [P, NT, E])
        pair = sc.sb("pair", [P, NT, E * E])
        pair2 = sc.sb("pair2", [P, NT, E * E])
        pieces = sc.sb("pieces", [P, NT, 3 * E])
        pieceb = sc.sb("pieceb", [P, NT, E], BF16)
        lp = [sc.pb(f"lp{j}", [P, BLK]) for j in range(2)]
        tm = sc.pb("tm", [P, NT, E])
        ct = [sc.pb(f"ct{j}", [P, BLK]) for j in range(2)]
        if out_bias:
            routed_b, shared_b = out_bias
            NB = E + shared_b.shape[0]
            sx = sc.sb("sx", [P, NT, NB])
            cb = sc.sb("cb", [NB, TOK])
            ob = sc.sb("ob", [NB, D])
            sx_ready = sc.sem("sx_ready")
            sx_turned = sc.sem("sx_turned")
            cb_out = sc.sem("cb_out")
            bias_ready = sc.sem("bias_ready")
            bias_added = sc.sem("bias_added")
        loaded = sc.sem("loaded")
        ones_set = sc.sem("ones_set")
        lt_ready = sc.sem("lt_ready")
        logits_ready = sc.sem("logits_ready")
        logits_out = sc.sem("logits_out")
        turned = sc.sem("turned")
        max_off = sc.sem("max_off")
        prob_ready = sc.sem("prob_ready")
        step = sc.sem("step")
        pieces_ready = sc.sem("pieces_ready")
        comb_turned = sc.sem("comb_turned")
        comb_out = sc.sem("comb_out")
        with nc.Block() as block:
            @block.sync
            def _(sp):
                sp.dma_start(wg[:, :, :], wg_view).then_inc(loaded, 16)
                if out_bias:
                    sp.dma_start(ob[0:E, :], routed_b).then_inc(loaded, 16)
                    sp.dma_start(ob[E:NB, :], shared_b).then_inc(loaded, 16)

            @block.gpsimd
            def _(pool):
                pool.memset(lt[:, :, :], 1.0).then_inc(ones_set, 1)
                pool.wait_ge(ones_set, 1)
                pool.affine_select(out=lt[:, :, :], in_=lt[:, :, :], compare_op=ALU.is_gt, fill=0.0,
                                   base=0, pattern=[[1, E], [-1, E]], channel_multiplier=0).then_inc(lt_ready, 1)

            @block.tensor
            def _(pe):
                pe.wait_ge(loaded, 48 if out_bias else 16)
                for b in range(NBLK):
                    if b >= 2:
                        pe.wait_ge(logits_out, b - 1)
                    for c in range(CH):
                        mm = pe.matmul(lp[b % 2][0:E, :], wg[:, c, :], xnT[:, c, b * BLK:(b + 1) * BLK],
                                       start=(c == 0), stop=(c == CH - 1))
                    mm.then_inc(logits_ready, 1)
                pe.wait_ge(logits_out, NBLK)
                for t in range(NT):
                    mm = pe.transpose(tm[:, t, :], lgT[:, t * P:(t + 1) * P], ident[0:E, 0:E])
                mm.then_inc(turned, 1)
                pe.wait_ge(pieces_ready, 3)
                for b in range(NBLK):
                    if b >= 2:
                        pe.wait_ge(comb_out, b - 1)
                    for j in range(TPB):
                        mm = pe.transpose(ct[b % 2][0:3 * E, j * P:(j + 1) * P], pieces[:, b * TPB + j, :], ident[:, :])
                    mm.then_inc(comb_turned, 1)
                if out_bias:
                    pe.wait_ge(sx_ready, 2)
                    for b in range(NBLK):
                        if b >= 2:
                            pe.wait_ge(cb_out, b - 1)
                        for j in range(TPB):
                            mm = pe.transpose(lp[b % 2][0:NB, j * P:(j + 1) * P], sx[:, b * TPB + j, :], ident[:, :])
                        mm.then_inc(sx_turned, 1)
                    pe.wait_ge(cb_out, NBLK)
                    for t2 in range(NT // 2):
                        if t2 >= 2:
                            pe.wait_ge(bias_added, t2 - 1)
                        for j in range(2):
                            mm = pe.matmul(lp[t2 % 2][:, j * D:(j + 1) * D], cb[:, (2 * t2 + j) * P:(2 * t2 + j + 1) * P],
                                           ob[:, :], start=True, stop=True)
                        mm.then_inc(bias_ready, 1)

            @block.scalar
            def _(act):
                for b in range(NBLK):
                    act.wait_ge(logits_ready, b + 1)
                    act.activation(lgT[:, b * BLK:(b + 1) * BLK], lp[b % 2][0:E, :], ACT.Copy).then_inc(logits_out, 1)
                if grouped:
                    act.wait_ge(max_off, 1)
                    act.activation(s[:, :, :], tmp[:, :, :], ACT.Exp).then_inc(prob_ready, 1)
                else:
                    act.wait_ge(turned, 1)
                    act.activation(s[:, :, :], tm[:, :, :], ACT.Sigmoid).then_inc(prob_ready, 1)
                for b in range(NBLK):
                    act.wait_ge(comb_turned, b + 1)
                    act.activation(combT[0:3 * E, b * BLK:(b + 1) * BLK], ct[b % 2][0:3 * E, :], ACT.Copy).then_inc(comb_out, 1)
                if out_bias:
                    for b in range(NBLK):
                        act.wait_ge(sx_turned, b + 1)
                        act.activation(cb[:, b * BLK:(b + 1) * BLK], lp[b % 2][0:NB, :], ACT.Copy).then_inc(cb_out, 1)

            @block.vector
            def _(dve):
                ch = Chain(dve, step)

                def bc(ap, n):
                    return ap.unsqueeze(2).to_broadcast([P, NT, n])

                def ranks(keys, n, out):
                    pv = pair[:, :, 0:n * n].rearrange("p t (i j) -> p t i j", j=n)
                    pv2 = pair2[:, :, 0:n * n].rearrange("p t (i j) -> p t i j", j=n)
                    kj = keys.unsqueeze(2).to_broadcast([P, NT, n, n])
                    ki = keys.unsqueeze(3).to_broadcast([P, NT, n, n])
                    ch.link(dve.tensor_tensor(pv2, kj, ki, ALU.is_equal))
                    ch.link(dve.tensor_tensor(pv2, pv2, lt[:, 0:n, 0:n].unsqueeze(1).to_broadcast([P, NT, n, n]), ALU.mult))
                    ch.link(dve.tensor_tensor(pv, kj, ki, ALU.is_gt))
                    ch.link(dve.tensor_tensor(pv, pv, pv2, ALU.add))
                    ch.link(dve.tensor_reduce(out, pv, AX.X, ALU.add))

                dve.wait_ge(turned, 1)
                if grouped:
                    ch.link(dve.tensor_reduce(col[:, :], tm[:, :, :], AX.X, ALU.max))
                    dve.tensor_tensor(tmp[:, :, :], tm[:, :, :], bc(col[:, :], E), ALU.subtract).then_inc(max_off, 1)
                    dve.wait_ge(prob_ready, 1)
                    ch.link(dve.tensor_reduce(col[:, :], s[:, :, :], AX.X, ALU.add))
                    ch.link(dve.reciprocal(col[:, :], col[:, :]))
                    ch.link(dve.tensor_tensor(s[:, :, :], s[:, :, :], bc(col[:, :], E), ALU.mult))
                    dve.wait_ge(lt_ready, 1)
                    ch.link(dve.tensor_reduce(gkey[:, :, :], s[:, :, :].rearrange("p t (g k) -> p t g k", g=GROUPS), AX.X, ALU.max))
                    ranks(gkey[:, :, :], GROUPS, rank[:, :, 0:GROUPS])
                    ch.link(dve.tensor_scalar(gkey[:, :, :], rank[:, :, 0:GROUPS], TOPK_G - 0.5, None, ALU.is_lt))
                    g4 = gkey[:, :, :].unsqueeze(3).to_broadcast([P, NT, GROUPS, PER_G])
                    k4 = key[:, :, :].rearrange("p t (g k) -> p t g k", g=GROUPS)
                    s4 = s[:, :, :].rearrange("p t (g k) -> p t g k", g=GROUPS)
                    t4 = tmp[:, :, :].rearrange("p t (g k) -> p t g k", g=GROUPS)
                    ch.link(dve.tensor_tensor(k4, s4, g4, ALU.mult))
                    ch.link(dve.tensor_copy(t4, g4))
                    ch.link(dve.scalar_tensor_tensor(key[:, :, :], tmp[:, :, :], 1.0, key[:, :, :], ALU.subtract, ALU.add))
                    ranks(key[:, :, :], E, rank[:, :, :])
                    ch.link(dve.scalar_tensor_tensor(s[:, :, :], rank[:, :, :], TOPK0 - 0.5, s[:, :, :], ALU.is_lt, ALU.mult))
                else:
                    dve.wait_ge(prob_ready, 1)
                    dve.wait_ge(lt_ready, 1)
                    ranks(s[:, :, :], E, rank[:, :, :])
                    ch.link(dve.scalar_tensor_tensor(s[:, :, :], rank[:, :, :], TOPK1 - 0.5, s[:, :, :], ALU.is_lt, ALU.mult))
                    ch.link(dve.tensor_reduce(col[:, :], s[:, :, :], AX.X, ALU.add))
                    ch.link(dve.reciprocal(col[:, :], col[:, :]))
                    ch.link(dve.tensor_tensor(s[:, :, :], s[:, :, :], bc(col[:, :], E), ALU.mult))
                    dve.tensor_copy(sx[:, :, 0:E], s[:, :, :]).then_inc(sx_ready, 1)
                    dve.memset(sx[:, :, E:NB], 1.0).then_inc(sx_ready, 1)
                for k in range(3):
                    ch.link(dve.tensor_copy(pieceb[:, :, :], s[:, :, :]))
                    dve.tensor_copy(pieces[:, :, k * E:(k + 1) * E], pieceb[:, :, :]).then_inc(pieces_ready, 1)
                    if k < 2:
                        ch.link(dve.tensor_tensor(s[:, :, :], s[:, :, :], pieceb[:, :, :], ALU.subtract))
                if out_bias:
                    for t2 in range(NT // 2):
                        dve.wait_ge(bias_ready, t2 + 1)
                        xt = x_sb[:, 2 * t2:2 * t2 + 2, :]
                        dve.tensor_tensor(xt, xt, lp[t2 % 2][:, :].rearrange("p (j c) -> p j c", j=2),
                                          ALU.add).then_inc(bias_added, 1)


def experts(nc, tag, x_sb, xnT, combT, chunks, act_func, load_weights, n_feat, n_loads, biases=None):
    NC = len(chunks)
    with scope(nc, tag) as sc:
        w1 = sc.sb("w1", [P, CH, n_feat])
        w3 = sc.sb("w3", [P, CH, n_feat])
        w2 = sc.sb("w2", [P, NC, D])
        n_routed = sum(n for n, r in chunks if r)
        ex = sc.sb("ex", [3 * E, n_routed], BF16)
        gate = sc.sb("gate", [P, 2, BLK])
        up = sc.sb("up", [P, 2, BLK])
        hid = sc.sb("hid", [P, 2, BLK])
        if biases:
            b1 = sc.sb("b1", [P, NC])
            b3 = sc.sb("b3", [P, NC])
        p1 = [sc.pb(f"p1_{j}", [P, BLK]) for j in range(2)]
        p3 = [sc.pb(f"p3_{j}", [P, BLK]) for j in range(2)]
        px = [sc.pb(f"px_{j}", [P, BLK]) for j in range(2)]
        acc = sc.pb("acc", [P, TPB, D])
        loads = [sc.sem(f"loaded{k}") for k in range(n_loads)]
        h1_ready = sc.sem("h1_ready")
        h3_ready = sc.sem("h3_ready")
        cx_ready = sc.sem("cx_ready")
        gate_done = sc.sem("gate_done")
        up_done = sc.sem("up_done")
        hid_done = sc.sem("hid_done")
        down_done = sc.sem("down_done")
        acc_ready = sc.sem("acc_ready")
        acc_free = sc.sem("acc_free")
        AHEAD = 2
        need = {}
        with nc.Block() as block:
            @block.sync
            def _(sp):
                need.update(load_weights(sp, w1, w3, w2, ex, loads, (b1, b3) if biases else None))

            @block.tensor
            def _(pe):
                pe.sem_inc(down_done, AHEAD)
                with pe.Fori(0, NBLK) as b:
                    toks = bass.ds(b * BLK, BLK)
                    for f in range(NC + 1):
                        if f < NC:
                            rows, routed = chunks[f]
                            f0 = sum(n for n, _ in chunks[:f])
                            n = b * NC + f
                            for arrived in need[f]:
                                pe.wait_ge(*arrived)
                            pe.wait_ge(gate_done, n + 1)
                            for c in range(CH):
                                mm = pe.matmul(p1[f % 2][0:rows, :], w1[:, c, f0:f0 + rows], xnT[:, c, toks],
                                               start=(c == 0), stop=(c == CH - 1))
                            mm.then_inc(h1_ready, 1)
                            pe.wait_ge(up_done, n + 1)
                            pe.wait_ge(hid_done, n + 1)
                            for c in range(CH):
                                mm = pe.matmul(p3[f % 2][0:rows, :], w3[:, c, f0:f0 + rows], xnT[:, c, toks],
                                               start=(c == 0), stop=(c == CH - 1))
                            mm.then_inc(h3_ready, 1)
                            if routed:
                                pe.matmul(px[f % 2][0:rows, :], ex[:, f0:f0 + rows], combT[0:3 * E, toks],
                                          start=True, stop=True).then_inc(cx_ready, 1)
                        if f == 0:
                            pe.wait_ge(acc_free, b + 1)
                        if f >= 1:
                            rows, _ = chunks[f - 1]
                            pe.wait_ge(hid_done, b * NC + f + AHEAD)
                            for j in range(TPB):
                                mm = pe.matmul(acc[:, j, :], hid[0:rows, (f - 1) % 2, j * P:(j + 1) * P],
                                               w2[0:rows, f - 1, :], start=(f == 1 and j % 2 == 0),
                                               stop=(f == NC), skip_group_check=True)
                            mm.then_inc(down_done, 1)
                    pe.wait_ge(down_done, b * NC + NC + AHEAD)
                    pe.sem_inc(acc_ready, 1)

            @block.scalar
            def _(act):
                act.sem_inc(gate_done, AHEAD)
                if biases:
                    act.wait_ge(*need["bias"])
                with act.Fori(0, NBLK) as b:
                    for f, (rows, routed) in enumerate(chunks):
                        n = b * NC + f
                        act.wait_ge(h1_ready, n + 1)
                        act.wait_ge(up_done, n + 1)
                        bias = b1[0:rows, f:f + 1] if biases else 0.0
                        act.activation(gate[0:rows, f % 2, :], p1[f % 2][0:rows, :], act_func,
                                       bias=bias).then_inc(gate_done, 1)

            @block.vector
            def _(dve):
                n_rt = sum(1 for _, r in chunks if r)
                dve.sem_inc(up_done, AHEAD)
                dve.sem_inc(hid_done, AHEAD)
                dve.sem_inc(acc_free, 1)
                if biases:
                    dve.wait_ge(*need["bias"])
                with dve.Fori(0, NBLK) as b:
                    for f, (rows, routed) in enumerate(chunks):
                        n = b * NC + f
                        dve.wait_ge(h3_ready, n + 1)
                        dve.wait_ge(gate_done, n + 1 + AHEAD)
                        dve.wait_ge(down_done, n + 1)
                        dst = up if routed else hid
                        if biases:
                            ins = dve.scalar_tensor_tensor(dst[0:rows, f % 2, :], p3[f % 2][0:rows, :],
                                                           b3[0:rows, f:f + 1], gate[0:rows, f % 2, :], ALU.add, ALU.mult)
                        else:
                            ins = dve.tensor_tensor(dst[0:rows, f % 2, :], p3[f % 2][0:rows, :],
                                                    gate[0:rows, f % 2, :], ALU.mult)
                        ins.then_inc(up_done, 1)
                        dve.wait_ge(up_done, n + 1 + AHEAD)
                        if routed:
                            dve.wait_ge(cx_ready, b * n_rt + sum(1 for _, r in chunks[:f] if r) + 1)
                            dve.tensor_tensor(hid[0:rows, f % 2, :], up[0:rows, f % 2, :], px[f % 2][0:rows, :],
                                              ALU.mult).then_inc(hid_done, 1)
                        else:
                            dve.sem_inc(hid_done, 1)
                    dve.wait_ge(acc_ready, b + 1)
                    xb = x_sb[:, bass.ds(b * TPB, TPB), :]
                    for h in range(2):
                        xh = x_sb[:, bass.ds(b * TPB + 2 * h, 2), :]
                        ins = dve.tensor_tensor(xh, xh, acc[:, 2 * h:2 * h + 2, :], ALU.add)
                    ins.then_inc(acc_free, 1)


HID0, SHID0 = 176, 352
F0 = E * HID0
CHUNKS0 = [(P, True)] * (F0 // P) + [(P, False), (P, False), (SHID0 - 2 * P, False)]
PIECE = 5


def ffn0(nc, x_sb, xnT, ident, combT, w):
    routing(nc, "route0", xnT, ident, w["Wg"].rearrange("(h p) e -> p h e", p=P), combT, True)

    n_all = F0 + SHID0
    n_loads = 1 + -(-len(CHUNKS0) // PIECE)

    def load(sp, w1, w3, w2, ex, loads, _):
        need = {}
        sp.dma_start(ex[:, :], w["expand"].bitcast(BF16)).then_inc(loads[0], 16)
        for n, k in enumerate(range(0, len(CHUNKS0), PIECE)):
            f0, f1 = k * P, min((k + PIECE) * P, n_all)
            landed, count = loads[1 + n], 48
            for dst, src in ((w1, w["W1"]), (w3, w["W3"])):
                sp.dma_start(dst[:, :, f0:f1], src[:, f0:f1].rearrange("(h p) f -> p h f", p=P)).then_inc(landed, 16)
            whole = (f1 - f0) // P
            sp.dma_start(w2[:, k:k + whole, :], w["W2"][f0:f0 + whole * P, :].rearrange("(k p) c -> p k c", p=P)).then_inc(landed, 16)
            if whole * P < f1 - f0:
                sp.dma_start(w2[0:f1 - f0 - whole * P, k + whole, :], w["W2"][f0 + whole * P:f1, :]).then_inc(landed, 16)
                count += 16
            for f in range(k, min(k + PIECE, len(CHUNKS0))):
                need[f] = [(loads[0], 16), (landed, count)] if f == k else []
        return need

    experts(nc, "ffn0", x_sb, xnT, combT, CHUNKS0, ACT.Silu, load, n_all, n_loads)


SH1 = 2
CHUNKS1 = [(P, True)] * E + [(P, False)] * SH1


def ffn1(nc, x_sb, xnT, ident, combT, w):
    routing(nc, "route1", xnT, ident, w["wa"].rearrange("(h p) e -> p h e", p=P), combT, False, x_sb, (w["rb2"], w["sb2"]))

    n_loads = 2 + E // 4

    def load(sp, w1, w3, w2, ex, loads, bias):
        b1, b3 = bias
        sp.dma_start(ex[:, :], w["expand1"].bitcast(BF16)).then_inc(loads[0], 16)
        sp.dma_start(b1[:, :], w["gate_bias"]).then_inc(loads[0], 16)
        sp.dma_start(b3[:, :], w["up_bias"]).then_inc(loads[0], 16)
        need = {"bias": (loads[0], 48)}
        for n, (k, m, g, u, dn) in enumerate([(k, 4, w["rg"], w["rw1"], w["rw2"]) for k in range(0, E, 4)]
                                             + [(E, SH1, w["sg"], w["sw1"], w["sw2"])]):
            k0 = k if k < E else 0
            for dst, src in ((w1, g), (w3, u)):
                for h in range(CH):
                    sp.dma_start(dst[:, h, k * P:(k + m) * P].rearrange("p (e f) -> p e f", e=m),
                                 src[k0:k0 + m, h * P:(h + 1) * P, :].rearrange("e p f -> p e f")).then_inc(loads[1 + n], 16)
            sp.dma_start(w2[:, k:k + m, :], dn[k0:k0 + m, :, :].rearrange("e f c -> f e c")).then_inc(loads[1 + n], 16)
            for f in range(k, k + m):
                need[f] = [(loads[0], 48), (loads[1 + n], 80)] if f == k else []
        return need

    experts(nc, "ffn1", x_sb, xnT, combT, CHUNKS1, ACT.Gelu, load, (E + SH1) * P, n_loads, biases=True)


LH, LD, FD = 16, 16, 64
LE = LD + 1
LF = LH * FD
NJ = LF // P
PAIR = 2 * LE
WIN = P
VW = PAIR * (NJ - 1) + WIN
SKM = 2 * P
SPG = P // SQ
NG = B // SPG
DEN_EPS = 1e-8


def linear_attention(nc, x_sb, xnT, ident, ctx_dram, w, k_last, v_last):
    with scope(nc, "la") as osc:
        wq, wk, wv, wo = (osc.sb(n, [P, CH, D]) for n in ("wq", "wk", "wv", "wo"))
        qf = osc.sb("qf", [P, LF // CH])
        kf = osc.sb("kf", [P, LF // CH])
        bq = osc.sb("bq", [P, CH])
        bk = osc.sb("bk", [P, CH])
        bv = osc.sb("bv", [P, D])
        bo = osc.sb("bo", [1, D])
        ones = osc.sb("ones", [1, P])
        maskT = osc.sb("maskT", [P, 2, B])
        w_loaded = osc.sem("w_loaded")

        with scope(nc, "ll") as sc:
            cl = sc.sb("cl", [B, D])
            clT = sc.sb("clT", [P, CH, B])
            mk = sc.sb("mk", [B, SK])
            kT = sc.sb("kT", [P, CH, B])
            kp = sc.sb("kp", [B, LF])
            vb = sc.sb("vb", [B, LH, LD])
            vx = sc.sb("vx", [B, VW])
            pt = sc.pb("pt", [P, BLK])
            pm = sc.pb("pm", [P, BLK])
            pk = [sc.pb(f"pk{i}", [P, BLK]) for i in range(3)]
            pv = sc.pb("pv", [P, BLK])
            cl_loaded = sc.sem("cl_loaded")
            zeroed = sc.sem("zeroed")
            turned = sc.sem("turned")
            turned_out = sc.sem("turned_out")
            k_ready = sc.sem("k_ready")
            k_out = sc.sem("k_out")
            v_ready = sc.sem("v_ready")
            kp_ready = sc.sem("kp_ready")
            kp_out = sc.sem("kp_out")
            step = sc.sem("step")
            vx_ready = sc.sem("vx_ready")
            stored = sc.sem("stored")
            NW = 9
            with nc.Block() as block:
                @block.sync
                def _(sp):
                    sp.dma_start(cl[:, :], ctx_dram[:, SKM, :]).then_inc(cl_loaded, 16)
                    sp.dma_start(mk[:, :], w["mask"]).then_inc(cl_loaded, 16)
                    for dst, src in ((wk, w["Wk"]), (wv, w["Wv"]), (wq, w["Wq"]), (wo, w["Wo"])):
                        sp.dma_start(dst[:, :, :], src.rearrange("(h p) n -> p h n", p=P)).then_inc(w_loaded, 16)
                    sp.dma_start(bk[:, :], w["bkT"]).then_inc(w_loaded, 16)
                    sp.dma_start(bq[:, :], w["bqT"]).then_inc(w_loaded, 16)
                    sp.dma_start(bv[:, :], w["bv"].rearrange("(o n) -> o n", o=1).to_broadcast([P, D])).then_inc(w_loaded, 16)
                    sp.dma_start(bo[:, :], w["bo"].rearrange("(o n) -> o n", o=1)).then_inc(w_loaded, 16)
                    sp.wait_ge(zeroed, 1)
                    for h in range(P // LD):
                        sp.dma_start(kf[h * LD:(h + 1) * LD, h * FD:(h + 1) * FD], w["WkfT"]).then_inc(w_loaded, 16)
                        sp.dma_start(qf[h * LD:(h + 1) * LD, h * FD:(h + 1) * FD], w["WqfT"]).then_inc(w_loaded, 16)
                    sp.wait_ge(kp_out, 2)
                    sp.dma_start(k_last, kp[:, :]).then_inc(stored, 16)
                    sp.wait_ge(vx_ready, 1)
                    sp.dma_start(v_last, vx[:, :]).then_inc(stored, 16)
                    sp.wait_ge(stored, 32)
                    sp.wait_ge(w_loaded, 16 * (8 + 16))

                @block.gpsimd
                def _(pool):
                    pool.memset(ones[:, :], 1.0)
                    pool.memset(vx[:, :], 0.0)
                    pool.memset(kf[:, :], 0.0)
                    pool.memset(qf[:, :], 0.0).then_inc(zeroed, 1)

                @block.tensor
                def _(pe):
                    pe.wait_ge(cl_loaded, 32)
                    for c in range(CH):
                        pe.transpose(pt[:, c * B:(c + 1) * B], cl[:, c * P:(c + 1) * P], ident[0:B, 0:B]).then_inc(turned, 1)
                    for t in range(2):
                        pe.transpose(pm[:, t * B:(t + 1) * B], mk[:, t * P:(t + 1) * P], ident[0:B, 0:B]).then_inc(turned, 1)
                    pe.wait_ge(turned_out, 1)
                    pe.wait_ge(w_loaded, 16 * 24)
                    for h in range(CH):
                        for c in range(CH):
                            mm = pe.matmul(pk[2][:, h * B:(h + 1) * B], wk[:, c, h * P:(h + 1) * P], clT[:, c, :], start=(c == 0), stop=(c == 1))
                    mm.then_inc(k_ready, 1)
                    for c in range(CH):
                        mm = pe.matmul(pv[0:B, 0:D], clT[:, c, :], wv[:, c, :], start=(c == 0), stop=(c == 1))
                    mm.then_inc(v_ready, 1)
                    pe.wait_ge(k_out, 2)
                    for h in range(CH):
                        pe.matmul(pk[h][0:B, :], kT[:, h, :], kf[:, :], start=True, stop=True).then_inc(kp_ready, 1)

                @block.scalar
                def _(act):
                    act.wait_ge(w_loaded, 16 * 24)
                    act.wait_ge(k_ready, 1)
                    for h in range(CH):
                        act.activation(kT[:, h, :], pk[2][:, h * B:(h + 1) * B], ACT.Identity, bias=bk[:, h:h + 1]).then_inc(k_out, 1)
                    for h in range(CH):
                        act.wait_ge(kp_ready, h + 1)
                        act.activation(kp[:, h * BLK:(h + 1) * BLK], pk[h][0:B, :], ACT.Relu).then_inc(kp_out, 1)

                @block.vector
                def _(dve):
                    ch = Chain(dve, step)
                    dve.wait_ge(turned, 4)
                    dve.tensor_copy(clT[:, :, :], pt[:, 0:CH * B].rearrange("p (c n) -> p c n", c=CH)).then_inc(turned_out, 1)
                    dve.tensor_copy(maskT[:, :, :], pm[:, 0:2 * B].rearrange("p (c n) -> p c n", c=2))
                    dve.wait_ge(v_ready, 1)
                    dve.wait_ge(zeroed, 1)
                    dve.wait_ge(w_loaded, 16 * 24)
                    ch.link(dve.tensor_tensor(vb[:, :, :], pv[0:B, 0:D].rearrange("p (h d) -> p h d", h=LH),
                                              bv[0:B, :].rearrange("p (h d) -> p h d", h=LH), ALU.add))
                    v3 = vx[:, 0:LH * LE].rearrange("p (h e) -> p h e", h=LH)
                    dve.tensor_scalar(v3[:, :, 0:LD], vb[:, :, :], mk[:, SKM:SK], None, ALU.mult)
                    dve.tensor_copy(v3[:, :, LD:LE], mk[:, SKM:SK].unsqueeze(1).to_broadcast([B, LH, 1])).then_inc(vx_ready, 1)

        with scope(nc, "lm") as sc:
            cx = [sc.sb(f"cx{i}", [P, 2, D]) for i in range(2)]
            k1 = [sc.sb(f"k1_{i}", [1, LF]) for i in range(2)]
            v1 = [sc.sb(f"v1_{i}", [1, VW]) for i in range(2)]
            cxT = sc.sb("cxT", [P, CH, SKM])
            kT = sc.sb("kT", [P, CH, SKM])
            kp = sc.sb("kp", [P, 2, LF])
            vb = sc.sb("vb", [P, 2, D])
            vx = [sc.sb(f"vx{i}", [P, 2, VW]) for i in range(2)]
            kvd = sc.sb("kvd", [P, NJ, SPG, PAIR])
            qT = sc.sb("qT", [P, CH, P])
            qp = sc.sb("qp", [P, NJ, P])
            raw = sc.sb("raw", [P, NJ, PAIR])
            den = sc.sb("den", [P, LH])
            rden = sc.sb("rden", [P, LH])
            at = sc.sb("at", [P, LH, LD])
            atT = sc.sb("atT", [P, CH, P])
            T0 = sc.pb("T0", [P, BLK])
            KT = sc.pb("KT", [P, BLK])
            VP = sc.pb("VP", [P, BLK])
            KP = [sc.pb(f"KP{i}", [P, BLK]) for i in range(2)]
            KV = sc.pb("KV", [P, NJ, P])
            G = sc.pb("G", [P, BLK])
            zeroed = sc.sem("zeroed")
            cx_loaded = [sc.sem(f"cx_loaded{i}") for i in range(2)]
            last_loaded = [sc.sem(f"last_loaded{i}") for i in range(2)]
            cxT_ready = sc.sem("cxT_ready")
            cxT_out = sc.sem("cxT_out")
            kt_ready = sc.sem("kt_ready")
            kt_out = sc.sem("kt_out")
            v_ready = sc.sem("v_ready")
            vb_out = sc.sem("vb_out")
            vx_ready = sc.sem("vx_ready")
            kp_ready = sc.sem("kp_ready")
            kp_out = sc.sem("kp_out")
            kv_ready = sc.sem("kv_ready")
            kv_out = sc.sem("kv_out")
            q_ready = sc.sem("q_ready")
            q_out = sc.sem("q_out")
            qp_ready = sc.sem("qp_ready")
            qp_out = sc.sem("qp_out")
            o_ready = sc.sem("o_ready")
            raw_out = sc.sem("raw_out")
            step = sc.sem("step")
            at_ready = sc.sem("at_ready")
            at_turned = sc.sem("at_turned")
            atT_out = sc.sem("atT_out")
            wo_ready = sc.sem("wo_ready")
            wo_added = sc.sem("wo_added")
            JB = BLK // (SPG * PAIR)
            OB = [KP[0], KP[1], G]

            def groups(eng, group):
                with eng.Fori(0, NG - 1) as g:
                    group(g, True)
                group(NG - 1, False)

            with nc.Block() as block:
                @block.sync
                def _(sp):
                    with sp.Fori(0, B // 2) as i:
                        for k in range(2):
                            n = i * 2 + k
                            sp.wait_ge(cxT_ready, n + 1)
                            sp.dma_start(cx[k][:, :, :], ctx_dram[bass.ds(n, 1), 0:SKM, :].rearrange("o (t p) c -> p (o t) c", p=P)
                                         ).then_inc(cx_loaded[k], 16)
                            sp.wait_ge(kv_ready, n + 1)
                            sp.dma_start(k1[k][:, :], k_last[bass.ds(n, 1), :]).then_inc(last_loaded[k], 16)
                            sp.dma_start(v1[k][:, :], v_last[bass.ds(n, 1), :]).then_inc(last_loaded[k], 16)

                @block.gpsimd
                def _(pool):
                    pool.memset(kvd[:, :, :, :], 0.0).then_inc(zeroed, 1)
                    for i in range(2):
                        pool.memset(vx[i][:, :, :], 0.0).then_inc(zeroed, 1)

                @block.tensor
                def _(pe):
                    def context(n, k, use):
                        pe.wait_ge(cx_loaded[k], use * 16)
                        for t in range(2):
                            for c in range(CH):
                                mm = pe.transpose(T0[:, (c * 2 + t) * P:(c * 2 + t + 1) * P], cx[k][:, t, c * P:(c + 1) * P], ident[:, :])
                        mm.then_inc(cxT_ready, 1)

                    def key_value(n):
                        pe.wait_ge(cxT_out, n + 1)
                        for h in range(CH):
                            for c in range(CH):
                                mm = pe.matmul(KT[:, h * SKM:(h + 1) * SKM], wk[:, c, h * P:(h + 1) * P], cxT[:, c, :], start=(c == 0), stop=(c == 1))
                        mm.then_inc(kt_ready, 1)
                        for t in range(2):
                            for c in range(CH):
                                mm = pe.matmul(VP[:, t * D:(t + 1) * D], cxT[:, c, t * P:(t + 1) * P], wv[:, c, :], start=(c == 0), stop=(c == 1))
                        mm.then_inc(v_ready, 1)

                    def features(n):
                        pe.wait_ge(kt_out, n * 2 + 2)
                        for t in range(2):
                            for h in range(CH):
                                if t:
                                    pe.wait_ge(kp_out, n * 4 + h + 1)
                                pe.matmul(KP[h][:, :], kT[:, h, t * P:(t + 1) * P], kf[:, :], start=True, stop=True).then_inc(kp_ready, 1)

                    def key_times_value(n, k, use):
                        pe.wait_ge(kp_out, n * 4 + 4)
                        pe.wait_ge(vx_ready, n * 4 + 4)
                        pe.wait_ge(last_loaded[k], use * 32)
                        pe.wait_ge(kv_out, n + 1)
                        for j in range(NJ):
                            o = slice(j * P, (j + 1) * P)
                            win = slice(j * PAIR, j * PAIR + WIN)
                            for t in range(2):
                                pe.matmul(KV[:, j, :], kp[:, t, o], vx[k][:, t, win], start=(t == 0), stop=False)
                            mm = pe.matmul(KV[:, j, :], k1[k][:, o], v1[k][:, win], start=False, stop=True)
                        mm.then_inc(kv_ready, 1)

                    def queries(g):
                        pe.wait_ge(wo_added, g + 1)
                        for h in range(CH):
                            for c in range(CH):
                                mm = pe.matmul(G[:, h * P:(h + 1) * P], wq[:, c, h * P:(h + 1) * P], xnT[:, c, bass.ds(g * P, P)], start=(c == 0), stop=(c == 1))
                        mm.then_inc(q_ready, 1)
                        pe.wait_ge(q_out, g * 2 + 2)
                        for j in range(NJ):
                            mm = pe.matmul(KP[j // 4][:, (j % 4) * P:(j % 4 + 1) * P], qf[:, (j % 4) * P:(j % 4 + 1) * P], qT[:, j // 4, :], start=True, stop=True)
                            if j % 4 == 3:
                                mm.then_inc(qp_ready, 1)
                        pe.wait_ge(qp_out, g * 2 + 2)

                    def outputs(g, n):
                        pe.wait_ge(kv_out, n + 2)
                        pe.wait_ge(qp_out, g * 2 + 2)
                        for j in range(NJ):
                            mm = pe.matmul(OB[j // JB][:, (j % JB) * SPG * PAIR:(j % JB + 1) * SPG * PAIR], qp[:, j, :],
                                           kvd[:, j, :, :], start=True, stop=True)
                        mm.then_inc(o_ready, 1)

                    def project(g):
                        pe.wait_ge(at_ready, g + 1)
                        for c in range(CH):
                            mm = pe.transpose(T0[:, c * P:(c + 1) * P], at[:, c * 8:(c + 1) * 8, :], ident[:, :])
                        mm.then_inc(at_turned, 1)
                        pe.wait_ge(atT_out, g + 1)
                        for c in range(CH):
                            pe.matmul(G[:, 0:D], atT[:, c, :], wo[:, c, :], start=(c == 0), stop=False)
                        pe.matmul(G[:, 0:D], ones[:, :], bo[:, :], start=False, stop=True).then_inc(wo_ready, 1)

                    pe.sem_inc(cxT_ready, 2)
                    pe.sem_inc(kv_ready, 2)
                    context(0, 0, 1)
                    key_value(0)
                    features(0)

                    def group(g, more):
                        for i in range(SPG):
                            n = g * SPG + i
                            nxt = more or i < SPG - 1
                            k = (i + 1) % 2
                            if nxt:
                                context(n + 1, k, g * 2 + (i + 1) // 2 + 1)
                            key_times_value(n, i % 2, g * 2 + i // 2 + 1)
                            if i == 0:
                                queries(g)
                            if nxt:
                                pe.wait_ge(vb_out, n + 1)
                                key_value(n + 1)
                            if i == SPG - 1:
                                outputs(g, n)
                                pe.wait_ge(raw_out, g + 1)
                            if nxt:
                                features(n + 1)
                            if i == SPG - 1:
                                project(g)

                    groups(pe, group)

                @block.scalar
                def _(act):
                    def context(n):
                        act.wait_ge(cxT_ready, n + 3)
                        act.activation(cxT[:, :, :], T0[:, :].rearrange("p (c t) -> p c t", c=CH), ACT.Copy).then_inc(cxT_out, 1)

                    def keys(n):
                        act.wait_ge(kt_ready, n + 1)
                        for h in range(CH):
                            act.activation(kT[:, h, :], KT[:, h * SKM:(h + 1) * SKM], ACT.Identity, bias=bk[:, h:h + 1]).then_inc(kt_out, 1)

                    def features(n):
                        for t in range(2):
                            for h in range(CH):
                                act.wait_ge(kp_ready, n * 4 + t * 2 + h + 1)
                                act.activation(kp[:, t, h * BLK:(h + 1) * BLK], KP[h][:, :], ACT.Relu).then_inc(kp_out, 1)

                    def queries(g):
                        act.wait_ge(q_ready, g + 1)
                        for h in range(CH):
                            act.activation(qT[:, h, :], G[:, h * P:(h + 1) * P], ACT.Identity, bias=bq[:, h:h + 1]).then_inc(q_out, 1)
                        for h in range(CH):
                            act.wait_ge(qp_ready, g * 2 + h + 1)
                            act.activation(qp[:, 4 * h:4 * h + 4, :], KP[h][:, :].rearrange("p (j t) -> p j t", j=4), ACT.Relu).then_inc(qp_out, 1)

                    context(0)
                    keys(0)
                    features(0)

                    def group(g, more):
                        for i in range(SPG):
                            n = g * SPG + i
                            nxt = more or i < SPG - 1
                            if nxt:
                                context(n + 1)
                            if i == 0:
                                queries(g)
                            if nxt:
                                keys(n + 1)
                                features(n + 1)
                        act.wait_ge(at_turned, g + 1)
                        act.activation(atT[:, :, :], T0[:, 0:D].rearrange("p (c t) -> p c t", c=CH), ACT.Copy).then_inc(atT_out, 1)

                    groups(act, group)

                @block.vector
                def _(dve):
                    def values(n, k):
                        dve.wait_ge(v_ready, n + 1)
                        dve.tensor_tensor(vb[:, :, :], VP[:, :].rearrange("p (t c) -> p t c", t=2), bv[:, :].unsqueeze(1).to_broadcast([P, 2, D]),
                                          ALU.add).then_inc(vb_out, 1)
                        dve.wait_ge(vb_out, n + 1)
                        for t in range(2):
                            m = maskT[:, t, bass.ds(n, 1)]
                            v3 = vx[k][:, t, 0:LH * LE].rearrange("p (h e) -> p h e", h=LH)
                            dve.tensor_scalar(v3[:, :, 0:LD], vb[:, t, :].rearrange("p (h d) -> p h d", h=LH), m, None, ALU.mult).then_inc(vx_ready, 1)
                            dve.tensor_copy(v3[:, :, LD:LE], m.unsqueeze(1).to_broadcast([P, LH, 1])).then_inc(vx_ready, 1)

                    dve.sem_inc(kv_out, 1)
                    dve.sem_inc(wo_added, 1)
                    dve.wait_ge(zeroed, 3)
                    values(0, 0)

                    def group(g, more):
                        ch = Chain(dve, step, g * 2)
                        for i in range(SPG):
                            n = g * SPG + i
                            nxt = more or i < SPG - 1
                            dve.wait_ge(kv_ready, n + 3)
                            for h in range(2):
                                o = slice(h * FD, (h + 1) * FD)
                                e = slice(h * LE, (h + 1) * LE)
                                ins = dve.tensor_copy(kvd[o, :, i, e], KV[o, :, e])
                            ins.then_inc(kv_out, 1)
                            if nxt:
                                values(n + 1, (i + 1) % 2)
                        dve.wait_ge(o_ready, g + 1)
                        for s in range(SPG):
                            o = slice(s * SQ, (s + 1) * SQ)
                            for j in range(0, NJ, JB):
                                m = min(JB, NJ - j)
                                src = OB[j // JB][o, 0:m * SPG * PAIR].rearrange("p (j s e) -> p j s e", j=m, s=SPG)[:, :, s, :]
                                ins = dve.tensor_copy(raw[o, j:j + m, :], src)
                        ins.then_inc(raw_out, 1)
                        dve.wait_ge(raw_out, g + 1)
                        r3 = raw[:, :, :].rearrange("p j (h e) -> p (j h) e", h=2)
                        ch.link(dve.tensor_scalar(den[:, :], r3[:, :, LD], DEN_EPS, None, ALU.add))
                        ch.link(dve.reciprocal(rden[:, :], den[:, :]))
                        dve.tensor_tensor(at[:, :, :], r3[:, :, 0:LD], rden[:, :].unsqueeze(2).to_broadcast([P, LH, LD]), ALU.mult).then_inc(at_ready, 1)
                        dve.wait_ge(wo_ready, g + 1)
                        xt = x_sb[:, bass.ds(g, 1), :].rearrange("p o c -> p (o c)")
                        dve.tensor_tensor(xt, xt, G[:, 0:D], ALU.add).then_inc(wo_added, 1)

                    groups(dve, group)


AH, AD = 16, 16
HPH = AH // CH
PAIRS = P // 32


def self_attention(nc, x_sb, xnT, ident, w, scratch):
    with scope(nc, "sa") as osc:
        turnedT = osc.sb("turnedT", [P, CH, TOK])
        wp = osc.sb("wp", [P, CH, D])
        bp = osc.sb("bp", [1, D])
        ones = osc.sb("ones", [1, P])
        stored = [osc.sem(f"stored{i}") for i in range(2)]
        gathered = osc.sem("gathered")
        wp_loaded = osc.sem("wp_loaded")
        with scope(nc, "sa1") as sc:
            wq = sc.sb("wq", [P, CH, D])
            wk = sc.sb("wk", [P, CH, D])
            wv = sc.sb("wv", [P, CH, D])
            xb = sc.sb("xb", [P, CH, BLK])
            par = sc.sb("par", [P, 2])
            qT = sc.sb("qT", [P, CH, BLK])
            kT = sc.sb("kT", [P, 2, CH, BLK])
            WIDE = HPH * (P + AD)
            vx = sc.sb("vx", [P, TPB, CH, WIDE])
            s = sc.sb("s", [P, 2, AH, SQ])
            e = sc.sb("e", [P, 2, AH, SQ])
            pT = sc.sb("pT", [P, AH, SQ])
            pbd = sc.sb("pbd", [P, 2, AH, P])
            mx = sc.sb("mx", [P, 2, AH])
            sm = sc.sb("sm", [P, 2, AH])
            oT = sc.sb("oT", [P, 2, CH, P])
            S = sc.pb("S", [P, PAIRS, CH * 2, P])
            aux = [sc.pb(f"aux{i}", [P, BLK]) for i in range(4)]
            loaded = sc.sem("loaded")
            par_step = sc.sem("par_step")
            zeroed = sc.sem("zeroed")
            xb_ready = sc.sem("xb_ready")
            qk_ready = sc.sem("qk_ready")
            q_out = sc.sem("q_out")
            k_out = sc.sem("k_out")
            v_ready = sc.sem("v_ready")
            v_out = sc.sem("v_out")
            s_ready = sc.sem("s_ready")
            s_out_a = sc.sem("s_out_a")
            s_out_v = sc.sem("s_out_v")
            max_done = sc.sem("max_done")
            sub_done = sc.sem("sub_done")
            exp_done = sc.sem("exp_done")
            soft_step = sc.sem("soft_step")
            pT_ready = sc.sem("pT_ready")
            pbd_ready = sc.sem("pbd_ready")
            pT_free = sc.sem("pT_free")
            o_ready = sc.sem("o_ready")
            oT_ready = sc.sem("oT_ready")
            store_free = sc.sem("store_free")

            def spread(t, h):
                return vx[:, t, h, :].rearrange("p (n c) -> p n c", c=P + AD)[:, :, 0:AD]

            with nc.Block() as block:
                @block.sync
                def _(sp):
                    for dst, src in ((wq, w["Wq"]), (wk, w["Wk"]), (wv, w["Wv"])):
                        sp.dma_start(dst[:, :, :], src.rearrange("(h p) n -> p h n", p=P)).then_inc(loaded, 16)
                    sp.dma_start(wp[:, :, :], w["Wproj"].rearrange("(h p) n -> p h n", p=P)).then_inc(wp_loaded, 16)
                    sp.dma_start(bp[:, :], w["bproj"].rearrange("(o n) -> o n", o=1)).then_inc(wp_loaded, 16)
                    sp.sem_inc(store_free, 2)
                    out = scratch.rearrange("t b (h n) d s -> t h (n d) b s", h=CH)
                    back = scratch.rearrange("t b n d s -> t d (b n) s")
                    with sp.Fori(0, NT // 8) as i:
                        for k in range(8):
                            t = i * 8 + k
                            sp.wait_ge(oT_ready, t + 3)
                            for h in range(CH):
                                sp.dma_start(out[bass.ds(t, 1), h, :, :, :].rearrange("o p b s -> (o p) b s"),
                                             oT[:, k % 2, h, :].rearrange("p (b s) -> p b s", s=SQ)).then_inc(stored[k % 2], 16)
                            sp.wait_ge(stored[k % 2], (i * 4 + k // 2) * 32 + 32)
                            sp.sem_inc(store_free, 1)
                            sp.dma_start(turnedT[k * AD:(k + 1) * AD, bass.ds(i, 1), :].rearrange("p o (n s) -> p (o n) s", s=SQ),
                                         back[bass.ds(t, 1), :, :, :].rearrange("o d n s -> (o d) n s")).then_inc(gathered, 16)
                    sp.wait_ge(gathered, 16 * NT)

                @block.gpsimd
                def _(pool):
                    ch = Chain(pool, par_step)
                    pool.memset(ones[:, :], 1.0)
                    pf = pbd[:, 0, 0:PAIRS * 2, 0:1]
                    ch.link(pool.memset(pf, 1.0))
                    ch.link(pool.affine_select(out=pf, in_=pf, compare_op=ALU.is_ge, fill=0.0, base=0,
                                               pattern=[[-16, PAIRS * 2], [0, 1]], channel_multiplier=1))
                    ch.link(pool.affine_select(out=pf, in_=pf, compare_op=ALU.is_ge, fill=0.0, base=15,
                                               pattern=[[16, PAIRS * 2], [0, 1]], channel_multiplier=-1))
                    ch.link(pool.tensor_tensor(par[:, 0:1], pbd[:, 0, 0, 0:1], pbd[:, 0, 2, 0:1], ALU.add))
                    ch.link(pool.tensor_tensor(par[:, 0:1], par[:, 0:1], pbd[:, 0, 4, 0:1], ALU.add))
                    ch.link(pool.tensor_tensor(par[:, 0:1], par[:, 0:1], pbd[:, 0, 6, 0:1], ALU.add))
                    ch.link(pool.tensor_scalar(par[:, 1:2], par[:, 0:1], -1.0, 1.0, ALU.mult, ALU.add))
                    pool.memset(pbd[:, :, :, :], 0.0).then_inc(zeroed, 1)
                    pool.memset(vx[:, :, :, :], 0.0).then_inc(zeroed, 1)

                @block.tensor
                def _(pe):
                    pe.sem_inc(o_ready, 2)
                    pe.wait_ge(loaded, 48)
                    with pe.Fori(0, NBLK) as b:
                        pe.wait_ge(xb_ready, b + 1)
                        pe.wait_ge(oT_ready, b * TPB + 2)
                        for i, wt in enumerate((wq, wk)):
                            for h in range(CH):
                                for c in range(CH):
                                    mm = pe.matmul(aux[2 * i + h][:, :], wt[:, c, h * P:(h + 1) * P], xb[:, c, :],
                                                   start=(c == 0), stop=(c == CH - 1))
                                mm.then_inc(qk_ready, 1)
                        for i in range(2):
                            pe.wait_ge(q_out, b * 2 + i + 1)
                            for j in range(2):
                                for c in range(CH):
                                    mm = pe.matmul(aux[i][:, j * D:(j + 1) * D], xb[:, c, (2 * i + j) * P:(2 * i + j + 1) * P],
                                                   wv[:, c, :], start=(c == 0), stop=(c == CH - 1))
                            mm.then_inc(v_ready, 1)
                        pe.wait_ge(q_out, b * 2 + 2)
                        pe.wait_ge(k_out, b * 4 + 4)
                        for j in range(TPB + 1):
                            if j < TPB:
                                n = b * TPB + j
                                pe.wait_ge(s_out_a, n + 1)
                                pe.wait_ge(s_out_v, n + 1)
                                for h in range(CH):
                                    for o in range(2):
                                        for i in range(PAIRS):
                                            r = slice(32 * i, 32 * i + 32)
                                            mm = pe.matmul(S[:, i, 2 * h + o, :], qT[r, h, j * P:(j + 1) * P],
                                                           kT[r, o, h, j * P:(j + 1) * P], start=True, stop=True)
                                            if h == 1 and o == 1:
                                                mm.then_inc(s_ready, 1)
                            if j >= 1:
                                n = b * TPB + j - 1
                                pe.wait_ge(pbd_ready, n * 4 + 4)
                                pe.wait_ge(v_out, b * 2 + 3)
                                pe.wait_ge(oT_ready, n + 1)
                                for h in range(CH):
                                    for m in range(HPH):
                                        at = (m // 2) * 4 + 2 * h + m % 2
                                        mm = pe.matmul(aux[2 + (j - 1) % 2][:, h * P:(h + 1) * P],
                                                       vx[:, j - 1, h, m * P:(m + 1) * P], pbd[:, (j - 1) % 2, at, :],
                                                       start=(m == 0), stop=(m == HPH - 1))
                                mm.then_inc(o_ready, 1)

                @block.scalar
                def _(act):
                    act.sem_inc(s_out_a, 1)
                    act.sem_inc(oT_ready, 2)
                    act.sem_inc(v_out, 1)
                    act.sem_inc(pT_free, 1)
                    act.wait_ge(zeroed, 2)
                    with act.Fori(0, NBLK) as b:
                        act.wait_ge(v_out, b * 2 + 1)
                        act.activation(xb[:, :, :], xnT[:, :, bass.ds(b * BLK, BLK)], ACT.Copy).then_inc(xb_ready, 1)
                        for h in range(CH):
                            act.wait_ge(qk_ready, b * 4 + h + 1)
                            act.activation(qT[:, h, :], aux[h][:, :], ACT.Copy).then_inc(q_out, 1)
                        for i in range(2):
                            act.wait_ge(v_ready, b * 2 + i + 1)
                            for j in range(2):
                                for h in range(CH):
                                    ins = act.activation(spread(2 * i + j, h), aux[i][:, j * D + h * P:j * D + (h + 1) * P]
                                                         .rearrange("p (n c) -> p n c", c=AD), ACT.Copy)
                            ins.then_inc(v_out, 1)
                        for j in range(TPB + 1):
                            if j < TPB:
                                n = b * TPB + j
                                act.wait_ge(s_ready, n * PAIRS + PAIRS)
                                for q in range(2):
                                    o = slice(32 * q, 32 * q + 32)
                                    ins = act.activation(s[o, j % 2, :, :], S[o, :, :, 32 * q:32 * q + 32].rearrange("p i m k -> p (i m) k"), ACT.Copy)
                                ins.then_inc(s_out_a, 1)
                                act.wait_ge(sub_done, n + 1)
                                act.activation(e[:, j % 2, :, :], s[:, j % 2, :, :], ACT.Exp, scale=AD ** -0.5).then_inc(exp_done, 1)
                            if j >= 1:
                                n = b * TPB + j - 1
                                act.wait_ge(pT_ready, n + 1)
                                act.wait_ge(o_ready, n + 1)
                                for q in range(4):
                                    o = slice(32 * q, 32 * q + 32)
                                    act.activation(pbd[o, (j - 1) % 2, :, 32 * q:32 * q + 32], pT[o, :, :], ACT.Copy).then_inc(pbd_ready, 1)
                                act.wait_ge(pbd_ready, n * 4 + 4)
                                act.sem_inc(pT_free, 1)
                                act.wait_ge(o_ready, n + 3)
                                act.wait_ge(store_free, n + 1)
                                act.activation(oT[:, (j - 1) % 2, :, :], aux[2 + (j - 1) % 2][:, 0:D].rearrange("p (h n) -> p h n", h=CH),
                                               ACT.Copy).then_inc(oT_ready, 1)

                @block.vector
                def _(dve):
                    dve.sem_inc(s_out_v, 1)
                    dve.wait_ge(zeroed, 1)
                    PER = TPB * 3
                    with dve.Fori(0, NBLK) as b:
                        ch = Chain(dve, soft_step, b * PER)
                        for h in range(CH):
                            dve.wait_ge(qk_ready, b * 4 + h + 3)
                            for o in range(2):
                                dve.tensor_scalar(kT[:, o, h, :], aux[2 + h][:, :], par[:, o:o + 1], None, ALU.mult).then_inc(k_out, 1)
                        for j in range(TPB + 1):
                            if j < TPB:
                                n = b * TPB + j
                                k = j % 2
                                dve.wait_ge(s_ready, n * PAIRS + PAIRS)
                                for q in range(2, 4):
                                    o = slice(32 * q, 32 * q + 32)
                                    ins = dve.tensor_copy(s[o, k, :, :], S[o, :, :, 32 * q:32 * q + 32].rearrange("p i m k -> p (i m) k"))
                                ins.then_inc(s_out_v, 1)
                                dve.wait_ge(s_out_v, n + 2)
                                dve.wait_ge(s_out_a, n + 2)
                                dve.tensor_reduce(mx[:, k, :], s[:, k, :, :], AX.X, ALU.max).then_inc(max_done, 1)
                                dve.wait_ge(max_done, n + 1)
                                dve.tensor_tensor(s[:, k, :, :], s[:, k, :, :], mx[:, k, :].unsqueeze(2).to_broadcast([P, AH, SQ]),
                                                  ALU.subtract).then_inc(sub_done, 1)
                            if j >= 1:
                                n = b * TPB + j - 1
                                k = (j - 1) % 2
                                dve.wait_ge(exp_done, n + 1)
                                ch.link(dve.tensor_reduce(sm[:, k, :], e[:, k, :, :], AX.X, ALU.add))
                                ch.link(dve.reciprocal(sm[:, k, :], sm[:, k, :]))
                                ch.link(dve.tensor_tensor(e[:, k, :, :], e[:, k, :, :], sm[:, k, :].unsqueeze(2).to_broadcast([P, AH, SQ]), ALU.mult))
                                dve.wait_ge(pT_free, n + 1)
                                dve.transpose(pT[:, :, :], e[:, k, :, :]).then_inc(pT_ready, 1)
                        assert ch.n == PER

        with scope(nc, "sa2") as sc:
            po = [sc.pb(f"po{i}", [P, 2, D]) for i in range(4)]
            o_ready = sc.sem("o_ready")
            o_added = sc.sem("o_added")
            with nc.Block() as block:
                @block.tensor
                def _(pe):
                    pe.wait_ge(gathered, 16 * NT)
                    pe.wait_ge(wp_loaded, 32)
                    for t in range(NT):
                        if t % 2 == 0 and t >= 8:
                            pe.wait_ge(o_added, t // 2 - 3)
                        dst = po[(t // 2) % 4][:, t % 2, :]
                        for c in range(CH):
                            pe.matmul(dst, turnedT[:, c, t * P:(t + 1) * P], wp[:, c, :], start=(c == 0), stop=False)
                        mm = pe.matmul(dst, ones[:, :], bp[:, :], start=False, stop=True)
                        if t % 2:
                            mm.then_inc(o_ready, 1)

                @block.vector
                def _(dve):
                    for i in range(NT // 2):
                        dve.wait_ge(o_ready, i + 1)
                        xt = x_sb[:, 2 * i:2 * i + 2, :]
                        dve.tensor_tensor(xt, xt, po[i % 4][:, :, :], ALU.add).then_inc(o_added, 1)


def program(nc, t, out):
    def stage(prefix):
        return {k[len(prefix):]: v for k, v in t.items() if k.startswith(prefix)}

    xa_v_last = nc.dram_tensor("dram_xa_v_last", [B, NKV, KVW], F32, kind="Internal").ap()
    la_k_last = nc.dram_tensor("dram_la_k_last", [B, LF], F32, kind="Internal").ap()
    la_v_last = nc.dram_tensor("dram_la_v_last", [B, VW], F32, kind="Internal").ap()
    sa_turn = nc.dram_tensor("dram_sa_turn", [NT, SPG, AH, AD, SQ], F32, kind="Internal").ap()
    with ExitStack() as ctx:
        sc = Scope(nc, ctx, "main")
        x_sb = sc.sb("x", [P, NT, D])
        xnT = sc.sb("xnT", [P, CH, TOK])
        x_loaded = sc.sem("x_loaded")
        x_stored = sc.sem("x_stored")
        with nc.Block() as block:
            @block.sync
            def _(sp):
                sp.dma_start(x_sb[:, :, :], t["x"].rearrange("(t p) c -> p t c", p=P)).then_inc(x_loaded, 16)
                sp.wait_ge(x_loaded, 16)
        ident, neg_half = constants(nc, sc)
        layernorm(nc, "ln0", x_sb, xnT, ident, neg_half)
        cross_attention(nc, x_sb, xnT, ident, neg_half, t["ctx"], stage("xa_"), xa_v_last)
        layernorm(nc, "ln1", x_sb, xnT, ident, neg_half)
        rwkv(nc, x_sb, xnT, ident, stage("tm_"))
        layernorm(nc, "ln2", x_sb, xnT, ident, neg_half)
        with ExitStack() as inner:
            combT = Scope(nc, inner, "f0").sb("combT", [3 * E, TOK], BF16)
            ffn0(nc, x_sb, xnT, ident, combT, stage("f0_"))
        layernorm(nc, "ln3", x_sb, xnT, ident, neg_half)
        linear_attention(nc, x_sb, xnT, ident, t["ctx"], stage("la_"), la_k_last, la_v_last)
        layernorm(nc, "ln4", x_sb, xnT, ident, neg_half)
        self_attention(nc, x_sb, xnT, ident, stage("sa_"), sa_turn)
        layernorm(nc, "ln5", x_sb, xnT, ident, neg_half, add_to_x=True)
        with ExitStack() as inner:
            combT = Scope(nc, inner, "f1").sb("combT", [3 * E, TOK], BF16)
            ffn1(nc, x_sb, xnT, ident, combT, stage("f1_"))
        with nc.Block() as block:
            @block.sync
            def _(sp):
                sp.dma_start(out.rearrange("(t p) c -> p t c", p=P), x_sb[:, :, :]).then_inc(x_stored, 16)
                sp.wait_ge(x_stored, 16)


def expand(n):
    import numpy as np
    one = np.arange(E * n)[None] // n == np.arange(E)[:, None]
    return np.where(np.tile(one, (3, 1)), 0x3F80, 0).astype(np.uint16)


def layout(i):
    import numpy as np
    qkv = i["L1_attn_Wqkv"].reshape(AH, 3, AD, D)
    t = {"x": i["x"].reshape(TOK, D), "ctx": i["ctx_2048"]}
    for k in ("Wq", "bq", "Wk", "bk", "Wv", "Wo", "qn_w", "kn_w"):
        t["xa_" + k] = i["L0_xattn_" + k]
    t["xa_mask"] = i["mask_1xSxS2_ff0"]
    t["xa_bvT"] = i["L0_xattn_bv"].reshape(NKV, HD).T
    t["tm_prm"] = np.stack([i["L0_attn_" + k].reshape(-1) for k in PARAMS], axis=1)
    for k in ("W_r", "W_k", "W_v", "W_o", "w1", "w2", "a1", "a2", "g1", "g2"):
        t["tm_" + k] = i["L0_attn_" + k]
    t["f0_Wg"] = i["L0_ffn_Wg"].T
    for k in ("1", "3"):
        t["f0_W" + k] = np.concatenate([i["L0_ffn_W" + k].reshape(-1, D), i["L0_ffn_Ws" + k]]).T
    t["f0_W2"] = np.concatenate([i["L0_ffn_W2"].transpose(0, 2, 1).reshape(-1, D), i["L0_ffn_Ws2"].T])
    t["f0_expand"] = expand(HID0)
    for k in ("Wq", "Wk", "Wv", "Wo"):
        t["la_" + k] = i["L1_xattn_" + k].T
    for k in ("bq", "bk"):
        t[f"la_{k}T"] = i["L1_xattn_" + k].reshape(CH, P).T
    for k in ("bv", "bo"):
        t["la_" + k] = i["L1_xattn_" + k]
    for k in ("Wqf", "Wkf"):
        t[f"la_{k}T"] = i["L1_xattn_" + k].T
    t["la_mask"] = i["mask_BxS2_ff1"]
    for n, k in enumerate(("Wq", "Wk", "Wv")):
        t["sa_" + k] = qkv[:, n].reshape(D, D).T
    t["sa_Wproj"] = i["L1_attn_Wproj"].T
    t["sa_bproj"] = i["L1_attn_bproj"]
    for k in ("wa", "rg", "rw1", "rw2", "rb2", "sg", "sw1", "sw2", "sb2"):
        t["f1_" + k] = i["L1_ffn_" + k]
    t["f1_gate_bias"] = np.concatenate([i["L1_ffn_rgb"], i["L1_ffn_sgb"]]).T
    t["f1_up_bias"] = np.concatenate([i["L1_ffn_rb1"], i["L1_ffn_sb1"]]).T
    t["f1_expand1"] = expand(P)
    return {k: np.ascontiguousarray(v) for k, v in t.items()}


def kernel(**inputs):
    import concourse.bacc as bacc
    import numpy as np
    from concourse.bass_utils import run_bass_kernel_spmd

    arrays = layout({k: np.asarray(v) for k, v in inputs.items()})
    nc = bacc.Bacc("TRN2", target_bir_lowering=False, num_devices=1)
    t = {k: nc.dram_tensor("in_" + k, v.shape, mybir.dt.from_np(v.dtype), kind="ExternalInput").ap() for k, v in arrays.items()}
    out = nc.dram_tensor("out", (TOK, D), F32, kind="ExternalOutput").ap()
    program(nc, t, out)
    r = run_bass_kernel_spmd(nc, [{"in_" + k: v for k, v in arrays.items()}], core_ids=[0])
    return r.results[0]["out"].reshape(B, SQ, D)
```

```python
import math
from contextlib import ExitStack, contextmanager

import concourse.bass as bass
from concourse import mybir
from concourse.alu_op_type import AluOpType as ALU

F32 = mybir.dt.float32
F32R = mybir.dt.float32r
ACT = mybir.ActivationFunctionType
AX = mybir.AxisListType

P = 128
D = 256
CH = D // P
B = 64
SQ = 32
SK = 257
TOK = B * SQ
NT = TOK // P
BLK = 512
NBLK = TOK // BLK
TPB = BLK // P
LN_EPS = 1e-5


class Chain:

    def __init__(self, eng, sem, base=0):
        self.eng, self.sem, self.base, self.n = eng, sem, base, 0

    def link(self, ins):
        self.n += 1
        ins.then_inc(self.sem, 1)
        self.eng.wait_ge(self.sem, self.base + self.n)


class Scope:

    def __init__(self, nc, ctx, tag):
        self.nc, self.ctx, self.tag, self.sems = nc, ctx, tag, []

    def sb(self, name, shape, dt=F32):
        return self.ctx.enter_context(self.nc.sbuf_tensor(f"{self.tag}_{name}", shape, dt))

    def pb(self, name, shape, dt=F32):
        return self.ctx.enter_context(self.nc.psum_tensor(f"{self.tag}_{name}", shape, dt))

    def sem(self, name):
        s = self.ctx.enter_context(self.nc.semaphore(f"{self.tag}_{name}"))
        self.sems.append(s)
        return s

    def clear(self):
        nums = sorted(s.num for s in self.sems)
        with self.nc.Block() as block:
            @block.gpsimd
            def _(pool):
                first = 0
                for i in range(1, len(nums) + 1):
                    if i == len(nums) or nums[i] != nums[i - 1] + 1:
                        pool.sem_clear(range(nums[first], nums[i - 1] + 1))
                        first = i


@contextmanager
def scope(nc, tag):
    with ExitStack() as ctx:
        sc = Scope(nc, ctx, tag)
        yield sc
        sc.clear()


def constants(nc, sc):
    ident = sc.sb("ident", [P, P])
    neg_half = sc.sb("neg_half", [P, 16])
    zeroed = sc.sem("zeroed")
    with nc.Block() as block:
        @block.gpsimd
        def _(pool):
            pool.memset(neg_half[:, :], -0.5)
            pool.memset(ident[:, :], 0.0).then_inc(zeroed, 1)
            pool.wait_ge(zeroed, 1)
            pool.affine_select(out=ident[:, :], in_=ident[:, :], compare_op=ALU.not_equal, fill=1.0,
                               base=0, pattern=[[-1, P]], channel_multiplier=1)
    return ident, neg_half


def layernorm(nc, tag, x_sb, xnT, ident, neg_half, add_to_x=False):
    HALF = NT // 2
    with scope(nc, tag) as sc:
        stats = sc.sb("stats", [P, NT, 6])
        mv = sc.sb("mv", [P, NT, 2])
        veps = sc.sb("veps", [P, NT])
        rstd = sc.sb("rstd", [P, NT])
        xn = sc.sb("xn", [P, NT, D])
        tp = [sc.pb(f"tp{j}", [P, CH, 2 * P]) for j in range(NT // 2)]
        stats_done = sc.sem("stats_done")
        mv_done = sc.sem("mv_done")
        veps_done = sc.sem("veps_done")
        rstd_done = sc.sem("rstd_done")
        xn_ready = sc.sem("xn_ready")
        turned = sc.sem("turned")
        with nc.Block() as block:
            @block.vector
            def _(dve):
                for h in range(2):
                    tiles = range(h * HALF, (h + 1) * HALF)
                    for t in tiles:
                        dve.bn_stats(stats[:, t, :], x_sb[:, t, :]).then_inc(stats_done, 1)
                    for t in tiles:
                        dve.wait_ge(stats_done, t + 1)
                        dve.bn_aggr(mv[:, t, :], stats[:, t, :]).then_inc(mv_done, 1)
                    hs = slice(h * HALF, (h + 1) * HALF)
                    dve.wait_ge(mv_done, (h + 1) * HALF)
                    dve.tensor_scalar(veps[:, hs], mv[:, hs, 1], LN_EPS, None, ALU.add).then_inc(veps_done, 1)
                for t in range(NT):
                    dve.wait_ge(rstd_done, t // HALF + 1)
                    dve.tensor_scalar(xn[:, t, :], x_sb[:, t, :], mv[:, t, 0:1], rstd[:, t:t + 1],
                                      ALU.subtract, ALU.mult).then_inc(xn_ready, 1)
                if add_to_x:
                    dve.wait_ge(xn_ready, NT)
                    dve.tensor_tensor(x_sb[:, :, :], x_sb[:, :, :], xn[:, :, :], ALU.add)

            @block.gpsimd
            def _(pool):
                for h in range(2):
                    hs = slice(h * HALF, (h + 1) * HALF)
                    pool.wait_ge(veps_done, h + 1)
                    pool.tensor_tensor(rstd[:, hs], veps[:, hs], neg_half[:, hs], ALU.pow).then_inc(rstd_done, 1)

            @block.tensor
            def _(pe):
                for t in range(NT):
                    pe.wait_ge(xn_ready, t + 1)
                    for c in range(CH):
                        mm = pe.transpose(tp[t // 2][:, c, (t % 2) * P:(t % 2 + 1) * P], xn[:, t, c * P:(c + 1) * P], ident[:, :])
                    mm.then_inc(turned, 1)

            @block.scalar
            def _(act):
                for k in range(NT // 2):
                    act.wait_ge(turned, 2 * k + 2)
                    act.activation(xnT[:, :, 2 * k * P:(2 * k + 2) * P], tp[k][:, :, :], ACT.Copy)


NKV, HD, GQ = 4, 128, 4
QH = NKV * GQ
KVW = NKV * HD
SKM = 2 * P
SPG = P // SQ
NG = B // SPG
RMS_EPS = 1e-6
SCALE = HD ** -0.5


def cross_attention(nc, x_sb, xnT, ident, neg_half, ctxT_dram, ctx_lastT, w, v_last):
    with scope(nc, "xa") as osc:
        wqh, wql = (osc.sb(n, [P, CH, QH * HD], F32R) for n in ("wqh", "wql"))
        wkvh, wkvl = (osc.sb(n, [P, CH, 2 * KVW], F32R) for n in ("wkvh", "wkvl"))
        wo = osc.sb("wo", [P, QH, D])
        bq = osc.sb("bq", [P, QH * HD])
        bk = osc.sb("bk", [P, KVW])
        bv = osc.sb("bv", [P, NKV])
        qn = osc.sb("qn", [P, 1])
        kn = osc.sb("kn", [P, 1])
        mask = osc.sb("mask", [P, SK])
        kT_last = osc.sb("kT_last", [P, NKV, B])
        kv_w_loaded = osc.sem("kv_w_loaded")
        w_loaded = osc.sem("w_loaded")
        v_stored = osc.sem("v_stored")

        with scope(nc, "xl") as sc:
            wq = sc.sb("wq", [P, CH, QH * HD])
            wkv = sc.sb("wkv", [P, CH, 2 * KVW])
            clT = sc.sb("clT", [P, CH, B])
            kb = sc.sb("kb", [B, NKV, HD])
            sq = sc.sb("sq", [B, NKV, HD])
            vb = sc.sb("vb", [B, KVW])
            ss = sc.sb("ss", [B, NKV])
            zero = sc.sb("zero", [B, NKV * KVW])
            pt = sc.pb("pt", [P, BLK])
            pk = sc.pb("pk", [P, BLK])
            pv = sc.pb("pv", [P, BLK])
            cl_loaded = sc.sem("cl_loaded")
            wq_loaded = sc.sem("wq_loaded")
            upper_ready = sc.sem("upper_ready")
            zeroed = sc.sem("zeroed")
            zero_stored = sc.sem("zero_stored")
            k_ready = sc.sem("k_ready")
            step = sc.sem("step")
            ss_ready = sc.sem("ss_ready")
            rs_ready = sc.sem("rs_ready")
            vb_ready = sc.sem("vb_ready")
            kn_ready = sc.sem("kn_ready")
            kT_ready = sc.sem("kT_ready")
            with nc.Block() as block:
                @block.sync
                def _(sp):
                    sp.dma_start(clT[:, :, :], ctx_lastT).then_inc(cl_loaded, 16)
                    for dst, src in ((wkv[:, :, 0:KVW], w["Wk"].rearrange("(h p) n -> p h n", p=P)),
                                     (wkv[:, :, KVW:2 * KVW], w["Wv"].rearrange("(h p) n -> p h n", p=P)),
                                     (bk[:, :], w["bk"].rearrange("(o n) -> o n", o=1).to_broadcast([P, KVW])),
                                     (kn[:, :], w["kn_w"].rearrange("(p o) -> p o", o=1)),
                                     (qn[:, :], w["qn_w"].rearrange("(p o) -> p o", o=1))):
                        sp.dma_start(dst, src).then_inc(kv_w_loaded, 16)
                    sp.dma_start(wq[:, :, :], w["Wq"].rearrange("(h p) n -> p h n", p=P)).then_inc(wq_loaded, 16)
                    for dst, src in ((bv[:, :], w["bvT"]),
                                     (bq[:, :], w["bq"].rearrange("(o n) -> o n", o=1).to_broadcast([P, QH * HD])),
                                     (wo[:, :, :], w["Wo"].rearrange("(h p) n -> p h n", p=P))):
                        sp.dma_start(dst, src).then_inc(w_loaded, 16)
                    for i in range(GQ):
                        sp.dma_start(mask[i * SQ:(i + 1) * SQ, :], w["mask"][0, :, :]).then_inc(w_loaded, 16)
                    sp.wait_ge(zeroed, 1)
                    sp.dma_start(v_last.rearrange("b n c -> b (n c)"), zero[:, :]).then_inc(zero_stored, 16)
                    sp.wait_ge(zero_stored, 16)
                    sp.wait_ge(vb_ready, 1)
                    for n in range(NKV):
                        o = slice(n * HD, (n + 1) * HD)
                        sp.dma_start(v_last[:, n, o], vb[:, o]).then_inc(v_stored, 16)
                    sp.wait_ge(v_stored, 16 * NKV)

                @block.gpsimd
                def _(pool):
                    pool.memset(zero[:, :], 0.0).then_inc(zeroed, 1)
                    pool.wait_ge(ss_ready, 1)
                    pool.tensor_tensor(ss[:, :], ss[:, :], neg_half[0:B, 0:NKV], ALU.pow).then_inc(rs_ready, 1)

                @block.tensor
                def _(pe):
                    pe.wait_ge(cl_loaded, 16)
                    pe.wait_ge(kv_w_loaded, 5 * 16)
                    for i, dst in enumerate((pk, pv)):
                        for c in range(CH):
                            mm = pe.matmul(dst[0:B, :], clT[:, c, :], wkv[:, c, i * KVW:(i + 1) * KVW], start=(c == 0), stop=(c == 1))
                        mm.then_inc(k_ready, 1)
                    pe.wait_ge(kn_ready, 1)
                    for n in range(NKV):
                        mm = pe.transpose(pt[:, n * B:(n + 1) * B], kb[:, n, :], ident[0:B, 0:B])
                    mm.then_inc(kT_ready, 1)

                @block.vector
                def _(dve):
                    ch = Chain(dve, step)
                    dve.wait_ge(k_ready, 1)
                    dve.wait_ge(kv_w_loaded, 5 * 16)
                    k3 = pk[0:B, :].rearrange("p (n c) -> p n c", n=NKV)
                    ch.link(dve.tensor_tensor(kb[:, :, :], k3, bk[0:B, :].rearrange("p (n c) -> p n c", n=NKV), ALU.add))
                    ch.link(dve.tensor_tensor(sq[:, :, :], kb[:, :, :], kb[:, :, :], ALU.mult))
                    ch.link(dve.tensor_reduce(ss[:, :], sq[:, :, :], AX.X, ALU.add))
                    dve.tensor_scalar(ss[:, :], ss[:, :], 1.0 / HD, RMS_EPS, ALU.mult, ALU.add).then_inc(ss_ready, 1)
                    dve.wait_ge(k_ready, 2)
                    dve.tensor_copy(vb[:, :], pv[0:B, :]).then_inc(vb_ready, 1)
                    dve.wait_ge(rs_ready, 1)
                    dve.tensor_tensor(kb[:, :, :], kb[:, :, :], ss[:, :].unsqueeze(2).to_broadcast([B, NKV, HD]), ALU.mult).then_inc(kn_ready, 1)
                    ch.link(dve.tensor_scalar(qn[:, :], qn[:, :], SCALE, None, ALU.mult))
                    dve.wait_ge(kT_ready, 1)
                    dve.tensor_scalar(kT_last[:, :, :], pt[:, 0:NKV * B].rearrange("p (n b) -> p n b", n=NKV), kn[:, 0:1], None, ALU.mult)
                    dve.tensor_copy(wkvh[:, :, :], wkv[:, :, :]).then_inc(upper_ready, 1)
                    dve.wait_ge(wq_loaded, 16)
                    dve.tensor_copy(wqh[:, :, :], wq[:, :, :]).then_inc(upper_ready, 1)
                    dve.wait_ge(upper_ready, 1)
                    dve.tensor_tensor(wkvl[:, :, :], wkv[:, :, :], wkvh.bitcast(F32)[:, :, :], ALU.subtract)
                    dve.wait_ge(upper_ready, 2)
                    dve.tensor_tensor(wql[:, :, :], wq[:, :, :], wqh.bitcast(F32)[:, :, :], ALU.subtract)

        with scope(nc, "xm") as sc:
            cx = [sc.sb(f"cx{i}", [P, CH, SKM]) for i in range(2)]
            v4 = [sc.sb(f"v4_{i}", [NKV, KVW]) for i in range(2)]
            cxh, cxl = (sc.sb(n, [P, CH, SKM], F32R) for n in ("cxh", "cxl"))
            kb = sc.sb("kb", [P, 2 * NKV, HD])
            ksq = sc.sb("ksq", [P, 2 * NKV, HD])
            kss = sc.sb("kss", [P, 2 * NKV])
            krs = sc.sb("krs", [P, 2 * NKV])
            kT = sc.sb("kT", [P, NKV, SK])
            V = [sc.sb(f"V{i}", [P, 2, KVW]) for i in range(2)]
            xqh, xql = (sc.sb(n, [P, CH, P], F32R) for n in ("xqh", "xql"))
            qb = sc.sb("qb", [P, QH, HD])
            qsq = sc.sb("qsq", [P, QH, HD])
            qss = sc.sb("qss", [P, QH])
            qrs = sc.sb("qrs", [P, QH])
            qT = sc.sb("qT", [P, SPG, QH, SQ])
            sm = sc.sb("sm", [P, NKV, SK])
            pr = sc.sb("pr", [P, NKV, SK])
            mx = sc.sb("mx", [P, NKV])
            neg = sc.sb("neg", [P, NKV])
            tot = sc.sb("tot", [P, NKV])
            rtot = sc.sb("rtot", [P, NKV])
            pT = sc.sb("pT", [P, NKV, 2, P])
            pTl = sc.sb("pTl", [NKV, P])
            oT = sc.sb("oT", [P, QH, P])
            S = [sc.pb(f"S{i}", [P, BLK]) for i in range(2)]
            KA = [sc.pb(f"KA{i}", [P, BLK]) for i in range(4)]
            T = [sc.pb(f"T{i}", [P, BLK]) for i in range(2)]
            cx_loaded = [sc.sem(f"cx_loaded{i}") for i in range(2)]
            v4_loaded = [sc.sem(f"v4_loaded{i}") for i in range(2)]
            cxh_out = sc.sem("cxh_out")
            cx_cut = sc.sem("cx_cut")
            xqh_ready = sc.sem("xqh_ready")
            kv_ready = sc.sem("kv_ready")
            kb_out = sc.sem("kb_out")
            v_out = sc.sem("v_out")
            ksq_done = sc.sem("ksq_done")
            kss_ready = sc.sem("kss_ready")
            krs_ready = sc.sem("krs_ready")
            kn_ready = sc.sem("kn_ready")
            kt_ready = sc.sem("kt_ready")
            kt_out = sc.sem("kt_out")
            kt_last = sc.sem("kt_last")
            k_step = sc.sem("k_step")
            xq_ready = sc.sem("xq_ready")
            q_ready = sc.sem("q_ready")
            q_out = sc.sem("q_out")
            qsq_done = sc.sem("qsq_done")
            q_step = sc.sem("q_step")
            qss_ready = sc.sem("qss_ready")
            qrs_ready = sc.sem("qrs_ready")
            qn_ready = sc.sem("qn_ready")
            qt_ready = sc.sem("qt_ready")
            qt_out = sc.sem("qt_out")
            s_ready = sc.sem("s_ready")
            s_out = sc.sem("s_out")
            max_done = sc.sem("max_done")
            neg_ready = sc.sem("neg_ready")
            exp_out = sc.sem("exp_out")
            rtot_ready = sc.sem("rtot_ready")
            p_ready = [sc.sem(f"p_ready{h}") for h in range(2)]
            pt_ready = sc.sem("pt_ready")
            pt_out = sc.sem("pt_out")
            pv_ready = sc.sem("pv_ready")
            ot_out = sc.sem("ot_out")
            wo_ready = sc.sem("wo_ready")
            wo_added = sc.sem("wo_added")

            def groups(eng, group):
                with eng.Fori(0, NG - 1) as g:
                    group(g, True)
                group(NG - 1, False)

            with nc.Block() as block:
                @block.sync
                def _(sp):
                    with sp.Fori(0, B // 2) as i:
                        for k in range(2):
                            n = i * 2 + k
                            sp.wait_ge(cx_cut, n + 1)
                            sp.dma_start(cx[k][:, :, :], ctxT_dram[bass.ds(n, 1), :, :, :].rearrange("o p c t -> p (o c) t")).then_inc(cx_loaded[k], 16)
                            sp.wait_ge(pv_ready, n + 1)
                            sp.dma_start(v4[k][:, :], v_last[bass.ds(n, 1), :, :].rearrange("o n c -> (o n) c")).then_inc(v4_loaded[k], 16)

                @block.gpsimd
                def _(pool):
                    def keys(n):
                        pool.wait_ge(kss_ready, n + 1)
                        pool.tensor_tensor(krs[:, :], kss[:, :], neg_half[:, 0:2 * NKV], ALU.pow).then_inc(krs_ready, 1)

                    def context_rest(n, k):
                        pool.wait_ge(cxh_out, n + 1)
                        pool.tensor_tensor(cxl[:, :, :], cx[k][:, :, :], cxh.bitcast(F32)[:, :, :], ALU.subtract).then_inc(cx_cut, 1)

                    def queries(g):
                        pool.wait_ge(qss_ready, g + 1)
                        pool.tensor_tensor(qrs[:, :], qss[:, :], neg_half[:, 0:QH], ALU.pow).then_inc(qrs_ready, 1)

                    pool.sem_inc(cx_cut, 2)
                    context_rest(0, 0)
                    keys(0)
                    queries(0)
                    context_rest(1, 1)

                    def group(g, more):
                        for i in range(SPG):
                            if more or i < SPG - 1:
                                keys(g * SPG + i + 1)
                            if i == 2 and more:
                                queries(g + 1)
                            if more or i < SPG - 2:
                                context_rest(g * SPG + i + 2, i % 2)

                    groups(pool, group)

                @block.tensor
                def _(pe):
                    def product(out, terms):
                        flat = [(a, b) for (ah, al), (bh, bl) in terms for a, b in ((ah, bh), (ah, bl), (al, bh))]
                        for i, (a, b) in enumerate(flat):
                            mm = pe.matmul(out, a, b, start=(i == 0), stop=(i == len(flat) - 1))
                        return mm

                    def projected(i, t):
                        tt, cols = slice(t * P, (t + 1) * P), slice(i * KVW, (i + 1) * KVW)
                        product(KA[2 * i + t][:, :], [((cxh[:, c, tt], cxl[:, c, tt]), (wkvh[:, c, cols], wkvl[:, c, cols]))
                                                      for c in range(CH)]).then_inc(kv_ready, 1)

                    def keys_turned(n):
                        pe.wait_ge(kn_ready, n + 1)
                        for i in range(2):
                            for h in range(2):
                                for t in range(2):
                                    mm = pe.transpose(T[i][:, (h * 2 + t) * P:(h * 2 + t + 1) * P], kb[:, t * NKV + 2 * i + h, :], ident[:, :])
                            mm.then_inc(kt_ready, 1)

                    def queries(g):
                        pe.wait_ge(xq_ready, g + 1)
                        for i in range(4):
                            cols = slice(i * BLK, (i + 1) * BLK)
                            product(KA[i][:, :], [((xqh[:, c, :], xql[:, c, :]), (wqh[:, c, cols], wql[:, c, cols]))
                                                  for c in range(CH)]).then_inc(q_ready, 1)

                    def queries_turned(i):
                        for h in range(4):
                            mm = pe.transpose(T[i % 2][:, h * P:(h + 1) * P], qb[:, i * 4 + h, :], ident[:, :])
                        mm.then_inc(qt_ready, 1)

                    pe.sem_inc(pv_ready, 2)
                    pe.wait_ge(cx_cut, 3)
                    for i in range(2):
                        for t in range(2):
                            projected(i, t)
                    keys_turned(0)
                    pe.wait_ge(kb_out, 2)
                    pe.wait_ge(v_out, 2)
                    pe.wait_ge(w_loaded, 7 * 16)
                    queries(0)
                    pe.wait_ge(qn_ready, 1)
                    pe.wait_ge(kt_out, 2)
                    for i in range(4):
                        if i >= 2:
                            pe.wait_ge(qt_out, i - 1)
                        queries_turned(i)

                    def group(g, more):
                        for i in range(SPG):
                            n = g * SPG + i
                            nxt = more or i < SPG - 1
                            pe.wait_ge(kt_last, n + 1)
                            for j in range(NKV):
                                if j % 2 == 0:
                                    pe.wait_ge(kt_out, n * 2 + 1 + j // 2)
                                if j == 1:
                                    pe.wait_ge(ot_out, n + 1)
                                if j >= 2:
                                    pe.wait_ge(s_out, n * 4 + j - 1)
                                if i == 0:
                                    pe.wait_ge(qt_out, g * 4 + j + 1)
                                pe.matmul(S[j % 2][:, 0:SK], qT[:, i, 4 * j:4 * j + 4, :], kT[:, j, :], start=True, stop=True).then_inc(s_ready, 1)
                            if i == 1 and more:
                                pe.wait_ge(kb_out, n * 2 + 2)
                                pe.wait_ge(v_out, n * 2 + 2)
                                queries(g + 1)
                            if nxt:
                                pe.wait_ge(cx_cut, n + 4)
                                pe.wait_ge(kb_out, n * 2 + 1)
                                if i == 1 and more:
                                    pe.wait_ge(q_out, g * 4 + 5)
                                projected(0, 0)
                                pe.wait_ge(kb_out, n * 2 + 2)
                                if i == 0:
                                    pe.wait_ge(wo_added, g + 1)
                                if i == 1 and more:
                                    pe.wait_ge(q_out, g * 4 + 6)
                                projected(0, 1)
                                pe.wait_ge(v_out, n * 2 + 1)
                                if i == 1 and more:
                                    pe.wait_ge(q_out, g * 4 + 7)
                                projected(1, 0)
                            for h in range(2):
                                pe.wait_ge(p_ready[h], n + 1)
                                for j in range(2):
                                    for t in range(2):
                                        mm = pe.transpose(T[h][:, (j * 2 + t) * P:(j * 2 + t + 1) * P], pr[:, 2 * h + j, t * P:(t + 1) * P], ident[:, :])
                                mm.then_inc(pt_ready, 1)
                                if h == 0 and nxt:
                                    pe.wait_ge(v_out, n * 2 + 2)
                                    if i == 1 and more:
                                        pe.wait_ge(q_out, g * 4 + 8)
                                    projected(1, 1)
                            pe.wait_ge(s_out, n * 4 + 4)
                            pe.transpose(S[0][0:NKV, 0:P], pr[:, :, SKM], ident[:, :]).then_inc(pt_ready, 1)
                            pe.wait_ge(v_out, n * 2 + 2)
                            for j in range(NKV):
                                if j % 2 == 0:
                                    pe.wait_ge(pt_out, n * 3 + 1 + j // 2)
                                o = slice(j * HD, (j + 1) * HD)
                                for t in range(2):
                                    pe.matmul(S[1][:, o], V[i % 2][:, t, o], pT[:, j, t, :], start=(j == 0 and t == 0), stop=False, skip_group_check=True)
                            pe.wait_ge(v4_loaded[i % 2], (g * 2 + i // 2) * 16 + 16)
                            pe.wait_ge(pt_out, n * 3 + 3)
                            for j in range(NKV):
                                o = slice(j * HD, (j + 1) * HD)
                                mm = pe.matmul(S[1][:, o], v4[i % 2][:, o], pTl[:, :], start=False, stop=True, skip_group_check=True)
                            mm.then_inc(pv_ready, 1)
                            if nxt:
                                keys_turned(n + 1)
                            if i == SPG - 1:
                                pe.wait_ge(ot_out, n + 2)
                                if more:
                                    pe.wait_ge(kb_out, n * 2 + 4)
                                for h in range(QH):
                                    mm = pe.matmul(KA[1][:, 0:D], oT[:, h, :], wo[:, h, :], start=(h == 0), stop=(h == QH - 1))
                                    if more and h == QH // 2:
                                        pe.wait_ge(qn_ready, g + 2)
                                        pe.wait_ge(kt_out, n * 2 + 4)
                                        queries_turned(0)
                                        queries_turned(1)
                                mm.then_inc(wo_ready, 1)
                                if more:
                                    for h in (2, 3):
                                        pe.wait_ge(qt_out, g * 4 + 3 + h)
                                        queries_turned(h)

                    groups(pe, group)

                @block.scalar
                def _(act):
                    def context(k, use):
                        act.wait_ge(cx_loaded[k], use * 16)
                        act.activation(cxh[:, :, :], cx[k][:, :, :], ACT.Copy).then_inc(cxh_out, 1)

                    def squares(n):
                        for t in range(2):
                            ks = slice(t * NKV, (t + 1) * NKV)
                            act.wait_ge(kb_out, n * 2 + t + 1)
                            act.activation(ksq[:, ks, :], kb[:, ks, :], ACT.Square).then_inc(ksq_done, 1)

                    def values(n, k, t):
                        act.wait_ge(kv_ready, n * 4 + 3 + t)
                        act.activation(V[k][:, t, :], KA[2 + t][:, :], ACT.Copy).then_inc(v_out, 1)

                    def keys(n):
                        for i in range(2):
                            act.wait_ge(kt_ready, n * 2 + i + 1)
                            act.activation(kT[:, 2 * i:2 * i + 2, 0:SKM], T[i][:, :].rearrange("p (h t) -> p h t", h=2), ACT.Copy,
                                           scale=kn[:, 0:1]).then_inc(kt_out, 1)

                    def query_tokens(g):
                        act.activation(xqh[:, :, :], xnT[:, :, bass.ds(g * P, P)], ACT.Copy).then_inc(xqh_ready, 1)

                    def query_squares(g):
                        act.wait_ge(q_out, g * 4 + 4)
                        act.activation(qsq[:, :, :], qb[:, :, :], ACT.Square).then_inc(qsq_done, 1)

                    def queries_turned(g):
                        for i in range(4):
                            act.wait_ge(qt_ready, g * 4 + i + 1)
                            dst = qT[:, :, 4 * i:4 * i + 4, :].rearrange("p b h s -> p h b s")
                            act.activation(dst, T[i % 2][:, :].rearrange("p (h b s) -> p h b s", h=4, b=SPG), ACT.Copy,
                                           scale=qn[:, 0:1]).then_inc(qt_out, 1)

                    query_tokens(0)
                    context(0, 1)
                    squares(0)
                    values(0, 0, 0)
                    values(0, 0, 1)
                    keys(0)
                    query_squares(0)
                    context(1, 1)
                    queries_turned(0)

                    def group(g, more):
                        for i in range(SPG):
                            n = g * SPG + i
                            nxt = more or i < SPG - 1
                            if i == 0 and more:
                                query_tokens(g + 1)
                            for j in range(NKV):
                                if j % 2 == 0:
                                    act.wait_ge(neg_ready, n * 2 + j // 2 + 1)
                                act.activation(pr[:, j, :], sm[:, j, :], ACT.Exp, bias=neg[:, j:j + 1],
                                               accum_out=tot[:, j:j + 1]).then_inc(exp_out, 1)
                            fresh = i == 1 and more
                            if nxt and not fresh:
                                squares(n + 1)
                            act.wait_ge(rtot_ready, n * 2 + 2)
                            for j in (2, 3):
                                ins = act.activation(pr[:, j, :], pr[:, j, :], ACT.Copy, scale=rtot[:, j:j + 1])
                            ins.then_inc(p_ready[1], 1)
                            if fresh:
                                squares(n + 1)
                            if nxt:
                                values(n + 1, (i + 1) % 2, 0)
                            act.wait_ge(pt_ready, n * 3 + 1)
                            act.activation(pT[:, 0:2, :, :], T[0][:, :].rearrange("p (j t q) -> p j t q", j=2, t=2), ACT.Copy).then_inc(pt_out, 1)
                            act.wait_ge(pt_ready, n * 3 + 2)
                            act.activation(pT[:, 2:4, :, :], T[1][:, :].rearrange("p (j t q) -> p j t q", j=2, t=2), ACT.Copy).then_inc(pt_out, 1)
                            act.wait_ge(pt_ready, n * 3 + 3)
                            act.activation(pTl[:, :], S[0][0:NKV, 0:P], ACT.Copy).then_inc(pt_out, 1)
                            if nxt:
                                values(n + 1, (i + 1) % 2, 1)
                                if more or i < SPG - 2:
                                    context(i % 2, g * 2 + i // 2 + 2)
                                keys(n + 1)
                            if i == SPG - 1 and more:
                                queries_turned(g + 1)
                            if i == 1 and more:
                                query_squares(g + 1)

                    groups(act, group)

                @block.vector
                def _(dve):
                    def biased(n, t):
                        dve.wait_ge(kv_ready, n * 4 + t + 1)
                        dve.tensor_tensor(kb[:, t * NKV:(t + 1) * NKV, :], KA[t][:, :].rearrange("p (h c) -> p h c", h=NKV),
                                          bk[:, :].rearrange("p (h c) -> p h c", h=NKV), ALU.add).then_inc(kb_out, 1)

                    def query_tokens_rest(g):
                        dve.wait_ge(xqh_ready, g + 1)
                        dve.tensor_tensor(xql[:, :, :], xnT[:, :, bass.ds(g * P, P)], xqh.bitcast(F32)[:, :, :], ALU.subtract).then_inc(xq_ready, 1)

                    def sums(n):
                        for t in range(2):
                            ks = slice(t * NKV, (t + 1) * NKV)
                            dve.wait_ge(ksq_done, n * 2 + t + 1)
                            dve.tensor_reduce(kss[:, ks], ksq[:, ks, :], AX.X, ALU.add).then_inc(k_step, 1)
                        dve.wait_ge(k_step, n * 2 + 2)
                        dve.tensor_scalar(kss[:, :], kss[:, :], 1.0 / HD, RMS_EPS, ALU.mult, ALU.add).then_inc(kss_ready, 1)

                    def normed(n):
                        dve.wait_ge(krs_ready, n + 1)
                        dve.tensor_tensor(kb[:, :, :], kb[:, :, :], krs[:, :].unsqueeze(2).to_broadcast([P, 2 * NKV, HD]),
                                          ALU.mult).then_inc(kn_ready, 1)
                        dve.tensor_copy(kT[:, :, SKM:SK], kT_last[:, :, bass.ds(n, 1)]).then_inc(kt_last, 1)

                    def queries_biased(g, i):
                        dve.wait_ge(q_ready, g * 4 + i + 1)
                        dve.tensor_tensor(qb[:, 4 * i:4 * i + 4, :], KA[i][:, :].rearrange("p (h c) -> p h c", h=4),
                                          bq[:, i * BLK:(i + 1) * BLK].rearrange("p (h c) -> p h c", h=4), ALU.add).then_inc(q_out, 1)

                    def query_sums(g):
                        dve.wait_ge(qsq_done, g + 1)
                        dve.tensor_reduce(qss[:, :], qsq[:, :, :], AX.X, ALU.add).then_inc(q_step, 1)
                        dve.wait_ge(q_step, g + 1)
                        dve.tensor_scalar(qss[:, :], qss[:, :], 1.0 / HD, RMS_EPS, ALU.mult, ALU.add).then_inc(qss_ready, 1)

                    def queries_normed(g):
                        dve.wait_ge(qrs_ready, g + 1)
                        dve.tensor_tensor(qb[:, :, :], qb[:, :, :], qrs[:, :].unsqueeze(2).to_broadcast([P, QH, HD]), ALU.mult).then_inc(qn_ready, 1)

                    dve.sem_inc(ot_out, 1)
                    dve.sem_inc(wo_added, 1)
                    query_tokens_rest(0)
                    for t in range(2):
                        biased(0, t)
                    sums(0)
                    normed(0)
                    dve.wait_ge(w_loaded, 7 * 16)
                    for i in range(4):
                        queries_biased(0, i)
                    query_sums(0)
                    queries_normed(0)

                    def group(g, more):
                        for i in range(SPG):
                            n = g * SPG + i
                            nxt = more or i < SPG - 1
                            for j in range(NKV):
                                dve.wait_ge(s_ready, n * 4 + j + 1)
                                dve.tensor_tensor(sm[:, j, :], S[j % 2][:, 0:SK], mask[:, :], ALU.add).then_inc(s_out, 1)
                                if j % 2:
                                    dve.wait_ge(s_out, n * 4 + j + 1)
                                    dve.tensor_reduce(mx[:, j - 1:j + 1], sm[:, j - 1:j + 1, :], AX.X, ALU.max).then_inc(max_done, 1)
                                    dve.wait_ge(max_done, n * 2 + j // 2 + 1)
                                    dve.tensor_scalar(neg[:, j - 1:j + 1], mx[:, j - 1:j + 1], -1.0, None, ALU.mult).then_inc(neg_ready, 1)
                            fresh = i == 1 and more
                            if fresh:
                                queries_biased(g + 1, 0)
                                queries_biased(g + 1, 1)
                            elif nxt:
                                biased(n + 1, 0)
                            for h in range(2):
                                js = slice(2 * h, 2 * h + 2)
                                dve.wait_ge(exp_out, n * 4 + 2 * h + 2)
                                dve.reciprocal(rtot[:, js], tot[:, js]).then_inc(rtot_ready, 1)
                                if h == 0:
                                    dve.wait_ge(rtot_ready, n * 2 + 1)
                                    dve.tensor_tensor(pr[:, js, :], pr[:, js, :], rtot[:, js].unsqueeze(2).to_broadcast([P, 2, SK]), ALU.mult).then_inc(p_ready[0], 1)
                                    if nxt and not fresh:
                                        biased(n + 1, 1)
                            if fresh:
                                queries_biased(g + 1, 2)
                                queries_biased(g + 1, 3)
                                biased(n + 1, 0)
                                biased(n + 1, 1)
                            if nxt:
                                sums(n + 1)
                                if i == 2 and more:
                                    query_sums(g + 1)
                                if i == 3:
                                    queries_normed(g + 1)
                                normed(n + 1)
                            if i == 0 and more:
                                query_tokens_rest(g + 1)
                            dve.wait_ge(pv_ready, n + 3)
                            dst = oT[:, :, i * SQ:(i + 1) * SQ].rearrange("p (j h) s -> p j h s", j=NKV)
                            dve.tensor_tensor(dst, S[1][:, :].rearrange("p (j h s) -> p j h s", j=NKV, h=GQ),
                                              bv[:, :].unsqueeze(2).unsqueeze(3).to_broadcast([P, NKV, GQ, SQ]), ALU.add).then_inc(ot_out, 1)
                        dve.wait_ge(wo_ready, g + 1)
                        xt = x_sb[:, bass.ds(g, 1), :].rearrange("p o c -> p (o c)")
                        dve.tensor_tensor(xt, xt, KA[1][:, 0:D], ALU.add).then_inc(wo_added, 1)

                    groups(dve, group)


RN = 64
RH = D // RN
SEQ_BLK = BLK // SQ
LEVELS = (2, 4, 8, 16)
PARAMS = ("x_k", "x_w", "x_a", "x_r", "x_v", "x_g", "w0", "a0", "k_k", "k_a", "r_k", "gn_scale", "gn_offset")
DECAY = -math.exp(-0.5)
PROJ = ("k0", "k1", "w1", "a1", "ns0", "ns1", "r0", "r1", "z0", "z1", "aa0", "aa1", "v0", "v1", "g1",
        "vt0", "vt1", "gg0", "gg1")
NQ = len(PROJ)
RING = 6


def rwkv(nc, x_sb, xnT, ident, w):
    with scope(nc, "rwkv") as sc:
        prm = sc.sb("prm", [P, CH, len(PARAMS)])

        def par(name, c, p0=0, p1=P):
            i = PARAMS.index(name)
            return prm[p0:p1, c, i:i + 1]

        W = {n: sc.sb(n, [P, CH, D]) for n in ("Wr", "Wk", "Wv", "Wo")}
        w1 = sc.sb("w1", [P, CH, 64])
        a1 = sc.sb("a1", [P, CH, 64])
        g1 = sc.sb("g1", [P, CH, P])
        w2 = sc.sb("w2", [64, D])
        a2 = sc.sb("a2", [64, D])
        g2 = sc.sb("g2", [P, D])
        head_ones = sc.sb("head_ones", [P, P])
        up_incl = sc.sb("up_incl", [P, P])
        up_strict = sc.sb("up_strict", [P, P])
        lo_pair = sc.sb("lo_pair", [P, P])
        up_pair = sc.sb("up_pair", [P, P])
        merge = [sc.sb(f"merge{n}", [P, P]) for n in LEVELS]
        carry = sc.sb("carry", [P, BLK])
        mix = {n: sc.sb(f"mix_{n}", [P, CH, BLK]) for n in "kwarvg"}
        names = ("xx", "k", "r", "v", "lw", "a", "g", "kk", "tmp", "L", "Lx")
        T = {n: sc.sb(f"T{n}", [P, CH, BLK]) for n in names}
        low = {n: sc.sb(f"low_{n}", [m, BLK]) for n, m in (("w", 64), ("a", 64), ("g", P))}
        A, Bm, K = (sc.sb(n, [P, 2, CH, BLK]) for n in ("facA", "facB", "facK"))
        R = sc.sb("facR", [P, CH, BLK])
        bonus, yT, k_add = mix["g"], mix["v"], mix["r"]
        norm = R
        vtok = sc.sb("vtok", [P, TPB, D])
        inv, invT, ew, mT, akT, rbT, rkT = ([sc.sb(f"{n}{u}", [P, RH, P]) for u in range(2)]
                                            for n in ("inv", "invT", "ew", "mT", "akT", "rbT", "rkT"))
        eT = [[sc.sb(f"eT{u}_{l}", [P, RH, P]) for l in range(len(LEVELS))] for u in range(2)]
        xs, us = ([sc.sb(f"{n}{u}", [P, D]) for u in range(2)] for n in ("xs", "us"))
        bank = [[sc.pb(f"bank{u}_{i}", [P, BLK]) for i in range(4)] for u in range(2)]
        ring = [bank[0][0], bank[0][1], bank[0][2], bank[0][3], bank[1][0], bank[1][1]]
        late = [bank[1][2], bank[1][3]]

        prm_loaded = sc.sem("prm_loaded")
        loaded = sc.sem("loaded")
        m_step = sc.sem("m_step")
        masks_ready = sc.sem("masks_ready")
        carry_ready = sc.sem("carry_ready")
        step = sc.sem("step")
        mix_ready = sc.sem("mix_ready")
        proj_ready = sc.sem("proj_ready")
        proj_out = sc.sem("proj_out")
        xx_ready = sc.sem("xx_ready")
        L_ready = sc.sem("L_ready")
        k2_ready = sc.sem("k2_ready")
        K_ready = sc.sem("K_ready")
        rk_ready = sc.sem("rk_ready")
        bonus_ready = sc.sem("bonus_ready")
        bonus_out = sc.sem("bonus_out")
        decay_ready = sc.sem("decay_ready")
        exp_ready = sc.sem("exp_ready")
        factors_ready = sc.sem("factors_ready")
        gated_ready = sc.sem("gated_ready")
        o_ready = sc.sem("o_ready")
        o_added = sc.sem("o_added")
        g_ready, g_out, t_ready, t_out, e_ready, w_ready, w_out, xv_ready, xv_out, u_ready, u_out, y_ready, y_out = (
            [sc.sem(f"{n}{u}") for u in range(2)] for n in
            ("g_ready", "g_out", "t_ready", "t_out", "e_ready", "w_ready", "w_out",
             "xv_ready", "xv_out", "u_ready", "u_out", "y_ready", "y_out"))
        HALVES = (slice(0, BLK // 2), slice(BLK // 2, BLK))
        NL = len(LEVELS)
        NTO = 2 * NL + 2

        def head(buf, h, j):
            if buf is R:
                return buf[:, h // 2, j * P:(j + 1) * P]
            return buf[:, h % 2, h // 2, j * P:(j + 1) * P]

        def heads(mask):
            return mask[:, :].unsqueeze(1).to_broadcast([P, RH, P])

        def four(b):
            return b[:, :].rearrange("p (h s) -> p h s", h=RH)

        with nc.Block() as block:
            @block.sync
            def _(sp):
                sp.dma_start(prm[:, :, :], w["prm"].rearrange("(h p) n -> p h n", p=P)).then_inc(prm_loaded, 16)
                for dst, src in ((W["Wk"][:, :, :], w["W_k"].rearrange("(h p) n -> p h n", p=P)),
                                 (w1[:, :, :], w["w1"].rearrange("(h p) n -> p h n", p=P)),
                                 (a1[:, :, :], w["a1"].rearrange("(h p) n -> p h n", p=P)),
                                 (W["Wr"][:, :, :], w["W_r"].rearrange("(h p) n -> p h n", p=P)),
                                 (w2[:, :], w["w2"]), (a2[:, :], w["a2"]),
                                 (W["Wv"][:, :, :], w["W_v"].rearrange("(h p) n -> p h n", p=P)),
                                 (g1[:, :, :], w["g1"].rearrange("(h p) n -> p h n", p=P)), (g2[:, :], w["g2"]),
                                 (W["Wo"][:, :, :], w["W_o"].rearrange("(h p) n -> p h n", p=P))):
                    sp.dma_start(dst, src).then_inc(loaded, 16)

            LOADED = 10 * 16
            HEAD_ONES = 3

            @block.gpsimd
            def _(pool):
                ch = Chain(pool, m_step)

                def keep(m, pattern, base, mult, op=ALU.is_ge):
                    shape = [P] + [n for _, n in pattern]
                    v = m[:, :] if len(pattern) == 1 else m[:, :].rearrange("p (a b) -> p a b", b=pattern[1][1])
                    return pool.affine_select(out=v, in_=v, compare_op=op, fill=0.0, base=base,
                                              pattern=pattern, channel_multiplier=mult)

                def same_block(m, n):
                    ch.link(keep(m, [[-n, P // n], [0, n]], 0, 1))
                    ch.link(keep(m, [[n, P // n], [0, n]], n - 1, -1))

                ch.link(pool.memset(head_ones[:, :], 1.0))
                same_block(head_ones, RN)
                assert ch.n == HEAD_ONES
                for f in (A, Bm, K):
                    ch.link(pool.memset(f[0:RN, 1, :, :], 0.0))
                    ch.link(pool.memset(f[RN:P, 0, :, :], 0.0))
                ch.link(pool.memset(up_incl[:, :], 1.0))
                same_block(up_incl, SQ)
                ch.link(keep(up_incl, [[1, P]], 0, -1))
                ch.link(pool.tensor_copy(up_strict[:, :], up_incl[:, :]))
                ch.link(keep(up_strict, [[1, P]], 0, -1, ALU.is_gt))
                ch.link(pool.tensor_copy(up_pair[:, :], up_strict[:, :]))
                same_block(up_pair, 2)
                ch.link(pool.memset(lo_pair[:, :], 1.0))
                same_block(lo_pair, 2)
                ch.link(keep(lo_pair, [[-1, P]], 0, 1, ALU.is_gt))
                for l, n in enumerate(LEVELS):
                    m = merge[l]
                    ch.link(pool.memset(m[:, :], 1.0))
                    same_block(m, 2 * n)
                    ch.link(keep(m, [[2 * n, P // (2 * n)], [0, 2 * n]], n - 1, -1))
                    v = m[:, :].rearrange("p (a b) -> p a b", b=2 * n)
                    ch.link(pool.affine_select(out=v, in_=v, compare_op=ALU.is_ge, fill=0.0, base=-n,
                                               pattern=[[0, P // (2 * n)], [1, 2 * n]], channel_multiplier=0))
                ch.link(pool.memset(carry[:, :], 1.0))
                cv = carry[:, :].rearrange("p (a b) -> p a b", b=SQ)
                ch.link(pool.memset(cv[:, :, 0:1], 0.0))
                pool.tensor_copy(lo_pair[:, 0:1], lo_pair[:, 0:1]).then_inc(masks_ready, 1)
                with pool.Fori(0, NBLK) as b:
                    pool.wait_ge(L_ready, b + 1)
                    pool.tensor_tensor(T["Lx"][:, :, :], T["L"][:, :, :], T["lw"][:, :, :], ALU.subtract).then_inc(decay_ready, 1)
                    pool.wait_ge(k2_ready, b + 1)
                    pool.wait_ge(exp_ready, b * 3 + 1)
                    for n, ts in enumerate(HALVES):
                        for i in range(2):
                            o = slice(RN * i, RN * i + RN)
                            pool.tensor_tensor(K[o, i, :, ts], T["k"][o, :, ts], mix["w"][o, :, ts], ALU.mult).then_inc(K_ready, 1)
                            pool.wait_ge(K_ready, b * 4 + 2 * n + i + 1)
                    for pair in range(2):
                        m = b * 2 + pair
                        for u in range(2):
                            pool.wait_ge(g_out[u], m * 5 + 2)
                            for l in range(NL):
                                pool.tensor_tensor(eT[u][l][:, :, :], mT[u][:, :, :], heads(merge[l]),
                                                   ALU.mult).then_inc(e_ready[u], 1)

            def tile_pairs(stages, b):
                for pair in range(2):
                    for stage in stages:
                        for u in range(2):
                            stage(u, 2 * pair + u, b * 2 + pair)

            @block.tensor
            def _(pe):
                pe.wait_ge(loaded, LOADED)
                with pe.Fori(0, NBLK) as b:
                    def mixed(m):
                        return mix_ready, b * 6 + "kwarvg".index(m) + 1

                    def weights(q):
                        c = int(q[-1])
                        o = slice(c * P, (c + 1) * P)
                        full = {"k": "Wk", "r": "Wr", "v": "Wv"}
                        if q in ("w1", "a1", "g1"):
                            m = q[0]
                            wt = {"w": w1, "a": a1, "g": g1}[m]
                            return [(wt[:, i, :], mix[m][:, i, :]) for i in range(CH)], mixed(m)
                        if q[:-1] in full:
                            m = q[0]
                            return [(W[full[m]][:, i, o], mix[m][:, i, :]) for i in range(CH)], mixed(m)
                        lows = {"z": (w2, "w", "w1"), "aa": (a2, "a", "a1"), "gg": (g2, "g", "g1")}
                        if q[:-1] in lows:
                            wt, m, of = lows[q[:-1]]
                            return [(wt[:, o], low[m][:, :])], (proj_out, b * NQ + PROJ.index(of) + 1)
                        return [(head_ones[:, :], T["tmp"][:, c, :])], (m_step, HEAD_ONES)

                    for i, q in enumerate(PROJ):
                        if i >= RING:
                            pe.wait_ge(proj_out, b * NQ + i - RING + 1)
                        dst = ring[i % RING]
                        if q in ("vt0", "vt1"):
                            pe.wait_ge(proj_out, b * NQ + PROJ.index("v1") + 1)
                            for j in range(2):
                                for c in range(CH):
                                    mm = pe.transpose(dst[:, j * D + c * P:j * D + (c + 1) * P],
                                                      T["v"][:, c, (2 * int(q[-1]) + j) * P:(2 * int(q[-1]) + j + 1) * P],
                                                      ident[:, :])
                        else:
                            pairs, waits = weights(q)
                            if q == "ns0":
                                pe.wait_ge(proj_out, b * NQ + PROJ.index("k1") + 1)
                            pe.wait_ge(*waits)
                            for n, (lhsT, rhs) in enumerate(pairs):
                                mm = pe.matmul(dst[0:lhsT.shape[-1], :], lhsT, rhs, start=(n == 0), stop=(n == len(pairs) - 1))
                        mm.then_inc(proj_ready, 1)
                    pe.wait_ge(rk_ready, b + 1)
                    pe.wait_ge(o_added, b + 1)
                    for c in range(CH):
                        pe.matmul(late[c][:, :], head_ones[:, :], T["tmp"][:, c, :], start=True, stop=True).then_inc(bonus_ready, 1)

                    def products(dst, lhs, rhs, j):
                        for h in range(RH):
                            mm = pe.matmul(four(dst)[:, h, :], head(lhs, h, j), head(rhs, h, j), start=True, stop=True)
                        return mm

                    def s_m(u, j, m):
                        pe.wait_ge(factors_ready, m + 1)
                        products(bank[u][0], A, Bm, j).then_inc(g_ready[u], 1)
                        products(bank[u][1], Bm, A, j).then_inc(g_ready[u], 1)

                    def s_ak_rb(u, j, m):
                        pe.wait_ge(y_out[u], m + 1)
                        if u == 1 and j == 1:
                            pe.wait_ge(bonus_out, b + 1)
                        pe.wait_ge(K_ready, m * 2 + 2)
                        products(bank[u][2], K, A, j).then_inc(g_ready[u], 1)
                        products(bank[u][3], Bm, R, j).then_inc(g_ready[u], 1)

                    def s_rk(u, j, m):
                        pe.wait_ge(g_out[u], m * 5 + 1)
                        products(bank[u][0], K, R, j).then_inc(g_ready[u], 1)

                    def s_xv(u, j, m):
                        pe.wait_ge(g_out[u], m * 5 + 3)
                        for h in range(RH):
                            mm = pe.matmul(four(bank[u][1])[:, h, :], akT[u][:, h, :],
                                           vtok[:, j, (h // 2) * P:(h // 2 + 1) * P], start=True, stop=True)
                        mm.then_inc(xv_ready[u], 1)

                    def s_w(l):
                        def go(u, j, m):
                            pe.wait_ge(t_out[u], m * NTO + 2 * l + 3)
                            pe.wait_ge(e_ready[u], m * NL + l + 1)
                            for h in range(RH):
                                mm = pe.matmul(four(bank[u][2])[:, h, :], eT[u][l][:, h, :], inv[u][:, h, :], start=True, stop=True)
                            mm.then_inc(w_ready[u], 1)
                        return go

                    def s_t(l):
                        def go(u, j, m):
                            pe.wait_ge(w_out[u], m * NL + l + 1)
                            if l == 0:
                                pe.wait_ge(g_out[u], m * 5 + 5)
                            if l < NL - 1:
                                for h in range(RH):
                                    mm = pe.matmul(four(bank[u][3])[:, h, :], invT[u][:, h, :], ew[u][:, h, :], start=True, stop=True)
                                mm.then_inc(t_ready[u], 1)
                            for h in range(RH):
                                mm = pe.matmul(four(bank[u][0])[:, h, :], ew[u][:, h, :], invT[u][:, h, :], start=True, stop=True)
                            mm.then_inc(t_ready[u], 1)
                        return go

                    def s_u(u, j, m):
                        pe.wait_ge(t_out[u], (m + 1) * NTO)
                        pe.wait_ge(xv_out[u], m * 2 + 2)
                        for h in range(RH):
                            mm = pe.matmul(four(bank[u][1])[:, h, :], invT[u][:, h, :],
                                           xs[u][:, (h // 2) * P:(h // 2 + 1) * P], start=True, stop=True)
                        mm.then_inc(u_ready[u], 1)

                    def s_y(u, j, m):
                        pe.wait_ge(u_out[u], m * 2 + 2)
                        for c in range(CH):
                            o = slice(c * P, (c + 1) * P)
                            dst = bank[u][2][:, c * D:(c + 1) * D]
                            pe.matmul(dst, us[u][:, o], rbT[u][:, 2 * c:2 * c + 2, :], start=True, stop=False)
                            mm = pe.matmul(dst, vtok[:, j, o], rkT[u][:, 2 * c:2 * c + 2, :], start=False, stop=True)
                        mm.then_inc(y_ready[u], 1)

                    stages = [s_m, s_ak_rb, s_rk, s_xv]
                    for l in range(NL):
                        stages += [s_w(l), s_t(l)]
                    tile_pairs(stages + [s_u, s_y], b)
                    for j in range(TPB):
                        if j % 2 == 0:
                            pe.wait_ge(gated_ready, b * 2 + j // 2 + 1)
                        if j == 0:
                            pe.wait_ge(y_out[1], b * 2 + 3)
                        for c in range(CH):
                            mm = pe.matmul(late[j // 2][:, (j % 2) * D:(j % 2 + 1) * D], T["kk"][:, c, j * P:(j + 1) * P],
                                           W["Wo"][:, c, :], start=(c == 0), stop=(c == CH - 1))
                        mm.then_inc(o_ready, 1)

            @block.scalar
            def _(act):
                act.wait_ge(prm_loaded, 16)
                with act.Fori(0, NBLK) as b:
                    for i, q in enumerate(PROJ):
                        c = int(q[-1])
                        src = ring[i % RING]
                        act.wait_ge(proj_ready, b * NQ + i + 1)
                        if q in ("w1", "a1", "g1"):
                            fn = {"w": ACT.Tanh, "a": ACT.Copy, "g": ACT.Sigmoid}[q[0]]
                            dst = low[q[0]]
                            ins = act.activation(dst[:, :], src[0:dst.shape[0], :], fn)
                        elif q[:-1] == "k":
                            act.activation(T["k"][:, c, :], src[:, :], ACT.Copy)
                            act.activation(T["kk"][:, c, :], src[:, :], ACT.Copy, scale=par("k_k", c))
                            ins = act.activation(T["tmp"][:, c, :], src[:, :], ACT.Square, scale=par("k_k", c))
                        elif q[:-1] in "rv":
                            ins = act.activation(T[q[0]][:, c, :], src[:, :], ACT.Copy)
                        elif q[:-1] == "z":
                            ins = act.activation(T["lw"][:, c, :], src[:, :], ACT.Sigmoid, bias=par("w0", c))
                        elif q[:-1] == "aa":
                            ins = act.activation(T["a"][:, c, :], src[:, :], ACT.Sigmoid, bias=par("a0", c))
                        elif q[:-1] == "gg":
                            ins = act.activation(T["g"][:, c, :], src[:, :], ACT.Copy)
                        elif q[:-1] == "ns":
                            ins = act.activation(norm[:, c, :], src[:, :], ACT.Sqrt)
                        else:
                            ins = act.activation(vtok[:, 2 * c:2 * c + 2, :], src[:, :].rearrange("p (j c) -> p j c", j=2), ACT.Copy)
                        ins.then_inc(proj_out, 1)
                    act.wait_ge(L_ready, b + 1)
                    act.activation(mix["w"][:, :, :], T["L"][:, :, :], ACT.Exp, scale=-DECAY).then_inc(exp_ready, 1)
                    act.activation(mix["a"][:, :, :], T["L"][:, :, :], ACT.Exp, scale=DECAY).then_inc(exp_ready, 1)
                    act.wait_ge(decay_ready, b + 1)
                    act.activation(mix["k"][:, :, :], T["Lx"][:, :, :], ACT.Exp, scale=DECAY).then_inc(exp_ready, 1)

                    def pick(dst, src):
                        s4 = src[:, :].rearrange("p (c n) -> p c n", c=CH)
                        d4 = dst[:, :].rearrange("p (c n) -> p c n", c=CH)
                        yield act.activation(d4[:, :, 0:RN], s4[:, :, 0:RN], ACT.Copy)
                        yield act.activation(d4[:, :, RN:P], s4[:, :, P + RN:D], ACT.Copy)

                    def s_xv(u, j, m):
                        act.wait_ge(xv_ready[u], m + 1)
                        for ins in pick(xs[u], bank[u][1]):
                            ins.then_inc(xv_out[u], 1)

                    def s_w(l):
                        def go(u, j, m):
                            act.wait_ge(w_ready[u], m * NL + l + 1)
                            act.activation(ew[u][:, :, :], four(bank[u][2]), ACT.Copy).then_inc(w_out[u], 1)
                        return go

                    def s_u(u, j, m):
                        act.wait_ge(u_ready[u], m + 1)
                        for ins in pick(us[u], bank[u][1]):
                            ins.then_inc(u_out[u], 1)

                    tile_pairs([s_xv] + [s_w(l) for l in range(NL)] + [s_u], b)

            @block.vector
            def _(dve):
                for u in range(2):
                    dve.sem_inc(y_out[u], 1)
                dve.sem_inc(o_added, 1)
                dve.wait_ge(prm_loaded, 16)
                PER = 9
                with dve.Fori(0, NBLK) as b:
                    ch = Chain(dve, step, b * PER)
                    toks = bass.ds(b * BLK, BLK)

                    def projected(q):
                        dve.wait_ge(proj_out, b * NQ + PROJ.index(q) + 1)

                    for c in range(CH):
                        xv = xnT[:, c, toks].rearrange("p (s t) -> p s t", t=SQ)
                        xxv = T["xx"][:, c, :].rearrange("p (s t) -> p s t", t=SQ)
                        ins = dve.tensor_tensor(xxv[:, :, 1:SQ], xv[:, :, 0:SQ - 1], xv[:, :, 1:SQ], ALU.subtract)
                        ins = dve.tensor_scalar(xxv[:, :, 0:1], xv[:, :, 0:1], -1.0, None, ALU.mult)
                    ins.then_inc(xx_ready, 1)
                    dve.wait_ge(xx_ready, b + 1)
                    for m in "kwarvg":
                        for c in range(CH):
                            ins = dve.scalar_tensor_tensor(mix[m][:, c, :], T["xx"][:, c, :], par("x_" + m, c),
                                                           xnT[:, c, toks], ALU.mult, ALU.add)
                        ins.then_inc(mix_ready, 1)
                    projected("ns1")
                    ch.link(dve.tensor_scalar(norm[:, :, :], norm[:, :, :], 1e-12, None, ALU.max))
                    ch.link(dve.reciprocal(norm[:, :, :], norm[:, :, :]))
                    ch.link(dve.tensor_tensor(T["xx"][:, :, :], T["kk"][:, :, :], norm[:, :, :], ALU.mult))
                    projected("z1")
                    dve.wait_ge(masks_ready, 1)
                    for c in range(CH):
                        ins = dve.tensor_tensor_scan(T["L"][:, c, :], carry[:, :], T["lw"][:, c, :], 0.0, ALU.mult, ALU.add)
                    ins.then_inc(L_ready, 1)
                    projected("aa1")
                    for c in range(CH):
                        ins = dve.tensor_scalar(k_add[:, c, :], T["a"][:, c, :], 1.0, par("k_a", c), ALU.subtract, ALU.mult)
                    ch.link(ins)
                    dve.scalar_tensor_tensor(T["k"][:, :, :], k_add[:, :, :], 1.0, T["k"][:, :, :], ALU.add, ALU.mult).then_inc(k2_ready, 1)
                    dve.wait_ge(k2_ready, b + 1)
                    for c in range(CH):
                        ins = dve.scalar_tensor_tensor(T["tmp"][:, c, :], T["r"][:, c, :], par("r_k", c), T["k"][:, c, :], ALU.mult, ALU.mult)
                    ins.then_inc(rk_ready, 1)
                    ch.link(dve.tensor_tensor(k_add[:, :, :], T["xx"][:, :, :], T["a"][:, :, :], ALU.mult))

                    def factors(ts, part):
                        dve.wait_ge(exp_ready, b * 3 + part + 1)
                        for i in range(2):
                            o = slice(RN * i, RN * i + RN)
                            if part == 0:
                                dve.tensor_tensor(Bm[o, i, :, ts], k_add[o, :, ts], mix["w"][o, :, ts], ALU.mult)
                            elif part == 2:
                                ins = dve.scalar_tensor_tensor(A[o, i, :, ts], T["xx"][o, :, ts], -1.0, mix["k"][o, :, ts], ALU.mult, ALU.mult)
                        if part == 1:
                            dve.tensor_tensor(R[:, :, ts], T["r"][:, :, ts], mix["a"][:, :, ts], ALU.mult)
                        elif part == 2:
                            ins.then_inc(factors_ready, 1)

                    def s_factors(part):
                        def go(u, j, m):
                            if j == 1:
                                factors(HALVES[1], part)
                        return go

                    for part in range(3):
                        factors(HALVES[0], part)
                    dve.wait_ge(bonus_ready, b * 2 + 2)
                    projected("v1")
                    projected("g1")
                    for c in range(CH):
                        ins = dve.tensor_tensor(bonus[:, c, :], late[c][:, :], T["v"][:, c, :], ALU.mult)
                    ins.then_inc(bonus_out, 1)

                    def masked(u, dst, i, mask, m, k):
                        dve.wait_ge(g_ready[u], m * 5 + k)
                        dve.tensor_tensor(dst[u][:, :, :], four(bank[u][i]), heads(mask), ALU.mult).then_inc(g_out[u], 1)

                    def s_m(u, j, m):
                        masked(u, inv, 0, lo_pair, m, 1)
                        masked(u, mT, 1, up_strict, m, 2)
                        dve.wait_ge(g_out[u], m * 5 + 2)
                        dve.tensor_tensor(inv[u][:, :, :], inv[u][:, :, :], heads(ident), ALU.add).then_inc(t_out[u], 1)
                        dve.tensor_tensor(invT[u][:, :, :], mT[u][:, :, :], heads(up_pair), ALU.mult).then_inc(t_out[u], 1)
                        dve.wait_ge(t_out[u], m * NTO + 2)
                        dve.tensor_tensor(invT[u][:, :, :], invT[u][:, :, :], heads(ident), ALU.add).then_inc(t_out[u], 1)

                    def s_ak_rb(u, j, m):
                        masked(u, akT, 2, up_strict, m, 3)
                        masked(u, rbT, 3, up_incl, m, 4)

                    def s_rk(u, j, m):
                        masked(u, rkT, 0, up_incl, m, 5)

                    def s_t(l):
                        def go(u, j, m):
                            n = m * (2 * NL - 1) + 2 * l
                            if l < NL - 1:
                                dve.wait_ge(t_ready[u], n + 1)
                                dve.tensor_tensor(inv[u][:, :, :], inv[u][:, :, :], four(bank[u][3]), ALU.add).then_inc(t_out[u], 1)
                                n += 1
                            dve.wait_ge(t_ready[u], n + 1)
                            dve.tensor_tensor(invT[u][:, :, :], invT[u][:, :, :], four(bank[u][0]), ALU.add).then_inc(t_out[u], 1)
                        return go

                    def s_y(u, j, m):
                        dve.wait_ge(y_ready[u], m + 1)
                        yb = bank[u][2][:, :].rearrange("p (c n) -> p c n", c=CH)
                        dve.tensor_copy(yT[0:RN, :, j * P:(j + 1) * P], yb[0:RN, :, 0:P])
                        dve.tensor_copy(yT[RN:P, :, j * P:(j + 1) * P], yb[RN:P, :, P:D]).then_inc(y_out[u], 1)

                    def gated(j, m):
                        for v in range(2):
                            dve.wait_ge(y_out[v], m + 2)
                        ts = HALVES[j]
                        for c in range(CH):
                            ins = dve.tensor_scalar(yT[:, c, ts], yT[:, c, ts], par("gn_scale", c), par("gn_offset", c), ALU.mult, ALU.add)
                        ch.link(ins)
                        ch.link(dve.tensor_tensor(yT[:, :, ts], yT[:, :, ts], bonus[:, :, ts], ALU.add))
                        dve.tensor_tensor(T["kk"][:, :, ts], yT[:, :, ts], T["g"][:, :, ts], ALU.mult).then_inc(gated_ready, 1)

                    merges = []
                    for l in range(NL):
                        merges += [s_t(l)] + ([s_factors(l)] if l < 3 else [])
                    def s_gated(u, j, m):
                        if j == 3:
                            gated(0, b * 2)

                    tile_pairs([s_m, s_ak_rb, s_rk, s_gated] + merges + [s_y], b)
                    gated(1, b * 2 + 1)
                    dve.wait_ge(o_ready, b * TPB + TPB)
                    for h in range(2):
                        xh = x_sb[:, bass.ds(b * TPB + 2 * h, 2), :]
                        ins = dve.tensor_tensor(xh, xh, late[h][:, :].rearrange("p (j c) -> p j c", j=2), ALU.add)
                    ins.then_inc(o_added, 1)
                    assert ch.n == PER, ch.n


BF16 = mybir.dt.bfloat16
CUT_AHEAD = 3
E = 16
TOPK0, GROUPS, TOPK_G, PER_G = 4, 4, 2, 4
TOPK1 = 2


def routing(nc, tag, xnT, ident, wg_view, combT, grouped, load_experts, x_sb=None, out_bias=None):
    with scope(nc, tag) as sc:
        wg = sc.sb("wg", [P, CH, E])
        lgT = sc.sb("lgT", [E, TOK])
        lt = sc.sb("lt", [P, E, E], BF16)
        s = sc.sb("s", [P, NT, E])
        key = sc.sb("key", [P, NT, E])
        tmp = sc.sb("tmp", [P, NT, E])
        col = sc.sb("col", [P, NT])
        gkey = sc.sb("gkey", [P, NT, GROUPS])
        rank = sc.sb("rank", [P, NT, E])
        pair = sc.sb("pair", [P, NT, E * E], BF16)
        pair2 = sc.sb("pair2", [P, NT, E * E], BF16)
        pieces = sc.sb("pieces", [P, NT, 3 * E])
        pieceb = sc.sb("pieceb", [P, NT, E], BF16)
        lp = [sc.pb(f"lp{j}", [P, BLK]) for j in range(2)]
        tm = sc.pb("tm", [P, NT, E])
        ct = [sc.pb(f"ct{j}", [P, BLK]) for j in range(2)]
        if out_bias:
            routed_b, shared_b = out_bias
            NB = E + shared_b.shape[0]
            sx = sc.sb("sx", [P, NT, NB])
            cb = sc.sb("cb", [NB, TOK])
            ob = sc.sb("ob", [NB, D])
            sx_ready = sc.sem("sx_ready")
            sx_turned = sc.sem("sx_turned")
            cb_out = sc.sem("cb_out")
            bias_ready = sc.sem("bias_ready")
            bias_added = sc.sem("bias_added")
        loaded = sc.sem("loaded")
        ones_set = sc.sem("ones_set")
        lt_ready = sc.sem("lt_ready")
        logits_ready = sc.sem("logits_ready")
        logits_out = sc.sem("logits_out")
        turned = sc.sem("turned")
        max_off = sc.sem("max_off")
        prob_ready = sc.sem("prob_ready")
        step = sc.sem("step")
        pieces_ready = sc.sem("pieces_ready")
        comb_turned = sc.sem("comb_turned")
        comb_out = sc.sem("comb_out")
        with nc.Block() as block:
            @block.sync
            def _(sp):
                sp.dma_start(wg[:, :, :], wg_view).then_inc(loaded, 16)
                if out_bias:
                    sp.dma_start(ob[0:E, :], routed_b).then_inc(loaded, 16)
                    sp.dma_start(ob[E:NB, :], shared_b).then_inc(loaded, 16)
                load_experts(sp)

            @block.gpsimd
            def _(pool):
                pool.memset(lt[:, :, :], 1.0).then_inc(ones_set, 1)
                pool.wait_ge(ones_set, 1)
                pool.affine_select(out=lt[:, :, :], in_=lt[:, :, :], compare_op=ALU.is_gt, fill=0.0,
                                   base=0, pattern=[[1, E], [-1, E]], channel_multiplier=0).then_inc(lt_ready, 1)

            @block.tensor
            def _(pe):
                pe.wait_ge(loaded, 48 if out_bias else 16)
                for b in range(NBLK):
                    if b >= 2:
                        pe.wait_ge(logits_out, b - 1)
                    for c in range(CH):
                        mm = pe.matmul(lp[b % 2][0:E, :], wg[:, c, :], xnT[:, c, b * BLK:(b + 1) * BLK],
                                       start=(c == 0), stop=(c == CH - 1))
                    mm.then_inc(logits_ready, 1)
                pe.wait_ge(logits_out, NBLK)
                for t in range(NT):
                    mm = pe.transpose(tm[:, t, :], lgT[:, t * P:(t + 1) * P], ident[0:E, 0:E])
                mm.then_inc(turned, 1)
                pe.wait_ge(pieces_ready, 3)
                for b in range(NBLK):
                    if b >= 2:
                        pe.wait_ge(comb_out, b - 1)
                    for j in range(TPB):
                        mm = pe.transpose(ct[b % 2][0:3 * E, j * P:(j + 1) * P], pieces[:, b * TPB + j, :], ident[:, :])
                    mm.then_inc(comb_turned, 1)
                if out_bias:
                    pe.wait_ge(sx_ready, 2)
                    for b in range(NBLK):
                        if b >= 2:
                            pe.wait_ge(cb_out, b - 1)
                        for j in range(TPB):
                            mm = pe.transpose(lp[b % 2][0:NB, j * P:(j + 1) * P], sx[:, b * TPB + j, :], ident[:, :])
                        mm.then_inc(sx_turned, 1)
                    pe.wait_ge(cb_out, NBLK)
                    for t2 in range(NT // 2):
                        if t2 >= 2:
                            pe.wait_ge(bias_added, t2 - 1)
                        for j in range(2):
                            mm = pe.matmul(lp[t2 % 2][:, j * D:(j + 1) * D], cb[:, (2 * t2 + j) * P:(2 * t2 + j + 1) * P],
                                           ob[:, :], start=True, stop=True)
                        mm.then_inc(bias_ready, 1)

            @block.scalar
            def _(act):
                for b in range(NBLK):
                    act.wait_ge(logits_ready, b + 1)
                    act.activation(lgT[:, b * BLK:(b + 1) * BLK], lp[b % 2][0:E, :], ACT.Copy).then_inc(logits_out, 1)
                if grouped:
                    act.wait_ge(max_off, 1)
                    act.activation(s[:, :, :], tmp[:, :, :], ACT.Exp).then_inc(prob_ready, 1)
                else:
                    act.wait_ge(turned, 1)
                    act.activation(s[:, :, :], tm[:, :, :], ACT.Sigmoid).then_inc(prob_ready, 1)
                for b in range(NBLK):
                    act.wait_ge(comb_turned, b + 1)
                    act.activation(combT[0:3 * E, b * BLK:(b + 1) * BLK], ct[b % 2][0:3 * E, :], ACT.Copy).then_inc(comb_out, 1)
                if out_bias:
                    for b in range(NBLK):
                        act.wait_ge(sx_turned, b + 1)
                        act.activation(cb[:, b * BLK:(b + 1) * BLK], lp[b % 2][0:NB, :], ACT.Copy).then_inc(cb_out, 1)

            @block.vector
            def _(dve):
                ch = Chain(dve, step)

                def bc(ap, n):
                    return ap.unsqueeze(2).to_broadcast([P, NT, n])

                def ranks(keys, n, out):
                    pv = pair[:, :, 0:n * n].rearrange("p t (i j) -> p t i j", j=n)
                    pv2 = pair2[:, :, 0:n * n].rearrange("p t (i j) -> p t i j", j=n)
                    kj = keys.unsqueeze(2).to_broadcast([P, NT, n, n])
                    ki = keys.unsqueeze(3).to_broadcast([P, NT, n, n])
                    ch.link(dve.tensor_tensor(pv2, kj, ki, ALU.is_equal))
                    ch.link(dve.tensor_tensor(pv2, pv2, lt[:, 0:n, 0:n].unsqueeze(1).to_broadcast([P, NT, n, n]), ALU.mult))
                    ch.link(dve.tensor_tensor(pv, kj, ki, ALU.is_gt))
                    ch.link(dve.tensor_tensor(pv, pv, pv2, ALU.add))
                    ch.link(dve.tensor_reduce(out, pv, AX.X, ALU.add))

                dve.wait_ge(turned, 1)
                if grouped:
                    ch.link(dve.tensor_reduce(col[:, :], tm[:, :, :], AX.X, ALU.max))
                    dve.tensor_tensor(tmp[:, :, :], tm[:, :, :], bc(col[:, :], E), ALU.subtract).then_inc(max_off, 1)
                    dve.wait_ge(prob_ready, 1)
                    ch.link(dve.tensor_reduce(col[:, :], s[:, :, :], AX.X, ALU.add))
                    ch.link(dve.reciprocal(col[:, :], col[:, :]))
                    ch.link(dve.tensor_tensor(s[:, :, :], s[:, :, :], bc(col[:, :], E), ALU.mult))
                    dve.wait_ge(lt_ready, 1)
                    ch.link(dve.tensor_reduce(gkey[:, :, :], s[:, :, :].rearrange("p t (g k) -> p t g k", g=GROUPS), AX.X, ALU.max))
                    ranks(gkey[:, :, :], GROUPS, rank[:, :, 0:GROUPS])
                    ch.link(dve.tensor_scalar(gkey[:, :, :], rank[:, :, 0:GROUPS], TOPK_G - 0.5, None, ALU.is_lt))
                    g4 = gkey[:, :, :].unsqueeze(3).to_broadcast([P, NT, GROUPS, PER_G])
                    k4 = key[:, :, :].rearrange("p t (g k) -> p t g k", g=GROUPS)
                    s4 = s[:, :, :].rearrange("p t (g k) -> p t g k", g=GROUPS)
                    t4 = tmp[:, :, :].rearrange("p t (g k) -> p t g k", g=GROUPS)
                    ch.link(dve.tensor_tensor(k4, s4, g4, ALU.mult))
                    ch.link(dve.tensor_copy(t4, g4))
                    ch.link(dve.scalar_tensor_tensor(key[:, :, :], tmp[:, :, :], 1.0, key[:, :, :], ALU.subtract, ALU.add))
                    ranks(key[:, :, :], E, rank[:, :, :])
                    ch.link(dve.scalar_tensor_tensor(s[:, :, :], rank[:, :, :], TOPK0 - 0.5, s[:, :, :], ALU.is_lt, ALU.mult))
                else:
                    dve.wait_ge(prob_ready, 1)
                    dve.wait_ge(lt_ready, 1)
                    ranks(s[:, :, :], E, rank[:, :, :])
                    ch.link(dve.scalar_tensor_tensor(s[:, :, :], rank[:, :, :], TOPK1 - 0.5, s[:, :, :], ALU.is_lt, ALU.mult))
                    ch.link(dve.tensor_reduce(col[:, :], s[:, :, :], AX.X, ALU.add))
                    ch.link(dve.reciprocal(col[:, :], col[:, :]))
                    ch.link(dve.tensor_tensor(s[:, :, :], s[:, :, :], bc(col[:, :], E), ALU.mult))
                    dve.tensor_copy(sx[:, :, 0:E], s[:, :, :]).then_inc(sx_ready, 1)
                    dve.memset(sx[:, :, E:NB], 1.0).then_inc(sx_ready, 1)
                for k in range(3):
                    ch.link(dve.tensor_copy(pieceb[:, :, :], s[:, :, :]))
                    dve.tensor_copy(pieces[:, :, k * E:(k + 1) * E], pieceb[:, :, :]).then_inc(pieces_ready, 1)
                    if k < 2:
                        ch.link(dve.tensor_tensor(s[:, :, :], s[:, :, :], pieceb[:, :, :], ALU.subtract))
                if out_bias:
                    for t2 in range(NT // 2):
                        dve.wait_ge(bias_ready, t2 + 1)
                        xt = x_sb[:, 2 * t2:2 * t2 + 2, :]
                        dve.tensor_tensor(xt, xt, lp[t2 % 2][:, :].rearrange("p (j c) -> p j c", j=2),
                                          ALU.add).then_inc(bias_added, 1)


class Weights:
    STAGES = 4

    def __init__(self, sc, chunks, piece, cut_down, biases):
        NC = len(chunks)
        self.chunks, self.piece, self.cut_down = chunks, piece, cut_down
        self.pieces = -(-NC // piece)
        self.raw1 = [sc.sb(f"raw1_{i}", [P, CH, piece * P]) for i in range(self.STAGES)]
        self.raw3 = [sc.sb(f"raw3_{i}", [P, CH, piece * P]) for i in range(self.STAGES)]
        self.arrived = [sc.sem(f"arrived{i}") for i in range(self.STAGES)]
        if cut_down:
            self.raw2 = [sc.sb(f"raw2_{i}", [P, piece, D]) for i in range(self.STAGES)]
        else:
            self.w2 = sc.sb("w2", [P, NC, D])
            self.w2_loaded = sc.sem("w2_loaded")
        self.ex = sc.sb("ex", [3 * E, sum(n for n, r in chunks if r)], BF16)
        if biases:
            self.b1 = sc.sb("b1", [P, NC])
            self.b3 = sc.sb("b3", [P, NC])
        self.small_loaded = sc.sem("small_loaded")
        self.small_loads, self.w2_loads, self.piece_loads = 1 + 2 * bool(biases), 2, None


def experts(nc, tag, x_sb, xnT, combT, act_func, w, load_piece, biases=False):
    chunks = w.chunks
    NC = len(chunks)
    n_feat = sum(n for n, _ in chunks)
    first = [sum(n for n, _ in chunks[:f]) for f in range(NC)]
    PARTS = 2 + w.cut_down
    with scope(nc, tag) as sc:
        xh = sc.sb("xh", [P, CH, BLK], F32R)
        xl = sc.sb("xl", [P, CH, BLK], F32R)
        w1h, w1l, w3h, w3l = (sc.sb(n, [P, CH, n_feat], F32R) for n in ("w1h", "w1l", "w3h", "w3l"))
        if w.cut_down:
            w2h, w2l = (sc.sb(n, [P, NC, D], F32R) for n in ("w2h", "w2l"))
        else:
            w2h, w2l = (sc.sb(n, [P, 2, D], F32R) for n in ("w2h", "w2l"))
            w2h_done = sc.sem("w2h_done")
            w2_cut = sc.sem("w2_cut")
        hh, hl = (sc.sb(n, [P, 2, BLK], F32R) for n in ("hh", "hl"))
        gate = sc.sb("gate", [P, 2, BLK])
        p1 = [sc.pb(f"p1_{j}", [P, BLK]) for j in range(2)]
        p3 = [sc.pb(f"p3_{j}", [P, BLK]) for j in range(2)]
        px = [sc.pb(f"px_{j}", [P, BLK]) for j in range(2)]
        acc = sc.pb("acc", [P, TPB, D])
        x_upper = sc.sem("x_upper")
        x_cut = sc.sem("x_cut")
        w_upper = sc.sem("w_upper")
        w_cut = sc.sem("w_cut")
        h1_ready = sc.sem("h1_ready")
        h3_ready = sc.sem("h3_ready")
        cx_ready = sc.sem("cx_ready")
        gate_done = sc.sem("gate_done")
        up_done = sc.sem("up_done")
        comb_done = sc.sem("comb_done")
        hh_done = sc.sem("hh_done")
        hl_done = sc.sem("hl_done")
        down_done = sc.sem("down_done")
        acc_ready = sc.sem("acc_ready")
        acc_free = sc.sem("acc_free")
        AHEAD = 2

        def blocks(eng, block):
            block(0, True)
            with eng.Fori(1, NBLK) as b:
                block(b, False)

        with nc.Block() as block:
            @block.sync
            def _(sp):
                for p in range(w.STAGES, w.pieces):
                    sp.wait_ge(w_cut, (p - w.STAGES + 1) * w.piece * PARTS)
                    load_piece(sp, p)

            @block.tensor
            def _(pe):
                def product(out, terms, last_stop=True, first_start=True):
                    flat = [(a, b) for (ah, al), (bh, bl) in terms for a, b in ((ah, bh), (ah, bl), (al, bh))]
                    for i, (a, b) in enumerate(flat):
                        mm = pe.matmul(out, a, b, start=first_start and i == 0,
                                       stop=last_stop and i == len(flat) - 1, skip_group_check=True)
                    return mm

                def one_block(b, cutting):
                    toks = bass.ds(b * BLK, BLK)
                    pe.wait_ge(x_cut, b + 1)
                    for f in range(NC + 1):
                        if f < NC:
                            rows, routed = chunks[f]
                            fs = slice(first[f], first[f] + rows)
                            n = b * NC + f
                            if cutting:
                                pe.wait_ge(w_cut, (f + 1) * PARTS)
                            pe.wait_ge(gate_done, n + 1)
                            product(p1[f % 2][0:rows, :], [((w1h[:, c, fs], w1l[:, c, fs]), (xh[:, c, :], xl[:, c, :]))
                                                           for c in range(CH)]).then_inc(h1_ready, 1)
                            pe.wait_ge(up_done, n + 1)
                            pe.wait_ge(comb_done, n + 1)
                            product(p3[f % 2][0:rows, :], [((w3h[:, c, fs], w3l[:, c, fs]), (xh[:, c, :], xl[:, c, :]))
                                                           for c in range(CH)]).then_inc(h3_ready, 1)
                            if routed:
                                pe.matmul(px[f % 2][0:rows, :], w.ex[:, fs], combT[0:3 * E, toks],
                                          start=True, stop=True).then_inc(cx_ready, 1)
                        if f == 0:
                            pe.wait_ge(acc_free, b + 1)
                        if f >= 1:
                            rows, _ = chunks[f - 1]
                            k = (f - 1) % 2
                            pe.wait_ge(hl_done, b * NC + f + AHEAD)
                            at = f - 1
                            if not w.cut_down:
                                pe.wait_ge(w2_cut, b * NC + f)
                                at = k
                            for j in range(TPB):
                                js = slice(j * P, (j + 1) * P)
                                clear, last = f == 1 and j % 2 == 0, f == NC
                                mm = product(acc[:, j, :], [((hh[0:rows, k, js], hl[0:rows, k, js]), (w2h[0:rows, at, :], w2l[0:rows, at, :]))],
                                             last_stop=last, first_start=clear)
                            mm.then_inc(down_done, 1)
                    pe.wait_ge(down_done, b * NC + NC + AHEAD)
                    pe.sem_inc(acc_ready, 1)

                pe.sem_inc(down_done, AHEAD)
                pe.wait_ge(w.small_loaded, 16 * w.small_loads)
                blocks(pe, one_block)

            if not w.cut_down:
                @block.gpsimd
                def _(pool):
                    def one_block(b, _):
                        for f, (rows, _) in enumerate(chunks):
                            pool.wait_ge(w2h_done, b * NC + f + 1)
                            pool.tensor_tensor(w2l[0:rows, f % 2, :], w.w2[0:rows, f, :], w2h.bitcast(F32)[0:rows, f % 2, :],
                                               ALU.subtract).then_inc(w2_cut, 1)

                    blocks(pool, one_block)

            @block.scalar
            def _(act):
                def one_block(b, _):
                    for f, (rows, routed) in enumerate(chunks):
                        n = b * NC + f
                        act.wait_ge(h1_ready, n + 1)
                        act.wait_ge(hl_done, n + 1)
                        bias = w.b1[0:rows, f:f + 1] if biases else 0.0
                        act.activation(gate[0:rows, f % 2, :], p1[f % 2][0:rows, :], act_func,
                                       bias=bias).then_inc(gate_done, 1)
                        if not w.cut_down:
                            act.wait_ge(down_done, n + 1)
                            act.activation(w2h[0:rows, f % 2, :], w.w2[0:rows, f, :], ACT.Copy).then_inc(w2h_done, 1)

                act.sem_inc(gate_done, AHEAD)
                act.wait_ge(w.small_loaded, 16 * w.small_loads)
                if not w.cut_down:
                    act.wait_ge(w.w2_loaded, 16 * w.w2_loads)
                blocks(act, one_block)

            @block.vector
            def _(dve):
                n_rt = sum(1 for _, r in chunks if r)

                def cut(f):
                    rows, _ = chunks[f]
                    fs = slice(first[f], first[f] + rows)
                    p, i = divmod(f, w.piece)
                    k = p % w.STAGES
                    if i == 0:
                        dve.wait_ge(w.arrived[k], (p // w.STAGES + 1) * 16 * w.piece_loads)
                    raw = slice(i * P, i * P + rows)
                    parts = [(w1h[:, :, fs], w1l[:, :, fs], w.raw1[k][:, :, raw]), (w3h[:, :, fs], w3l[:, :, fs], w.raw3[k][:, :, raw])]
                    if w.cut_down:
                        parts.append((w2h[0:rows, f, :], w2l[0:rows, f, :], w.raw2[k][0:rows, i, :]))
                    for upper, _, src in parts:
                        dve.tensor_copy(upper, src).then_inc(w_upper, 1)
                    for i, (upper, rest, src) in enumerate(parts):
                        dve.wait_ge(w_upper, f * PARTS + i + 1)
                        dve.tensor_tensor(rest, src, upper.bitcast(F32), ALU.subtract).then_inc(w_cut, 1)

                def add_to_x(b):
                    dve.wait_ge(acc_ready, b + 1)
                    for h in range(2):
                        xt = x_sb[:, bass.ds(b * TPB + 2 * h, 2), :]
                        ins = dve.tensor_tensor(xt, xt, acc[:, 2 * h:2 * h + 2, :], ALU.add)
                    ins.then_inc(acc_free, 1)

                def one_block(b, cutting):
                    xt = xnT[:, :, bass.ds(b * BLK, BLK)]
                    dve.tensor_copy(xh[:, :, :], xt).then_inc(x_upper, 1)
                    dve.wait_ge(x_upper, b + 1)
                    dve.tensor_tensor(xl[:, :, :], xt, xh.bitcast(F32)[:, :, :], ALU.subtract).then_inc(x_cut, 1)
                    if cutting:
                        for f in range(CUT_AHEAD):
                            cut(f)
                    else:
                        add_to_x(b - 1)
                    for f, (rows, routed) in enumerate(chunks):
                        n = b * NC + f
                        k = f % 2
                        hid = gate[0:rows, k, :]
                        dve.wait_ge(h3_ready, n + 1)
                        dve.wait_ge(gate_done, n + 1 + AHEAD)
                        if biases:
                            ins = dve.scalar_tensor_tensor(hid, p3[k][0:rows, :], w.b3[0:rows, f:f + 1], hid, ALU.add, ALU.mult)
                        else:
                            ins = dve.tensor_tensor(hid, p3[k][0:rows, :], hid, ALU.mult)
                        ins.then_inc(up_done, 1)
                        dve.wait_ge(up_done, n + 1 + AHEAD)
                        if routed:
                            dve.wait_ge(cx_ready, b * n_rt + sum(1 for _, r in chunks[:f] if r) + 1)
                            dve.tensor_tensor(hid, hid, px[k][0:rows, :], ALU.mult).then_inc(comb_done, 1)
                            dve.wait_ge(comb_done, n + 1 + AHEAD)
                        else:
                            dve.sem_inc(comb_done, 1)
                        dve.wait_ge(down_done, n + 1)
                        dve.tensor_copy(hh[0:rows, k, :], hid).then_inc(hh_done, 1)
                        dve.wait_ge(hh_done, n + 1)
                        dve.tensor_tensor(hl[0:rows, k, :], hid, hh.bitcast(F32)[0:rows, k, :], ALU.subtract).then_inc(hl_done, 1)
                        if cutting and f + CUT_AHEAD < NC:
                            cut(f + CUT_AHEAD)

                dve.sem_inc(up_done, AHEAD)
                dve.sem_inc(comb_done, AHEAD)
                dve.sem_inc(hl_done, AHEAD)
                dve.sem_inc(acc_free, 1)
                dve.wait_ge(w.small_loaded, 16 * w.small_loads)
                blocks(dve, one_block)
                add_to_x(NBLK - 1)


HID0, SHID0 = 176, 352
F0 = E * HID0
CHUNKS0 = [(P, True)] * (F0 // P) + [(P, False), (P, False), (SHID0 - 2 * P, False)]


def ffn0(nc, x_sb, xnT, ident, combT, w):
    n_all = F0 + SHID0
    with scope(nc, "w0") as sc:
        wt = Weights(sc, CHUNKS0, 2, False, False)
        wt.piece_loads = 2

        def load_piece(sp, p):
            f0, f1 = p * wt.piece * P, min((p + 1) * wt.piece * P, n_all)
            k = p % wt.STAGES
            for dst, src in ((wt.raw1[k], w["W1"]), (wt.raw3[k], w["W3"])):
                sp.dma_start(dst[:, :, 0:f1 - f0], src[:, f0:f1].rearrange("(h p) f -> p h f", p=P)).then_inc(wt.arrived[k], 16)

        def load(sp):
            sp.dma_start(wt.ex[:, :], w["expand"].bitcast(BF16)).then_inc(wt.small_loaded, 16)
            for p in range(wt.STAGES):
                load_piece(sp, p)
            whole = n_all // P
            sp.dma_start(wt.w2[:, 0:whole, :], w["W2"][0:whole * P, :].rearrange("(k p) c -> p k c", p=P)).then_inc(wt.w2_loaded, 16)
            sp.dma_start(wt.w2[0:n_all - whole * P, whole, :], w["W2"][whole * P:n_all, :]).then_inc(wt.w2_loaded, 16)

        routing(nc, "route0", xnT, ident, w["Wg"].rearrange("(h p) e -> p h e", p=P), combT, True, load)
        experts(nc, "ffn0", x_sb, xnT, combT, ACT.Silu, wt, load_piece)


SH1 = 2
CHUNKS1 = [(P, True)] * E + [(P, False)] * SH1


def ffn1(nc, x_sb, xnT, ident, combT, w):
    with scope(nc, "w1") as sc:
        wt = Weights(sc, CHUNKS1, SH1, True, True)
        wt.piece_loads = 2 * CH + 1

        def load_piece(sp, p):
            k, m, e0 = p % wt.STAGES, wt.piece, p * wt.piece
            gate, up, down = (w["rg"], w["rw1"], w["rw2"]) if e0 < E else (w["sg"], w["sw1"], w["sw2"])
            e0 = e0 if e0 < E else 0
            for dst, src in ((wt.raw1[k], gate), (wt.raw3[k], up)):
                for h in range(CH):
                    sp.dma_start(dst[:, h, :].rearrange("p (e f) -> p e f", e=m),
                                 src[e0:e0 + m, h * P:(h + 1) * P, :].rearrange("e p f -> p e f")).then_inc(wt.arrived[k], 16)
            sp.dma_start(wt.raw2[k][:, :, :], down[e0:e0 + m, :, :].rearrange("e f c -> f e c")).then_inc(wt.arrived[k], 16)

        def load(sp):
            sp.dma_start(wt.ex[:, :], w["expand1"].bitcast(BF16)).then_inc(wt.small_loaded, 16)
            sp.dma_start(wt.b1[:, :], w["gate_bias"]).then_inc(wt.small_loaded, 16)
            sp.dma_start(wt.b3[:, :], w["up_bias"]).then_inc(wt.small_loaded, 16)
            for p in range(wt.STAGES):
                load_piece(sp, p)

        routing(nc, "route1", xnT, ident, w["wa"].rearrange("(h p) e -> p h e", p=P), combT, False, load, x_sb, (w["rb2"], w["sb2"]))
        experts(nc, "ffn1", x_sb, xnT, combT, ACT.Gelu, wt, load_piece, biases=True)


LH, LD, FD = 16, 16, 64
LE = LD + 1
LF = LH * FD
NJ = LF // P
PAIR = 2 * LE
WIN = P
VW = PAIR * (NJ - 1) + WIN
SKM = 2 * P
SPG = P // SQ
NG = B // SPG
DEN_EPS = 1e-8


def linear_attention(nc, x_sb, xnT, ident, ctxT_dram, ctx_lastT, w, v_last):
    with scope(nc, "la") as osc:
        wq, wo = (osc.sb(n, [P, CH, D]) for n in ("wq", "wo"))
        wkh, wkl, wvh, wvl = (osc.sb(n, [P, CH, D], F32R) for n in ("wkh", "wkl", "wvh", "wvl"))
        qf = osc.sb("qf", [P, LF // CH])
        kfh, kfl = (osc.sb(n, [P, LF // CH], F32R) for n in ("kfh", "kfl"))
        kp_last = osc.sb("kp_last", [P, NJ, B])
        bq = osc.sb("bq", [P, CH])
        bk = osc.sb("bk", [P, CH])
        bv = osc.sb("bv", [P, D])
        bo = osc.sb("bo", [1, D])
        ones = osc.sb("ones", [1, P])
        maskT = osc.sb("maskT", [P, 2, B])
        w_loaded = osc.sem("w_loaded")

        with scope(nc, "ll") as sc:
            wk, wv = (sc.sb(n, [P, CH, D]) for n in ("wk", "wv"))
            kf = sc.sb("kf", [P, LF // CH])
            clT = sc.sb("clT", [P, CH, B])
            mk = sc.sb("mk", [B, SK])
            kT = sc.sb("kT", [P, CH, B])
            vb = sc.sb("vb", [B, LH, LD])
            vx = sc.sb("vx", [B, VW])
            pk = sc.pb("pk", [P, BLK])
            pf = sc.pb("pf", [P, NJ, B])
            pv = sc.pb("pv", [P, BLK])
            cl_loaded = sc.sem("cl_loaded")
            zeroed = sc.sem("zeroed")
            k_ready = sc.sem("k_ready")
            k_out = sc.sem("k_out")
            v_ready = sc.sem("v_ready")
            kp_ready = sc.sem("kp_ready")
            upper_ready = sc.sem("upper_ready")
            step = sc.sem("step")
            vx_ready = sc.sem("vx_ready")
            stored = sc.sem("stored")
            NW = 9
            with nc.Block() as block:
                @block.sync
                def _(sp):
                    sp.dma_start(clT[:, :, :], ctx_lastT).then_inc(cl_loaded, 16)
                    sp.dma_start(mk[:, :], w["mask"]).then_inc(cl_loaded, 16)
                    sp.dma_start(maskT[:, :, :], w["maskT"]).then_inc(cl_loaded, 16)
                    for dst, src in ((wk, w["Wk"]), (wv, w["Wv"]), (wq, w["Wq"]), (wo, w["Wo"])):
                        sp.dma_start(dst[:, :, :], src.rearrange("(h p) n -> p h n", p=P)).then_inc(w_loaded, 16)
                    sp.dma_start(bk[:, :], w["bkT"]).then_inc(w_loaded, 16)
                    sp.dma_start(bq[:, :], w["bqT"]).then_inc(w_loaded, 16)
                    sp.dma_start(bv[:, :], w["bv"].rearrange("(o n) -> o n", o=1).to_broadcast([P, D])).then_inc(w_loaded, 16)
                    sp.dma_start(bo[:, :], w["bo"].rearrange("(o n) -> o n", o=1)).then_inc(w_loaded, 16)
                    sp.wait_ge(zeroed, 1)
                    for h in range(P // LD):
                        sp.dma_start(kf[h * LD:(h + 1) * LD, h * FD:(h + 1) * FD], w["WkfT"]).then_inc(w_loaded, 16)
                        sp.dma_start(qf[h * LD:(h + 1) * LD, h * FD:(h + 1) * FD], w["WqfT"]).then_inc(w_loaded, 16)
                    sp.wait_ge(vx_ready, 1)
                    sp.dma_start(v_last, vx[:, :]).then_inc(stored, 16)
                    sp.wait_ge(stored, 16)
                    sp.wait_ge(w_loaded, 16 * (8 + 16))

                @block.gpsimd
                def _(pool):
                    pool.memset(ones[:, :], 1.0)
                    pool.memset(vx[:, :], 0.0)
                    pool.memset(kf[:, :], 0.0)
                    pool.memset(qf[:, :], 0.0).then_inc(zeroed, 1)

                @block.tensor
                def _(pe):
                    pe.wait_ge(cl_loaded, 48)
                    pe.wait_ge(w_loaded, 16 * 24)
                    for h in range(CH):
                        for c in range(CH):
                            mm = pe.matmul(pk[:, h * B:(h + 1) * B], wk[:, c, h * P:(h + 1) * P], clT[:, c, :], start=(c == 0), stop=(c == 1))
                    mm.then_inc(k_ready, 1)
                    for c in range(CH):
                        mm = pe.matmul(pv[0:B, 0:D], clT[:, c, :], wv[:, c, :], start=(c == 0), stop=(c == 1))
                    mm.then_inc(v_ready, 1)
                    pe.wait_ge(k_out, 2)
                    for j in range(NJ):
                        mm = pe.matmul(pf[:, j, :], kf[:, (j % 4) * P:(j % 4 + 1) * P], kT[:, j // 4, :], start=True, stop=True)
                    mm.then_inc(kp_ready, 1)

                @block.scalar
                def _(act):
                    act.wait_ge(w_loaded, 16 * 24)
                    act.wait_ge(k_ready, 1)
                    for h in range(CH):
                        act.activation(kT[:, h, :], pk[:, h * B:(h + 1) * B], ACT.Identity, bias=bk[:, h:h + 1]).then_inc(k_out, 1)
                    act.wait_ge(kp_ready, 1)
                    act.activation(kp_last[:, :, :], pf[:, :, :], ACT.Relu)

                @block.vector
                def _(dve):
                    ch = Chain(dve, step)
                    dve.wait_ge(cl_loaded, 48)
                    dve.wait_ge(v_ready, 1)
                    dve.wait_ge(zeroed, 1)
                    dve.wait_ge(w_loaded, 16 * 24)
                    ch.link(dve.tensor_tensor(vb[:, :, :], pv[0:B, 0:D].rearrange("p (h d) -> p h d", h=LH),
                                              bv[0:B, :].rearrange("p (h d) -> p h d", h=LH), ALU.add))
                    v3 = vx[:, 0:LH * LE].rearrange("p (h e) -> p h e", h=LH)
                    dve.tensor_scalar(v3[:, :, 0:LD], vb[:, :, :], mk[:, SKM:SK], None, ALU.mult)
                    dve.tensor_copy(v3[:, :, LD:LE], mk[:, SKM:SK].unsqueeze(1).to_broadcast([B, LH, 1])).then_inc(vx_ready, 1)
                    cuts = ((wkh, wkl, wk), (wvh, wvl, wv), (kfh, kfl, kf))
                    for up, _, src in cuts:
                        dve.tensor_copy(up.ap(), src.ap()).then_inc(upper_ready, 1)
                    for i, (up, rest, src) in enumerate(cuts):
                        dve.wait_ge(upper_ready, i + 1)
                        dve.tensor_tensor(rest.ap(), src.ap(), up.bitcast(F32).ap(), ALU.subtract)

        with scope(nc, "lm") as sc:
            cx = [sc.sb(f"cx{i}", [P, CH, SKM]) for i in range(2)]
            v1 = [sc.sb(f"v1_{i}", [P, NJ, 2, LE]) for i in range(2)]
            cxh, cxl, kTh, kTl = (sc.sb(n, [P, CH, SKM], F32R) for n in ("cxh", "cxl", "kTh", "kTl"))
            kp = sc.sb("kp", [P, 2, LF])
            vb = sc.sb("vb", [P, 2, D])
            vx = [sc.sb(f"vx{i}", [P, 2, VW]) for i in range(2)]
            kvd = sc.sb("kvd", [P, NJ, SPG, PAIR])
            qT = sc.sb("qT", [P, CH, P])
            qp = sc.sb("qp", [P, NJ, P])
            raw = sc.sb("raw", [P, NJ, PAIR])
            den = sc.sb("den", [P, LH])
            rden = sc.sb("rden", [P, LH])
            at = sc.sb("at", [P, LH, LD])
            atT = sc.sb("atT", [P, CH, P])
            T0 = sc.pb("T0", [P, BLK])
            KT = sc.pb("KT", [P, BLK])
            VP = sc.pb("VP", [P, BLK])
            KP = [sc.pb(f"KP{i}", [P, BLK]) for i in range(2)]
            KV = sc.pb("KV", [P, NJ, P])
            G = sc.pb("G", [P, BLK])
            zeroed = sc.sem("zeroed")
            cx_loaded = [sc.sem(f"cx_loaded{i}") for i in range(2)]
            last_loaded = [sc.sem(f"last_loaded{i}") for i in range(2)]
            cxh_out = sc.sem("cxh_out")
            cx_cut = sc.sem("cx_cut")
            kth_out = sc.sem("kth_out")
            last_done = sc.sem("last_done")
            last_used = sc.sem("last_used")
            kt_ready = sc.sem("kt_ready")
            kt_out = sc.sem("kt_out")
            v_ready = sc.sem("v_ready")
            vb_out = sc.sem("vb_out")
            vx_ready = sc.sem("vx_ready")
            kp_ready = sc.sem("kp_ready")
            kp_out = sc.sem("kp_out")
            kv_ready = sc.sem("kv_ready")
            kv_out = sc.sem("kv_out")
            q_ready = sc.sem("q_ready")
            q_out = sc.sem("q_out")
            qp_ready = sc.sem("qp_ready")
            qp_out = sc.sem("qp_out")
            o_ready = sc.sem("o_ready")
            raw_out = sc.sem("raw_out")
            step = sc.sem("step")
            at_ready = sc.sem("at_ready")
            at_turned = sc.sem("at_turned")
            atT_out = sc.sem("atT_out")
            wo_ready = sc.sem("wo_ready")
            wo_added = sc.sem("wo_added")
            JB = BLK // (SPG * PAIR)
            OB = [KP[0], KP[1], G]

            def groups(eng, group):
                with eng.Fori(0, NG - 1) as g:
                    group(g, True)
                group(NG - 1, False)

            with nc.Block() as block:
                @block.sync
                def _(sp):
                    with sp.Fori(0, B // 2) as i:
                        for k in range(2):
                            n = i * 2 + k
                            sp.wait_ge(cx_cut, n + 1)
                            sp.dma_start(cx[k][:, :, :], ctxT_dram[bass.ds(n, 1), :, :, :].rearrange("o p c t -> p (o c) t")).then_inc(cx_loaded[k], 16)
                            sp.wait_ge(last_used, n + 1)
                            sp.dma_start(v1[k][:, :, :, :].rearrange("p j h e -> p (j h e)"),
                                         v_last[bass.ds(n, 1), 0:LH * LE].to_broadcast([P, LH * LE])).then_inc(last_loaded[k], 16)

                @block.gpsimd
                def _(pool):
                    pool.memset(kvd[:, :, :, :], 0.0).then_inc(zeroed, 1)
                    for i in range(2):
                        pool.memset(vx[i][:, :, :], 0.0).then_inc(zeroed, 1)

                    def context_rest(n, k):
                        pool.wait_ge(cxh_out, n + 1)
                        pool.tensor_tensor(cxl[:, :, :], cx[k][:, :, :], cxh.bitcast(F32)[:, :, :], ALU.subtract).then_inc(cx_cut, 1)

                    pool.sem_inc(cx_cut, 2)
                    context_rest(0, 0)
                    context_rest(1, 1)

                    def group(g, more):
                        for i in range(SPG):
                            if more or i < SPG - 2:
                                context_rest(g * SPG + i + 2, i % 2)

                    groups(pool, group)

                @block.tensor
                def _(pe):
                    def product(out, terms):
                        flat = [(a, b) for (ah, al), (bh, bl) in terms for a, b in ((ah, bh), (ah, bl), (al, bh))]
                        for i, (a, b) in enumerate(flat):
                            mm = pe.matmul(out, a, b, start=(i == 0), stop=(i == len(flat) - 1))
                        return mm

                    def keys(n):
                        pe.wait_ge(cx_cut, n + 3)
                        for h in range(CH):
                            hs = slice(h * P, (h + 1) * P)
                            mm = product(KT[:, h * SKM:(h + 1) * SKM], [((wkh[:, c, hs], wkl[:, c, hs]), (cxh[:, c, :], cxl[:, c, :])) for c in range(CH)])
                        mm.then_inc(kt_ready, 1)

                    def values(n):
                        for t in range(2):
                            ts = slice(t * P, (t + 1) * P)
                            mm = product(VP[:, t * D:(t + 1) * D], [((cxh[:, c, ts], cxl[:, c, ts]), (wvh[:, c, :], wvl[:, c, :])) for c in range(CH)])
                        mm.then_inc(v_ready, 1)

                    def features(n, g=None):
                        pe.wait_ge(kt_out, n * 2 + 2)
                        for t in range(2):
                            for h in range(CH):
                                if t:
                                    pe.wait_ge(kp_out, n * 4 + h + 1)
                                elif g is not None:
                                    pe.wait_ge(raw_out, g * 3 + h + 1)
                                ts = slice(t * P, (t + 1) * P)
                                product(KP[h][:, :], [((kTh[:, h, ts], kTl[:, h, ts]), (kfh[:, :], kfl[:, :]))]).then_inc(kp_ready, 1)

                    def key_times_value(n, k):
                        pe.wait_ge(kp_out, n * 4 + 4)
                        pe.wait_ge(vx_ready, n * 4 + 4)
                        pe.wait_ge(kv_out, n + 1)
                        for j in range(NJ):
                            o = slice(j * P, (j + 1) * P)
                            win = slice(j * PAIR, j * PAIR + WIN)
                            for t in range(2):
                                mm = pe.matmul(KV[:, j, :], kp[:, t, o], vx[k][:, t, win], start=(t == 0), stop=(t == 1))
                        mm.then_inc(kv_ready, 1)

                    def queries(g):
                        pe.wait_ge(wo_added, g + 1)
                        for h in range(CH):
                            for c in range(CH):
                                mm = pe.matmul(G[:, h * P:(h + 1) * P], wq[:, c, h * P:(h + 1) * P], xnT[:, c, bass.ds(g * P, P)], start=(c == 0), stop=(c == 1))
                        mm.then_inc(q_ready, 1)

                    def query_features(g, n):
                        pe.wait_ge(q_out, g * 2 + 2)
                        pe.wait_ge(kp_out, n * 4 + 4)
                        for j in range(NJ):
                            mm = pe.matmul(KP[j // 4][:, (j % 4) * P:(j % 4 + 1) * P], qf[:, (j % 4) * P:(j % 4 + 1) * P], qT[:, j // 4, :], start=True, stop=True)
                            if j % 4 == 3:
                                mm.then_inc(qp_ready, 1)

                    def outputs(g, n):
                        pe.wait_ge(kv_out, n + 2)
                        for j in range(NJ):
                            mm = pe.matmul(OB[j // JB][:, (j % JB) * SPG * PAIR:(j % JB + 1) * SPG * PAIR], qp[:, j, :],
                                           kvd[:, j, :, :], start=True, stop=True)
                            if j % JB == JB - 1 or j == NJ - 1:
                                mm.then_inc(o_ready, 1)

                    def project(g):
                        pe.wait_ge(at_ready, g + 1)
                        for c in range(CH):
                            mm = pe.transpose(T0[:, c * P:(c + 1) * P], at[:, c * 8:(c + 1) * 8, :], ident[:, :])
                        mm.then_inc(at_turned, 1)
                        pe.wait_ge(atT_out, g + 1)
                        for c in range(CH):
                            pe.matmul(G[:, 0:D], atT[:, c, :], wo[:, c, :], start=(c == 0), stop=False)
                        pe.matmul(G[:, 0:D], ones[:, :], bo[:, :], start=False, stop=True).then_inc(wo_ready, 1)

                    keys(0)
                    values(0)
                    features(0)

                    def group(g, more):
                        for i in range(SPG):
                            n = g * SPG + i
                            nxt = more or i < SPG - 1
                            if nxt:
                                keys(n + 1)
                            if i == 1:
                                queries(g)
                            if i == 2:
                                query_features(g, n)
                            if nxt:
                                pe.wait_ge(vb_out, n + 1)
                                values(n + 1)
                            key_times_value(n, i % 2)
                            if i == 2:
                                pe.wait_ge(qp_out, g * 2 + 2)
                            if i == SPG - 1:
                                outputs(g, n)
                            if nxt:
                                features(n + 1, g if i == SPG - 1 else None)
                            if i == SPG - 1:
                                project(g)

                    groups(pe, group)

                @block.scalar
                def _(act):
                    def context(n, k, use, first=False):
                        act.wait_ge(cx_loaded[k], use * 16)
                        if not first:
                            act.wait_ge(v_ready, n)
                        act.activation(cxh[:, :, :], cx[k][:, :, :], ACT.Copy).then_inc(cxh_out, 1)

                    def keys(n):
                        act.wait_ge(kt_ready, n + 1)
                        for h in range(CH):
                            act.activation(kTh[:, h, :], KT[:, h * SKM:(h + 1) * SKM], ACT.Identity, bias=bk[:, h:h + 1]).then_inc(kth_out, 1)

                    def features(n):
                        for t in range(2):
                            for h in range(CH):
                                act.wait_ge(kp_ready, n * 4 + t * 2 + h + 1)
                                act.activation(kp[:, t, h * BLK:(h + 1) * BLK], KP[h][:, :], ACT.Relu).then_inc(kp_out, 1)

                    def queries(g):
                        act.wait_ge(q_ready, g + 1)
                        for h in range(CH):
                            act.activation(qT[:, h, :], G[:, h * P:(h + 1) * P], ACT.Identity, bias=bq[:, h:h + 1]).then_inc(q_out, 1)

                    def query_features(g):
                        for h in range(CH):
                            act.wait_ge(qp_ready, g * 2 + h + 1)
                            act.activation(qp[:, 4 * h:4 * h + 4, :], KP[h][:, :].rearrange("p (j t) -> p j t", j=4), ACT.Relu).then_inc(qp_out, 1)

                    context(0, 0, 1, first=True)
                    keys(0)
                    context(1, 1, 1)
                    features(0)

                    def group(g, more):
                        for i in range(SPG):
                            n = g * SPG + i
                            nxt = more or i < SPG - 1
                            if nxt:
                                keys(n + 1)
                            if i == 1:
                                queries(g)
                            if i == 2:
                                query_features(g)
                            if more or i < SPG - 2:
                                context(n + 2, i % 2, g * 2 + i // 2 + 2)
                            if nxt:
                                features(n + 1)
                        act.wait_ge(at_turned, g + 1)
                        act.activation(atT[:, :, :], T0[:, 0:D].rearrange("p (c t) -> p c t", c=CH), ACT.Copy).then_inc(atT_out, 1)

                    groups(act, group)

                @block.vector
                def _(dve):
                    def values(n, k):
                        dve.wait_ge(v_ready, n + 1)
                        dve.tensor_tensor(vb[:, :, :], VP[:, :].rearrange("p (t c) -> p t c", t=2), bv[:, :].unsqueeze(1).to_broadcast([P, 2, D]),
                                          ALU.add).then_inc(vb_out, 1)
                        dve.wait_ge(vb_out, n + 1)
                        for t in range(2):
                            m = maskT[:, t, bass.ds(n, 1)]
                            v3 = vx[k][:, t, 0:LH * LE].rearrange("p (h e) -> p h e", h=LH)
                            dve.tensor_scalar(v3[:, :, 0:LD], vb[:, t, :].rearrange("p (h d) -> p h d", h=LH), m, None, ALU.mult).then_inc(vx_ready, 1)
                            dve.tensor_copy(v3[:, :, LD:LE], m.unsqueeze(1).to_broadcast([P, LH, 1])).then_inc(vx_ready, 1)

                    def keys_rest(n):
                        dve.wait_ge(kth_out, n * 2 + 2)
                        for h in range(CH):
                            dve.scalar_tensor_tensor(kTl[:, h, :], KT[:, h * SKM:(h + 1) * SKM], bk[:, h:h + 1], kTh.bitcast(F32)[:, h, :],
                                                     ALU.add, ALU.subtract).then_inc(kt_out, 1)

                    def own(h):
                        return slice(h * FD, (h + 1) * FD), slice(h * LE, (h + 1) * LE)

                    dve.sem_inc(kv_out, 1)
                    dve.sem_inc(wo_added, 1)
                    dve.sem_inc(last_used, 2)
                    dve.wait_ge(zeroed, 3)
                    keys_rest(0)
                    values(0, 0)

                    def group(g, more):
                        ch = Chain(dve, step, g * 2)
                        for i in range(SPG):
                            n = g * SPG + i
                            nxt = more or i < SPG - 1
                            dve.wait_ge(last_loaded[i % 2], (g * 2 + i // 2 + 1) * 16)
                            for h in range(2):
                                o, e = own(h)
                                ins = dve.tensor_tensor(kvd[o, :, i, e], v1[i % 2][o, :, h, :], kp_last[o, :, bass.ds(n, 1)].to_broadcast([FD, NJ, LE]),
                                                        ALU.mult).then_inc(last_done, 1)
                            dve.wait_ge(last_done, n * 2 + 2)
                            dve.sem_inc(last_used, 1)
                            if nxt:
                                keys_rest(n + 1)
                                values(n + 1, (i + 1) % 2)
                            dve.wait_ge(kv_ready, n + 1)
                            for h in range(2):
                                o, e = own(h)
                                ins = dve.tensor_tensor(kvd[o, :, i, e], kvd[o, :, i, e], KV[o, :, e], ALU.add)
                            ins.then_inc(kv_out, 1)
                        for k, j in enumerate(range(0, NJ, JB)):
                            dve.wait_ge(o_ready, g * 3 + k + 1)
                            m = min(JB, NJ - j)
                            for s in range(SPG):
                                o = slice(s * SQ, (s + 1) * SQ)
                                src = OB[k][o, 0:m * SPG * PAIR].rearrange("p (j s e) -> p j s e", j=m, s=SPG)[:, :, s, :]
                                ins = dve.tensor_copy(raw[o, j:j + m, :], src)
                            ins.then_inc(raw_out, 1)
                        dve.wait_ge(raw_out, g * 3 + 3)
                        r3 = raw[:, :, :].rearrange("p j (h e) -> p (j h) e", h=2)
                        ch.link(dve.tensor_scalar(den[:, :], r3[:, :, LD], DEN_EPS, None, ALU.add))
                        ch.link(dve.reciprocal(rden[:, :], den[:, :]))
                        dve.tensor_tensor(at[:, :, :], r3[:, :, 0:LD], rden[:, :].unsqueeze(2).to_broadcast([P, LH, LD]), ALU.mult).then_inc(at_ready, 1)
                        dve.wait_ge(wo_ready, g + 1)
                        xt = x_sb[:, bass.ds(g, 1), :].rearrange("p o c -> p (o c)")
                        dve.tensor_tensor(xt, xt, G[:, 0:D], ALU.add).then_inc(wo_added, 1)

                    groups(dve, group)


AH, AD = 16, 16
HPH = AH // CH
PAIRS = P // 32


def self_attention(nc, x_sb, xnT, ident, w, scratch):
    with scope(nc, "sa") as osc:
        turnedT = osc.sb("turnedT", [P, CH, TOK])
        wp = osc.sb("wp", [P, CH, D])
        bp = osc.sb("bp", [1, D])
        ones = osc.sb("ones", [1, P])
        stored = [osc.sem(f"stored{i}") for i in range(2)]
        gathered = osc.sem("gathered")
        wp_loaded = osc.sem("wp_loaded")
        with scope(nc, "sa1") as sc:
            wq = sc.sb("wq", [P, CH, D])
            wk = sc.sb("wk", [P, CH, D])
            wv = sc.sb("wv", [P, CH, D])
            xb = sc.sb("xb", [P, CH, BLK])
            par = sc.sb("par", [P, 2])
            qT = sc.sb("qT", [P, CH, BLK])
            kT = sc.sb("kT", [P, 2, CH, BLK])
            WIDE = HPH * (P + AD)
            vx = sc.sb("vx", [P, TPB, CH, WIDE])
            s = sc.sb("s", [P, 2, AH, SQ])
            e = sc.sb("e", [P, 2, AH, SQ])
            pT = sc.sb("pT", [P, AH, SQ])
            pbd = sc.sb("pbd", [P, 2, AH, P])
            mx = sc.sb("mx", [P, 2, AH])
            sm = sc.sb("sm", [P, 2, AH])
            oT = sc.sb("oT", [P, 2, CH, P])
            S = sc.pb("S", [P, PAIRS, CH * 2, P])
            aux = [sc.pb(f"aux{i}", [P, BLK]) for i in range(4)]
            loaded = sc.sem("loaded")
            par_step = sc.sem("par_step")
            zeroed = sc.sem("zeroed")
            xb_ready = sc.sem("xb_ready")
            qk_ready = sc.sem("qk_ready")
            q_out = sc.sem("q_out")
            k_out = sc.sem("k_out")
            v_ready = sc.sem("v_ready")
            v_out = sc.sem("v_out")
            s_ready = sc.sem("s_ready")
            s_out_a = sc.sem("s_out_a")
            s_out_v = sc.sem("s_out_v")
            max_done = sc.sem("max_done")
            sub_done = sc.sem("sub_done")
            exp_done = sc.sem("exp_done")
            soft_step = sc.sem("soft_step")
            pT_ready = sc.sem("pT_ready")
            pbd_ready = sc.sem("pbd_ready")
            pT_free = sc.sem("pT_free")
            o_ready = sc.sem("o_ready")
            oT_ready = sc.sem("oT_ready")
            store_free = sc.sem("store_free")

            def spread(t, h):
                return vx[:, t, h, :].rearrange("p (n c) -> p n c", c=P + AD)[:, :, 0:AD]

            with nc.Block() as block:
                @block.sync
                def _(sp):
                    for dst, src in ((wq, w["Wq"]), (wk, w["Wk"]), (wv, w["Wv"])):
                        sp.dma_start(dst[:, :, :], src.rearrange("(h p) n -> p h n", p=P)).then_inc(loaded, 16)
                    sp.dma_start(wp[:, :, :], w["Wproj"].rearrange("(h p) n -> p h n", p=P)).then_inc(wp_loaded, 16)
                    sp.dma_start(bp[:, :], w["bproj"].rearrange("(o n) -> o n", o=1)).then_inc(wp_loaded, 16)
                    sp.sem_inc(store_free, 2)
                    out = scratch.rearrange("t b (h n) d s -> t h (n d) b s", h=CH)
                    back = scratch.rearrange("t b n d s -> t d (b n) s")
                    with sp.Fori(0, NT // 8) as i:
                        for k in range(8):
                            t = i * 8 + k
                            sp.wait_ge(oT_ready, t + 3)
                            for h in range(CH):
                                sp.dma_start(out[bass.ds(t, 1), h, :, :, :].rearrange("o p b s -> (o p) b s"),
                                             oT[:, k % 2, h, :].rearrange("p (b s) -> p b s", s=SQ)).then_inc(stored[k % 2], 16)
                            sp.wait_ge(stored[k % 2], (i * 4 + k // 2) * 32 + 32)
                            sp.sem_inc(store_free, 1)
                            sp.dma_start(turnedT[k * AD:(k + 1) * AD, bass.ds(i, 1), :].rearrange("p o (n s) -> p (o n) s", s=SQ),
                                         back[bass.ds(t, 1), :, :, :].rearrange("o d n s -> (o d) n s")).then_inc(gathered, 16)
                    sp.wait_ge(gathered, 16 * NT)

                @block.gpsimd
                def _(pool):
                    ch = Chain(pool, par_step)
                    pool.memset(ones[:, :], 1.0)
                    pf = pbd[:, 0, 0:PAIRS * 2, 0:1]
                    ch.link(pool.memset(pf, 1.0))
                    ch.link(pool.affine_select(out=pf, in_=pf, compare_op=ALU.is_ge, fill=0.0, base=0,
                                               pattern=[[-16, PAIRS * 2], [0, 1]], channel_multiplier=1))
                    ch.link(pool.affine_select(out=pf, in_=pf, compare_op=ALU.is_ge, fill=0.0, base=15,
                                               pattern=[[16, PAIRS * 2], [0, 1]], channel_multiplier=-1))
                    ch.link(pool.tensor_tensor(par[:, 0:1], pbd[:, 0, 0, 0:1], pbd[:, 0, 2, 0:1], ALU.add))
                    ch.link(pool.tensor_tensor(par[:, 0:1], par[:, 0:1], pbd[:, 0, 4, 0:1], ALU.add))
                    ch.link(pool.tensor_tensor(par[:, 0:1], par[:, 0:1], pbd[:, 0, 6, 0:1], ALU.add))
                    ch.link(pool.tensor_scalar(par[:, 1:2], par[:, 0:1], -1.0, 1.0, ALU.mult, ALU.add))
                    assert ch.n == 7
                    pool.memset(pbd[:, :, :, :], 0.0).then_inc(zeroed, 1)
                    pool.memset(vx[:, :, :, :], 0.0).then_inc(zeroed, 1)

                @block.tensor
                def _(pe):
                    pe.sem_inc(o_ready, 2)
                    pe.wait_ge(loaded, 48)
                    with pe.Fori(0, NBLK) as b:
                        pe.wait_ge(xb_ready, b + 1)
                        for i, wt in enumerate((wq, wk)):
                            if i == 1:
                                pe.wait_ge(oT_ready, b * TPB + 2)
                            for h in range(CH):
                                for c in range(CH):
                                    mm = pe.matmul(aux[2 * i + h][:, :], wt[:, c, h * P:(h + 1) * P], xb[:, c, :],
                                                   start=(c == 0), stop=(c == CH - 1))
                                mm.then_inc(qk_ready, 1)
                        for i in range(2):
                            pe.wait_ge(q_out, b * 2 + i + 1)
                            for j in range(2):
                                for c in range(CH):
                                    mm = pe.matmul(aux[i][:, j * D:(j + 1) * D], xb[:, c, (2 * i + j) * P:(2 * i + j + 1) * P],
                                                   wv[:, c, :], start=(c == 0), stop=(c == CH - 1))
                            mm.then_inc(v_ready, 1)
                        pe.wait_ge(q_out, b * 2 + 2)
                        pe.wait_ge(k_out, b * 4 + 4)
                        for j in range(TPB + 1):
                            if j < TPB:
                                n = b * TPB + j
                                pe.wait_ge(s_out_a, n + 1)
                                pe.wait_ge(s_out_v, n + 1)
                                for h in range(CH):
                                    for o in range(2):
                                        for i in range(PAIRS):
                                            r = slice(32 * i, 32 * i + 32)
                                            mm = pe.matmul(S[:, i, 2 * h + o, :], qT[r, h, j * P:(j + 1) * P],
                                                           kT[r, o, h, j * P:(j + 1) * P], start=True, stop=True)
                                            if h == 1 and o == 1:
                                                mm.then_inc(s_ready, 1)
                            if j >= 1:
                                n = b * TPB + j - 1
                                pe.wait_ge(pbd_ready, n * 4 + 4)
                                pe.wait_ge(v_out, b * 2 + 2)
                                pe.wait_ge(oT_ready, n + 1)
                                for h in range(CH):
                                    for m in range(HPH):
                                        at = (m // 2) * 4 + 2 * h + m % 2
                                        mm = pe.matmul(aux[2 + (j - 1) % 2][:, h * P:(h + 1) * P],
                                                       vx[:, j - 1, h, m * P:(m + 1) * P], pbd[:, (j - 1) % 2, at, :],
                                                       start=(m == 0), stop=(m == HPH - 1))
                                mm.then_inc(o_ready, 1)

                @block.scalar
                def _(act):
                    act.sem_inc(s_out_a, 1)
                    act.sem_inc(oT_ready, 2)
                    act.sem_inc(pT_free, 1)
                    with act.Fori(0, NBLK) as b:
                        for h in range(CH):
                            act.wait_ge(qk_ready, b * 4 + h + 1)
                            act.activation(qT[:, h, :], aux[h][:, :], ACT.Copy).then_inc(q_out, 1)
                        for i in range(2):
                            act.wait_ge(zeroed, 2)
                            act.wait_ge(v_ready, b * 2 + i + 1)
                            for j in range(2):
                                for h in range(CH):
                                    ins = act.activation(spread(2 * i + j, h), aux[i][:, j * D + h * P:j * D + (h + 1) * P]
                                                         .rearrange("p (n c) -> p n c", c=AD), ACT.Copy)
                            ins.then_inc(v_out, 1)
                        for j in range(TPB + 1):
                            if j >= 1:
                                n = b * TPB + j - 1
                                act.wait_ge(pT_ready, n + 1)
                                act.wait_ge(o_ready, n + 1)
                                for q in range(4):
                                    o = slice(32 * q, 32 * q + 32)
                                    act.activation(pbd[o, (j - 1) % 2, :, 32 * q:32 * q + 32], pT[o, :, :], ACT.Copy).then_inc(pbd_ready, 1)
                                act.wait_ge(pbd_ready, n * 4 + 4)
                                act.sem_inc(pT_free, 1)
                            if j < TPB:
                                n = b * TPB + j
                                act.wait_ge(s_ready, n * PAIRS + PAIRS)
                                for q in range(2):
                                    o = slice(32 * q, 32 * q + 32)
                                    ins = act.activation(s[o, j % 2, :, :], S[o, :, :, 32 * q:32 * q + 32].rearrange("p i m k -> p (i m) k"), ACT.Copy)
                                ins.then_inc(s_out_a, 1)
                                act.wait_ge(sub_done, n + 1)
                                act.activation(e[:, j % 2, :, :], s[:, j % 2, :, :], ACT.Exp, scale=AD ** -0.5).then_inc(exp_done, 1)
                            if j >= 1:
                                n = b * TPB + j - 1
                                act.wait_ge(o_ready, n + 3)
                                act.wait_ge(store_free, n + 1)
                                act.activation(oT[:, (j - 1) % 2, :, :], aux[2 + (j - 1) % 2][:, 0:D].rearrange("p (h n) -> p h n", h=CH),
                                               ACT.Copy).then_inc(oT_ready, 1)

                @block.vector
                def _(dve):
                    dve.sem_inc(s_out_v, 1)
                    PER = TPB * 3
                    with dve.Fori(0, NBLK) as b:
                        ch = Chain(dve, soft_step, b * PER)
                        dve.tensor_copy(xb[:, :, :], xnT[:, :, bass.ds(b * BLK, BLK)]).then_inc(xb_ready, 1)
                        dve.wait_ge(par_step, 7)
                        for h in range(CH):
                            dve.wait_ge(qk_ready, b * 4 + h + 3)
                            for o in range(2):
                                dve.tensor_scalar(kT[:, o, h, :], aux[2 + h][:, :], par[:, o:o + 1], None, ALU.mult).then_inc(k_out, 1)
                        for j in range(TPB + 1):
                            if j >= 1:
                                n = b * TPB + j - 1
                                k = (j - 1) % 2
                                dve.wait_ge(exp_done, n + 1)
                                ch.link(dve.tensor_reduce(sm[:, k, :], e[:, k, :, :], AX.X, ALU.add))
                                ch.link(dve.reciprocal(sm[:, k, :], sm[:, k, :]))
                                ch.link(dve.tensor_tensor(e[:, k, :, :], e[:, k, :, :], sm[:, k, :].unsqueeze(2).to_broadcast([P, AH, SQ]), ALU.mult))
                                dve.wait_ge(pT_free, n + 1)
                                dve.transpose(pT[:, :, :], e[:, k, :, :]).then_inc(pT_ready, 1)
                            if j < TPB:
                                n = b * TPB + j
                                k = j % 2
                                dve.wait_ge(s_ready, n * PAIRS + PAIRS)
                                for q in range(2, 4):
                                    o = slice(32 * q, 32 * q + 32)
                                    ins = dve.tensor_copy(s[o, k, :, :], S[o, :, :, 32 * q:32 * q + 32].rearrange("p i m k -> p (i m) k"))
                                ins.then_inc(s_out_v, 1)
                                dve.wait_ge(s_out_v, n + 2)
                                dve.wait_ge(s_out_a, n + 2)
                                dve.tensor_reduce(mx[:, k, :], s[:, k, :, :], AX.X, ALU.max).then_inc(max_done, 1)
                                dve.wait_ge(max_done, n + 1)
                                dve.tensor_tensor(s[:, k, :, :], s[:, k, :, :], mx[:, k, :].unsqueeze(2).to_broadcast([P, AH, SQ]),
                                                  ALU.subtract).then_inc(sub_done, 1)
                        assert ch.n == PER

        with scope(nc, "sa2") as sc:
            po = [sc.pb(f"po{i}", [P, 2, D]) for i in range(4)]
            o_ready = sc.sem("o_ready")
            o_added = sc.sem("o_added")
            with nc.Block() as block:
                @block.tensor
                def _(pe):
                    pe.wait_ge(gathered, 16 * NT)
                    pe.wait_ge(wp_loaded, 32)
                    for t in range(NT):
                        if t % 2 == 0 and t >= 8:
                            pe.wait_ge(o_added, t // 2 - 3)
                        dst = po[(t // 2) % 4][:, t % 2, :]
                        for c in range(CH):
                            pe.matmul(dst, turnedT[:, c, t * P:(t + 1) * P], wp[:, c, :], start=(c == 0), stop=False)
                        mm = pe.matmul(dst, ones[:, :], bp[:, :], start=False, stop=True)
                        if t % 2:
                            mm.then_inc(o_ready, 1)

                @block.vector
                def _(dve):
                    for i in range(NT // 2):
                        dve.wait_ge(o_ready, i + 1)
                        xt = x_sb[:, 2 * i:2 * i + 2, :]
                        dve.tensor_tensor(xt, xt, po[i % 4][:, :, :], ALU.add).then_inc(o_added, 1)


def program(nc, t, out):
    def stage(prefix):
        return {k[len(prefix):]: v for k, v in t.items() if k.startswith(prefix)}

    xa_v_last = nc.dram_tensor("dram_xa_v_last", [B, NKV, KVW], F32, kind="Internal").ap()
    la_v_last = nc.dram_tensor("dram_la_v_last", [B, VW], F32, kind="Internal").ap()
    sa_turn = nc.dram_tensor("dram_sa_turn", [NT, SPG, AH, AD, SQ], F32, kind="Internal").ap()
    with ExitStack() as ctx:
        sc = Scope(nc, ctx, "main")
        x_sb = sc.sb("x", [P, NT, D])
        xnT = sc.sb("xnT", [P, CH, TOK])
        x_loaded = sc.sem("x_loaded")
        x_stored = sc.sem("x_stored")
        with nc.Block() as block:
            @block.sync
            def _(sp):
                sp.dma_start(x_sb[:, :, :], t["x"].rearrange("(t p) c -> p t c", p=P)).then_inc(x_loaded, 16)
                sp.wait_ge(x_loaded, 16)
        ident, neg_half = constants(nc, sc)
        layernorm(nc, "ln0", x_sb, xnT, ident, neg_half)
        cross_attention(nc, x_sb, xnT, ident, neg_half, t["ctxT"], t["ctx_lastT"], stage("xa_"), xa_v_last)
        layernorm(nc, "ln1", x_sb, xnT, ident, neg_half)
        rwkv(nc, x_sb, xnT, ident, stage("tm_"))
        layernorm(nc, "ln2", x_sb, xnT, ident, neg_half)
        with ExitStack() as inner:
            combT = Scope(nc, inner, "f0").sb("combT", [3 * E, TOK], BF16)
            ffn0(nc, x_sb, xnT, ident, combT, stage("f0_"))
        layernorm(nc, "ln3", x_sb, xnT, ident, neg_half)
        linear_attention(nc, x_sb, xnT, ident, t["ctxT"], t["ctx_lastT"], stage("la_"), la_v_last)
        layernorm(nc, "ln4", x_sb, xnT, ident, neg_half)
        self_attention(nc, x_sb, xnT, ident, stage("sa_"), sa_turn)
        layernorm(nc, "ln5", x_sb, xnT, ident, neg_half, add_to_x=True)
        with ExitStack() as inner:
            combT = Scope(nc, inner, "f1").sb("combT", [3 * E, TOK], BF16)
            ffn1(nc, x_sb, xnT, ident, combT, stage("f1_"))
        with nc.Block() as block:
            @block.sync
            def _(sp):
                sp.dma_start(out.rearrange("(t p) c -> p t c", p=P), x_sb[:, :, :]).then_inc(x_stored, 16)
                sp.wait_ge(x_stored, 16)


def expand(n):
    import numpy as np
    one = np.arange(E * n)[None] // n == np.arange(E)[:, None]
    return np.where(np.tile(one, (3, 1)), 0x3F80, 0).astype(np.uint16)


def layout(i):
    import numpy as np
    qkv = i["L1_attn_Wqkv"].reshape(AH, 3, AD, D)
    t = {"x": i["x"].reshape(TOK, D)}
    ctxT = i["ctx_2048"].reshape(B, SK, CH, P).transpose(0, 3, 2, 1)
    t["ctxT"], t["ctx_lastT"] = ctxT[:, :, :, :SKM], ctxT[:, :, :, SKM].transpose(1, 2, 0)
    for k in ("Wq", "bq", "Wk", "bk", "Wv", "Wo", "qn_w", "kn_w"):
        t["xa_" + k] = i["L0_xattn_" + k]
    t["xa_mask"] = i["mask_1xSxS2_ff0"]
    t["xa_bvT"] = i["L0_xattn_bv"].reshape(NKV, HD).T
    t["tm_prm"] = np.stack([i["L0_attn_" + k].reshape(-1) for k in PARAMS], axis=1)
    for k in ("W_r", "W_k", "W_v", "W_o", "w1", "w2", "a1", "a2", "g1", "g2"):
        t["tm_" + k] = i["L0_attn_" + k]
    t["f0_Wg"] = i["L0_ffn_Wg"].T
    for k in ("1", "3"):
        t["f0_W" + k] = np.concatenate([i["L0_ffn_W" + k].reshape(-1, D), i["L0_ffn_Ws" + k]]).T
    t["f0_W2"] = np.concatenate([i["L0_ffn_W2"].transpose(0, 2, 1).reshape(-1, D), i["L0_ffn_Ws2"].T])
    t["f0_expand"] = expand(HID0)
    for k in ("Wq", "Wk", "Wv", "Wo"):
        t["la_" + k] = i["L1_xattn_" + k].T
    for k in ("bq", "bk"):
        t[f"la_{k}T"] = i["L1_xattn_" + k].reshape(CH, P).T
    for k in ("bv", "bo"):
        t["la_" + k] = i["L1_xattn_" + k]
    for k in ("Wqf", "Wkf"):
        t[f"la_{k}T"] = i["L1_xattn_" + k].T
    t["la_mask"] = i["mask_BxS2_ff1"]
    t["la_maskT"] = i["mask_BxS2_ff1"][:, :SKM].T.reshape(2, P, B).transpose(1, 0, 2)
    for n, k in enumerate(("Wq", "Wk", "Wv")):
        t["sa_" + k] = qkv[:, n].reshape(D, D).T
    t["sa_Wproj"] = i["L1_attn_Wproj"].T
    t["sa_bproj"] = i["L1_attn_bproj"]
    for k in ("wa", "rg", "rw1", "rw2", "rb2", "sg", "sw1", "sw2", "sb2"):
        t["f1_" + k] = i["L1_ffn_" + k]
    t["f1_gate_bias"] = np.concatenate([i["L1_ffn_rgb"], i["L1_ffn_sgb"]]).T
    t["f1_up_bias"] = np.concatenate([i["L1_ffn_rb1"], i["L1_ffn_sb1"]]).T
    t["f1_expand1"] = expand(P)
    return {k: np.ascontiguousarray(v) for k, v in t.items()}


def kernel(**inputs):
    import concourse.bacc as bacc
    import numpy as np
    from concourse.bass_utils import run_bass_kernel_spmd

    arrays = layout({k: np.asarray(v) for k, v in inputs.items()})
    nc = bacc.Bacc("TRN2", target_bir_lowering=False, num_devices=1)
    t = {k: nc.dram_tensor("in_" + k, v.shape, mybir.dt.from_np(v.dtype), kind="ExternalInput").ap() for k, v in arrays.items()}
    out = nc.dram_tensor("out", (TOK, D), F32, kind="ExternalOutput").ap()
    program(nc, t, out)
    r = run_bass_kernel_spmd(nc, [{"in_" + k: v for k, v in arrays.items()}], core_ids=[0])
    return r.results[0]["out"].reshape(B, SQ, D)
```
